# Optimizing a Trainium2 kernel written in Bass

```python
import numpy as np
import jax
import jax.numpy as jnp

def _softmax(x, axis=-1):
    return jax.nn.softmax(x, axis=axis)

def _gelu(x):
    return jax.nn.gelu(x, approximate=True)

def _silu(x):
    return jax.nn.silu(x)

def _sigmoid(x):
    return jax.nn.sigmoid(x)

def _layernorm(x, axis=-1, eps=1e-05):
    m = jnp.mean(x, axis=axis, keepdims=True)
    v = jnp.var(x, axis=axis, keepdims=True)
    return (x - m) / jnp.sqrt(v + eps)

def _scatter_add(tgt, idx, src, axis=0):
    return tgt.at[idx].add(src)

def _segment_sum(src, seg, n):
    return jax.ops.segment_sum(src, seg, n)
kernel_name = 'mk_perceiver_d1_seqx_r4_4f2611'

def setup_inputs(seed: int=0):
    np.random.seed(seed)
    _w = jnp.asarray

    def _rec_inputs():
        import jax
        import jax.numpy as jnp
        _rk = jax.random.key(seed)
        x = -0.0002928 + 1 * jax.random.normal(jax.random.fold_in(_rk, 1), (32, 64, 256), jnp.float32)
        _lenS = 64 - jax.random.randint(jax.random.fold_in(_rk, 7), (32,), 0, max(1, 64 // 4) + 1, jnp.int32)
        _lenS2 = 1601 - jax.random.randint(jax.random.fold_in(_rk, 8), (32,), 0, max(1, 1601 // 4) + 1, jnp.int32)
        _ctx_1024P = jax.random.normal(jax.random.fold_in(_rk, 11), (32, 16, 256), jnp.float32)
        _ctx_1024c = jax.random.dirichlet(jax.random.fold_in(_rk, 511), 0.3 * jnp.ones((16,), jnp.float32), (32, 1601))
        _ctx_1024t = jnp.einsum('bsk,bkd->bsd', _ctx_1024c, _ctx_1024P)
        _ctx_1024t = _ctx_1024t * jax.lax.rsqrt(jnp.mean(jnp.square(_ctx_1024t)) + 1e-12) * 0.953939
        ctx_1024 = -1.39393e-06 + 0.999914 * (_ctx_1024t + 0.3 * jax.random.normal(jax.random.fold_in(_rk, 611), (32, 1601, 256), jnp.float32))
        return (x, ctx_1024)
    x, ctx_1024 = _rec_inputs()

    def _L0_xattn_setup():
        import jax, jax.numpy as jnp
        import numpy as np
        NUM_HEADS = 16
        D_MODEL = 256
        D_K = D_MODEL // NUM_HEADS

        def _split_heads(x):
            B, S, _ = x.shape
            return x.reshape(B, S, NUM_HEADS, D_K).transpose(0, 2, 1, 3)
        key = jax.random.key(seed)
        ks = jax.random.split(key, 11)
        B, S, D = (1, 1024, D_MODEL)
        scale = 1.0 / np.sqrt(D)
        return {'Q': jax.random.normal(ks[0], (B, S, D), jnp.float32), 'K': jax.random.normal(ks[1], (B, S, D), jnp.float32), 'V': jax.random.normal(ks[2], (B, S, D), jnp.float32), 'W_Q': jax.random.normal(ks[3], (D, D), jnp.float32) * scale, 'b_Q': jax.random.normal(ks[4], (D,), jnp.float32) * 0.02, 'W_K': jax.random.normal(ks[5], (D, D), jnp.float32) * scale, 'b_K': jax.random.normal(ks[6], (D,), jnp.float32) * 0.02, 'W_V': jax.random.normal(ks[7], (D, D), jnp.float32) * scale, 'b_V': jax.random.normal(ks[8], (D,), jnp.float32) * 0.02, 'W_O': jax.random.normal(ks[9], (D, D), jnp.float32) * scale, 'b_O': jax.random.normal(ks[10], (D,), jnp.float32) * 0.02}
    _L0_xattn_all = _L0_xattn_setup()
    _L0_xattn_in = {k: v for k, v in _L0_xattn_all.items() if k in ('W_Q', 'b_Q', 'W_K', 'b_K', 'W_V', 'b_V', 'W_O', 'b_O')}
    del _L0_xattn_all

    def _L0_attn_setup():
        import jax, jax.numpy as jnp
        import numpy as np
        from jax import lax
        D_MODEL = 256
        B, T = (4, 512)
        LN_EPS = 1e-05

        def _ln(x, w, b):
            mu = jnp.mean(x, axis=-1, keepdims=True)
            var = jnp.mean((x - mu) ** 2, axis=-1, keepdims=True)
            return (x - mu) * lax.rsqrt(var + LN_EPS) * w + b

        def _wkv(u, k, v):
            Bb, Tt, C = k.shape

            def step(carry, kv):
                aa, bb = carry
                kk, vv = kv
                p = jnp.maximum(bb, u + kk)
                e1 = jnp.exp(bb - p)
                e2 = jnp.exp(u + kk - p)
                out = (e1 * aa + e2 * vv) / (e1 + e2)
                p2 = jnp.maximum(bb, kk)
                e1b = jnp.exp(bb - p2)
                e2b = jnp.exp(kk - p2)
                return ((e1b * aa + e2b * vv, p2 + jnp.log(e1b + e2b)), out)
            init = (jnp.zeros((Bb, C), k.dtype), jnp.zeros((Bb, C), k.dtype))
            _, outs = lax.scan(step, init, (jnp.swapaxes(k, 0, 1), jnp.swapaxes(v, 0, 1)))
            return jnp.swapaxes(outs, 0, 1)
        key = jax.random.key(seed)
        ks = jax.random.split(key, 12)
        C = D_MODEL
        s = 0.02
        return {'x': jax.random.normal(ks[0], (B, T, C), jnp.float32), 'time_decay': jax.random.normal(ks[1], (C,), jnp.float32), 'time_first': jax.random.normal(ks[2], (C,), jnp.float32) * 0.5, 'time_shift': jax.random.normal(ks[3], (1, 1, C), jnp.float32) * 0.1, 'Wk': jax.random.normal(ks[4], (C, C), jnp.float32) * s, 'Wv': jax.random.normal(ks[5], (C, C), jnp.float32) * s, 'Wr': jax.random.normal(ks[6], (C, C), jnp.float32) * s, 'Wck': jax.random.normal(ks[7], (4 * C, C), jnp.float32) * s, 'Wcv': jax.random.normal(ks[8], (C, 4 * C), jnp.float32) * s, 'Wcr': jax.random.normal(ks[9], (C, C), jnp.float32) * s, 'ln1_w': jnp.ones((C,), jnp.float32), 'ln1_b': jnp.zeros((C,), jnp.float32), 'ln2_w': jnp.ones((C,), jnp.float32), 'ln2_b': jnp.zeros((C,), jnp.float32)}
    _L0_attn_all = _L0_attn_setup()
    _L0_attn_in = {k: v for k, v in _L0_attn_all.items() if k in ('time_decay', 'time_first', 'time_shift', 'Wk', 'Wv', 'Wr', 'Wck', 'Wcv', 'Wcr', 'ln1_w', 'ln1_b', 'ln2_w', 'ln2_b')}
    del _L0_attn_all

    def _L0_ffn_setup():
        import jax, jax.numpy as jnp
        import numpy as np

        def _bitlinear(x, w_latent):
            scale = jax.lax.stop_gradient(jnp.clip(jnp.mean(jnp.abs(w_latent), axis=1, keepdims=True), 1e-05, None))
            tern = jnp.clip(jnp.round(w_latent / scale), -1.0, 1.0)
            w = w_latent + jax.lax.stop_gradient(tern - w_latent)
            return x @ (w * scale).T
        key = jax.random.key(seed)
        ks = jax.random.split(key, 6)
        dim, hidden, rank = (256, 1024, 16)
        B, S = (4, 1024)
        x = jax.random.normal(ks[0], (B, S, dim), dtype=jnp.float32)
        w_fc = 0.02 * jax.random.normal(ks[1], (hidden, dim), dtype=jnp.float32)
        w_proj = 0.02 * jax.random.normal(ks[2], (dim, hidden), dtype=jnp.float32)
        u = 0.02 * jax.random.normal(ks[3], (hidden, rank), dtype=jnp.float32)
        v = 0.02 * jax.random.normal(ks[4], (rank, dim), dtype=jnp.float32)
        fast_b = jax.random.normal(ks[5], (rank, rank), dtype=jnp.float32)
        gate = jnp.float32(0.05)
        return {'x': x, 'fast_b': fast_b, 'w_fc': w_fc, 'w_proj': w_proj, 'u': u, 'v': v, 'gate': gate}
    _L0_ffn_all = _L0_ffn_setup()
    _L0_ffn_in = {k: v for k, v in _L0_ffn_all.items() if k in ('fast_b', 'w_fc', 'w_proj', 'u', 'v', 'gate')}
    del _L0_ffn_all
    return {'x': x, 'ctx_1024': ctx_1024, 'L0_xattn_W_Q': _L0_xattn_in['W_Q'], 'L0_xattn_b_Q': _L0_xattn_in['b_Q'], 'L0_xattn_W_K': _L0_xattn_in['W_K'], 'L0_xattn_b_K': _L0_xattn_in['b_K'], 'L0_xattn_W_V': _L0_xattn_in['W_V'], 'L0_xattn_b_V': _L0_xattn_in['b_V'], 'L0_xattn_W_O': _L0_xattn_in['W_O'], 'L0_xattn_b_O': _L0_xattn_in['b_O'], 'L0_attn_time_decay': _L0_attn_in['time_decay'], 'L0_attn_time_first': _L0_attn_in['time_first'], 'L0_attn_time_shift': _L0_attn_in['time_shift'], 'L0_attn_Wk': _L0_attn_in['Wk'], 'L0_attn_Wv': _L0_attn_in['Wv'], 'L0_attn_Wr': _L0_attn_in['Wr'], 'L0_attn_Wck': _L0_attn_in['Wck'], 'L0_attn_Wcv': _L0_attn_in['Wcv'], 'L0_attn_Wcr': _L0_attn_in['Wcr'], 'L0_attn_ln1_w': _L0_attn_in['ln1_w'], 'L0_attn_ln1_b': _L0_attn_in['ln1_b'], 'L0_attn_ln2_w': _L0_attn_in['ln2_w'], 'L0_attn_ln2_b': _L0_attn_in['ln2_b'], 'L0_ffn_fast_b': _L0_ffn_in['fast_b'], 'L0_ffn_w_fc': _L0_ffn_in['w_fc'], 'L0_ffn_w_proj': _L0_ffn_in['w_proj'], 'L0_ffn_u': _L0_ffn_in['u'], 'L0_ffn_v': _L0_ffn_in['v'], 'L0_ffn_gate': _L0_ffn_in['gate']}

def reference(x, ctx_1024, L0_xattn_W_Q, L0_xattn_b_Q, L0_xattn_W_K, L0_xattn_b_K, L0_xattn_W_V, L0_xattn_b_V, L0_xattn_W_O, L0_xattn_b_O, L0_attn_time_decay, L0_attn_time_first, L0_attn_time_shift, L0_attn_Wk, L0_attn_Wv, L0_attn_Wr, L0_attn_Wck, L0_attn_Wcv, L0_attn_Wcr, L0_attn_ln1_w, L0_attn_ln1_b, L0_attn_ln2_w, L0_attn_ln2_b, L0_ffn_fast_b, L0_ffn_w_fc, L0_ffn_w_proj, L0_ffn_u, L0_ffn_v, L0_ffn_gate):
    import jax
    import jax.numpy as jnp

    def _L0_xattn_ref(Q, K, V, W_Q, b_Q, W_K, b_K, W_V, b_V, W_O, b_O):
        import jax, jax.numpy as jnp
        import numpy as np
        NUM_HEADS = 16
        D_MODEL = 256
        D_K = D_MODEL // NUM_HEADS

        def _split_heads(x):
            B, S, _ = x.shape
            return x.reshape(B, S, NUM_HEADS, D_K).transpose(0, 2, 1, 3)
        q = _split_heads(Q @ W_Q + b_Q)
        k = _split_heads(K @ W_K + b_K)
        v = _split_heads(V @ W_V + b_V)
        inv_sqrt_dk = jnp.asarray(1.0 / np.sqrt(D_K), q.dtype)
        scores = jnp.einsum('bhqd,bhkd->bhqk', q, k) * inv_sqrt_dk
        weights = jax.nn.softmax(scores, axis=-1)
        out = jnp.einsum('bhqk,bhkd->bhqd', weights, v)
        B, _, S, _ = out.shape
        combined = out.transpose(0, 2, 1, 3).reshape(B, S, D_MODEL)
        return combined @ W_O + b_O

    def _L0_attn_ref(x, time_decay, time_first, time_shift, Wk, Wv, Wr, Wck, Wcv, Wcr, ln1_w, ln1_b, ln2_w, ln2_b):
        import jax, jax.numpy as jnp
        import numpy as np
        from jax import lax
        D_MODEL = 256
        B, T = (4, 512)
        LN_EPS = 1e-05

        def _ln(x, w, b):
            mu = jnp.mean(x, axis=-1, keepdims=True)
            var = jnp.mean((x - mu) ** 2, axis=-1, keepdims=True)
            return (x - mu) * lax.rsqrt(var + LN_EPS) * w + b

        def _wkv(u, k, v):
            Bb, Tt, C = k.shape

            def step(carry, kv):
                aa, bb = carry
                kk, vv = kv
                p = jnp.maximum(bb, u + kk)
                e1 = jnp.exp(bb - p)
                e2 = jnp.exp(u + kk - p)
                out = (e1 * aa + e2 * vv) / (e1 + e2)
                p2 = jnp.maximum(bb, kk)
                e1b = jnp.exp(bb - p2)
                e2b = jnp.exp(kk - p2)
                return ((e1b * aa + e2b * vv, p2 + jnp.log(e1b + e2b)), out)
            init = (jnp.zeros((Bb, C), k.dtype), jnp.zeros((Bb, C), k.dtype))
            _, outs = lax.scan(step, init, (jnp.swapaxes(k, 0, 1), jnp.swapaxes(v, 0, 1)))
            return jnp.swapaxes(outs, 0, 1)
        Bb, Tt, C = x.shape
        ts = time_shift
        h = _ln(x, ln1_w, ln1_b)
        x_shifted = jnp.concatenate([jnp.broadcast_to(ts, (Bb, 1, C)), h[:, :-1, :]], axis=1)
        xxx = h + (h - x_shifted) * ts
        k = jnp.einsum('btc,oc->bto', xxx, Wk)
        v = jnp.einsum('btc,oc->bto', xxx, Wv)
        r = jax.nn.sigmoid(jnp.einsum('btc,oc->bto', xxx, Wr))
        wkv = _wkv(time_first, k, v)
        x = x + r * wkv
        h2 = _ln(x, ln2_w, ln2_b)
        xx2 = jnp.concatenate([h2[:, -1:, :], h2[:, :-1, :]], axis=1)
        xxx2 = h2 + (xx2 - h2) * ts
        kc = jnp.einsum('btc,oc->bto', xxx2, Wck)
        rc = jax.nn.sigmoid(jnp.einsum('btc,oc->bto', xxx2, Wcr))
        vv = jnp.einsum('bth,ch->btc', jax.nn.relu(kc) ** 2, Wcv)
        return x + rc * vv

    def _L0_ffn_ref(x, fast_b, w_fc, w_proj, u, v, gate):
        import jax, jax.numpy as jnp
        import numpy as np

        def _bitlinear(x, w_latent):
            scale = jax.lax.stop_gradient(jnp.clip(jnp.mean(jnp.abs(w_latent), axis=1, keepdims=True), 1e-05, None))
            tern = jnp.clip(jnp.round(w_latent / scale), -1.0, 1.0)
            w = w_latent + jax.lax.stop_gradient(tern - w_latent)
            return x @ (w * scale).T
        h = _bitlinear(x, w_fc) + gate * (x @ v.T @ fast_b.T @ u.T)
        r = jnp.maximum(h, 0.0)
        return _bitlinear(r * r, w_proj)
    x = x + _L0_xattn_ref(_layernorm(x, axis=-1), ctx_1024, ctx_1024, L0_xattn_W_Q, L0_xattn_b_Q, L0_xattn_W_K, L0_xattn_b_K, L0_xattn_W_V, L0_xattn_b_V, L0_xattn_W_O, L0_xattn_b_O)
    x = x + _L0_attn_ref(_layernorm(x, axis=-1), L0_attn_time_decay, L0_attn_time_first, L0_attn_time_shift, L0_attn_Wk, L0_attn_Wv, L0_attn_Wr, L0_attn_Wck, L0_attn_Wcv, L0_attn_Wcr, L0_attn_ln1_w, L0_attn_ln1_b, L0_attn_ln2_w, L0_attn_ln2_b)
    x = x + _L0_ffn_ref(_layernorm(x, axis=-1), L0_ffn_fast_b, L0_ffn_w_fc, L0_ffn_w_proj, L0_ffn_u, L0_ffn_v, L0_ffn_gate)
    return x

_drawn_inputs = setup_inputs


def setup_inputs(seed=0):
    import zlib

    import numpy as np

    out = dict(_drawn_inputs(seed))
    spreads = {'L0_attn_ln1_w': (1.0, 0.2),
     'L0_attn_ln1_b': (0.0, 0.322),
     'L0_attn_ln2_w': (1.0, 0.6),
     'L0_attn_ln2_b': (0.0, 0.8)}
    factors = {'L0_xattn_b_Q': 8.0,
     'L0_xattn_b_K': 8.0,
     'L0_xattn_b_V': 3.474,
     'L0_xattn_b_O': 2.97,
     'L0_attn_time_first': 8.0,
     'L0_attn_time_shift': 8.0,
     'L0_attn_Wck': 2.819,
     'L0_attn_Wcr': 8.0,
     'L0_ffn_fast_b': 8.0,
     'L0_ffn_u': 8.0,
     'L0_ffn_v': 8.0}
    for name, (base, spread) in spreads.items():
        noise = np.random.default_rng([zlib.crc32(name.encode()), seed]).standard_normal(out[name].shape)
        drawn = base * np.exp(spread * noise) if base else spread * noise
        out[name] = jnp.asarray(drawn.astype(out[name].dtype))
    for name, factor in factors.items():
        out[name] = (out[name] * factor).astype(out[name].dtype)
    return out
```

```python
from contextlib import ExitStack

import concourse.bass as bass
from concourse import mybir

F32 = mybir.dt.float32
F16 = mybir.dt.float16
ALU = mybir.AluOpType
ACT = mybir.ActivationFunctionType
AX = mybir.AxisListType

P = 128
NB, TQ, D = 32, 64, 256
NKEY = 1601
NH, DK = 16, 16
NC = D // P
NPAIR = NH // 2
KT = (NKEY + P - 1) // P
KLAST = NKEY - (KT - 1) * P
KPAD = KT * P
GT = 4
NG = (KT + GT - 1) // GT
GW = [min(512, NKEY - 512 * g) for g in range(NG)]
TOK = NB * TQ
NTT = TOK // P
EPS = 1e-5
MSC = 1.0 / 256.0


def rows(t):
    return P if t < KT - 1 else KLAST


RING = 3


def key_side_order():
    uses = []
    uses += [("T", 0), ("T", 1), ("K", 0, 0), ("T", 2), ("K", 0, 1), ("T", 3), ("K", 0, 2), ("K", 0, 3)]
    uses += [("K", 1, g) for g in range(NG)]
    maxima = []
    for h in range(2):
        maxima += [("B", p, g) for p in range(4 * h, 4 * h + 4) for g in range(NG - 1)] + [("R", h)]
    nv = (KT + 1) // 2
    v = 0
    for n, b in enumerate(maxima):
        if n % 5 == 0 and v < nv - 2:
            uses.append(("V", v))
            v += 1
        uses.append(b)
    uses += [("V", u) for u in range(v, nv)]
    uses.append(("M",))
    return uses


USES = key_side_order()
COUNT = {k: sum(u[0] == k for u in USES) for k in "TKVBRM"}
COST = {"T": 0.05, "K": 1.28, "V": 1.1, "B": 0.45, "R": 0.4, "M": 0.3}


def numbered(uses):
    seen = dict.fromkeys("TKVBRM", 0)
    out = []
    banks = 0
    for u in uses:
        out.append((u[0], u[1:], seen[u[0]], banks % RING if u[0] != "T" else None))
        seen[u[0]] += 1
        banks += u[0] != "T"
    return out


NUMBERED = numbered(USES)


def previous_in_slot(n):
    for m in range(n - 1, -1, -1):
        if NUMBERED[m][3] == NUMBERED[n][3]:
            return NUMBERED[m][0], NUMBERED[m][2], 0
    for m in range(len(NUMBERED) - 1, -1, -1):
        if NUMBERED[m][3] == NUMBERED[n][3]:
            return NUMBERED[m][0], NUMBERED[m][2], 1


def in_slots():
    body = range(len(NUMBERED) - 1)
    whole = sum(COST[NUMBERED[n][0]] for n in body)
    slots = [[] for _ in range(KT)]
    done = 0.0
    for n in body:
        slots[min(KT - 1, int(done / whole * KT))].append(n)
        done += COST[NUMBERED[n][0]]
    return slots


SLOTS = in_slots()


class Batch:

    def __init__(self, n, half, par, back):
        self.n, self.half, self.par, self.back = n, half, par, back

    def total(self, per, j):
        return self.n * per + j


def fixed(n):
    return Batch(n, n // 2, n % 2, n)


def perceiver_kernel(nc: bass.Bass, t, out):
    q_rows = nc.dram_tensor("q_rows", (96, NPAIR, NB * P), F16, kind="Internal").ap()
    with ExitStack() as st:
        def sb(name, shape, dt=F32):
            return st.enter_context(nc.sbuf_tensor(name, shape, dt))

        ident = sb("ident", [P, P])
        xN = sb("xN", [P, NTT, D])
        combT = sb("combT", [P, NC, TOK])
        with ExitStack() as st2:
            def sb2(name, shape, dt=F32):
                return st2.enter_context(nc.sbuf_tensor(name, shape, dt))

            ident16 = sb2("ident16", [P, P], F16)
            half = sb2("half", [P, 2])
            halfq = sb2("halfq", [P, 2])
            ones = sb2("ones", [P, 32])
            wkh, wkl, wvh, wvl = (sb2(n, [P, NC, D], F16) for n in ("wkh", "wkl", "wvh", "wvl"))
            bq_c, bk_c, bv_c = (sb2(n, [P, NC]) for n in ("bq_c", "bk_c", "bv_c"))
            setup_block(nc, t["x"], t["w_q"], t["b_q"], t["w_k"], t["b_k"], t["w_v"], t["b_v"], t["ident"], t["half"],
                        q_rows, ident, ident16, half, halfq, ones, xN, wkh, wkl, wvh, wvl, bq_c, bk_c, bv_c)
            attention_block(nc, t["ctx_T"], q_rows, ident, ident16, half, ones, wkh, wkl, wvh, wvl,
                            bk_c, bv_c, combT)
        tail_block(nc, t, out, ident, xN, combT)


def setup_block(nc, x, wq, bq, wk, bk, wv, bv, ident_in, half_in, q_rows,
                ident, ident16, half, halfq, ones, xN, wkh, wkl, wvh, wvl, bq_c, bk_c, bv_c):
    NQ = TOK // 512
    with ExitStack() as st:
        def sb(name, shape, dt):
            return st.enter_context(nc.sbuf_tensor(name, shape, dt))

        def sem(name):
            return st.enter_context(nc.semaphore(name))

        wq_s = sb("wq_s", [P, NC, D], F32)
        wk_s = sb("wk_s", [P, NC, D], F32)
        wv_s = sb("wv_s", [P, NC, D], F32)
        stats = sb("stats", [P, NTT, 6], F32)
        mv = sb("mv", [P, NTT, 2], F32)
        power = sb("power", [P, NTT], F32)
        veps = sb("veps", [P, NTT], F32)
        rstd = sb("rstd", [P, NTT], F32)
        xn = sb("xn", [P, NTT, D], F32)
        xnT = sb("xnT", [P, NC, TOK], F32)
        qf = sb("qf", [P, 2, 8, 2, TQ], F32)
        qh = sb("qh", [P, NC, NB, 2 * TQ], F16)
        ql = sb("ql", [P, NC, NB, 2 * TQ], F16)
        ps_t = [st.enter_context(nc.psum_tensor(f"ps_t{i}", [P, 512], F32)) for i in range(4)]
        ps_q = [st.enter_context(nc.psum_tensor(f"ps_q{i}", [P, 512], F32)) for i in range(4)]

        x_in, w_in, c_in = sem("x_in"), sem("w_in"), sem("c_in")
        consts, split = sem("consts"), sem("split")
        stat, aggr, eps_in, rstd_in, normed = sem("stat"), sem("aggr"), sem("eps_in"), sem("rstd_in"), sem("normed")
        turned, copied, q_ps, q_f, q_hi, q_lo, q_out = (
            sem("turned"), sem("copied"), sem("q_ps"), sem("q_f"), sem("q_hi"), sem("q_lo"), sem("q_out"))

        with nc.Block() as block:
            @block.sync
            def _(sp):
                sp.dma_start(xN[:], x.rearrange("b t d -> (b t) d").rearrange("(n p) d -> p n d", p=P)).then_inc(x_in, 16)
                for dst, src in ((ident, ident_in), (half, half_in)):
                    sp.dma_start(dst[:], src).then_inc(c_in, 16)
                for dst, src in ((bq_c, bq), (bk_c, bk), (bv_c, bv)):
                    sp.dma_start(dst[:], src).then_inc(c_in, 16)
                for dst, src in ((wq_s, wq), (wk_s, wk), (wv_s, wv)):
                    sp.dma_start(dst[:], src.rearrange("(c p) n -> p c n", p=P)).then_inc(w_in, 16)
                for p in range(NPAIR):
                    o, r = p // 4, 32 * (p % 4)
                    sp.wait_ge(q_lo, NQ * (o + 1))
                    sp.wait_ge(q_hi, NQ * (o + 1))
                    for blk, src in ((0, qh), (1, ql), (2, qh)):
                        sp.dma_start(q_rows[32 * blk:32 * blk + 32, p, :],
                                     src[r:r + 32, o, :, :].rearrange("p b t -> p (b t)")).then_inc(q_out, 16)
                sp.wait_ge(q_out, 16 * 3 * NPAIR)

            @block.gpsimd
            def _(pool):
                pool.memset(power[:], -0.5).then_inc(consts, 1)
                pool.memset(ones[:], 1.0).then_inc(consts, 1)
                pool.wait_ge(consts, 2)
                pool.wait_ge(eps_in, 1)
                pool.tensor_tensor(rstd[:], veps[:], power[:], ALU.pow).then_inc(rstd_in, 1)

            @block.vector
            def _(dve):
                dve.wait_ge(x_in, 16)
                for n in range(NTT):
                    dve.bn_stats(stats[:, n, :], xN[:, n, :]).then_inc(stat, 1)
                for n in range(NTT):
                    dve.wait_ge(stat, n + 1)
                    dve.bn_aggr(mv[:, n, :], stats[:, n, :]).then_inc(aggr, 1)
                dve.wait_ge(aggr, NTT)
                dve.tensor_scalar(veps[:], mv[:, :, 1], EPS, None, ALU.add).then_inc(eps_in, 1)
                dve.wait_ge(c_in, 16 * 5)
                dve.wait_ge(w_in, 16 * 3)
                dve.tensor_copy(ident16[:], ident[:]).then_inc(split, 1)
                dve.tensor_scalar(halfq[:], half[:], float(DK) ** -0.5, None, ALU.mult).then_inc(split, 1)
                dve.tensor_copy(wkh[:], wk_s[:]).then_inc(split, 1)
                dve.tensor_copy(wvh[:], wv_s[:]).then_inc(split, 1)
                dve.wait_ge(split, 4)
                dve.tensor_tensor(wkl[:], wk_s[:], wkh[:], ALU.subtract).then_inc(split, 1)
                dve.tensor_tensor(wvl[:], wv_s[:], wvh[:], ALU.subtract).then_inc(split, 1)
                dve.wait_ge(rstd_in, 1)
                for n in range(NTT):
                    dve.tensor_scalar(xn[:, n, :], xN[:, n, :], mv[:, n, 0:1], rstd[:, n:n + 1],
                                      ALU.subtract, ALU.mult).then_inc(normed, 1)
                for o in range(NC):
                    for n in range(NQ):
                        k = o * NQ + n
                        dve.wait_ge(q_ps, k + 1)
                        if k >= 2:
                            dve.wait_ge(q_lo, k - 1)
                            dve.wait_ge(q_hi, k - 1)
                        for h in range(2):
                            dve.tensor_scalar(qf[:, k % 2, :, h, :], ps_q[k % 4][:, :].rearrange("p (b t) -> p b t", t=TQ),
                                              bq_c[:, o:o + 1], halfq[:, h:h + 1], ALU.add, ALU.mult).then_inc(q_f, 1)
                        dve.wait_ge(q_hi, k + 1)
                        dve.wait_ge(q_f, 2 * k + 2)
                        dve.tensor_tensor(ql[:, o, 8 * n:8 * n + 8, :], qf[:, k % 2, :, :, :].rearrange("p b h t -> p b (h t)"),
                                          qh[:, o, 8 * n:8 * n + 8, :], ALU.subtract).then_inc(q_lo, 1)

            @block.scalar
            def _(act):
                for c in range(NC):
                    for n in range(NQ):
                        k = c * NQ + n
                        act.wait_ge(turned, k + 1)
                        act.copy(xnT[:, c, 512 * n:512 * n + 512], ps_t[k % 4][:, :]).then_inc(copied, 1)
                for o in range(NC):
                    for n in range(NQ):
                        k = o * NQ + n
                        act.wait_ge(q_f, 2 * k + 2)
                        act.copy(qh[:, o, 8 * n:8 * n + 8, :],
                                 qf[:, k % 2, :, :, :].rearrange("p b h t -> p b (h t)")).then_inc(q_hi, 1)

            @block.tensor
            def _(pe):
                pe.wait_ge(c_in, 16 * 5)
                pe.wait_ge(w_in, 16 * 3)
                for c in range(NC):
                    for n in range(NQ):
                        k = c * NQ + n
                        pe.wait_ge(normed, 4 * n + 4)
                        if k >= 4:
                            pe.wait_ge(copied, k - 3)
                        for j in range(4):
                            last = pe.transpose(ps_t[k % 4][:, P * j:P * j + P], xn[:, 4 * n + j, P * c:P * c + P], ident[:])
                        last.then_inc(turned, 1)
                pe.wait_ge(copied, NC * NQ)
                for o in range(NC):
                    for n in range(NQ):
                        k = o * NQ + n
                        if k >= 4:
                            pe.wait_ge(q_f, 2 * (k - 3))
                        for c in range(NC):
                            last = pe.matmul(ps_q[k % 4][:, :], wq_s[:, c, P * o:P * o + P],
                                             xnT[:, c, 512 * n:512 * n + 512], start=(c == 0), stop=(c == NC - 1))
                        last.then_inc(q_ps, 1)


def attention_block(nc, ctx_in, q_rows, ident, ident16, half, ones, wkh, wkl, wvh, wvl, bk_c, bv_c, combT):
    with ExitStack() as st:
        def sb(name, shape, dt):
            return st.enter_context(nc.sbuf_tensor(name, shape, dt))

        def sem(name):
            return st.enter_context(nc.semaphore(name))

        ctxT = [sb(f"ctxT{i}", [P, NC, NKEY], F32) for i in range(2)]
        cTh = sb("cTh", [P, NC, KPAD], F16)
        cTl = sb("cTl", [P, NC, KPAD], F16)
        Kh = sb("Kh", [P, NC, KPAD], F16)
        Kl = sb("Kl", [P, NC, KPAD], F16)
        KS = [sb(f"KS{i}", [P, NPAIR, KPAD], F16) for i in range(2)]
        V = [sb(f"V{i}", [P, KT, D], F32) for i in range(2)]
        QS = [sb(f"QS{i}", [P, NPAIR, P], F16) for i in range(2)]
        PR = [sb(f"PR{i}", [P, NPAIR * P], F32) for i in range(3)]
        acc = [sb(f"acc{i}", [P, NPAIR * P], F32) for i in range(2)]
        mx = sb("mx", [P, NPAIR, NG], F32)
        nmx = sb("nmx", [P, NPAIR], F32)
        mparts = sb("mparts", [P, NPAIR, 2], F16)
        s_sel = sb("s_sel", [P, NC, TQ], F32)
        o_sel = sb("o_sel", [P, NC, TQ], F32)
        s_all = sb("s_all", [P, NC, TQ], F32)
        o_all = sb("o_all", [P, NC, TQ], F32)
        s_inv = sb("s_inv", [P, NC, TQ], F32)
        o_nrm = sb("o_nrm", [P, NC, TQ], F32)

        sc = [st.enter_context(nc.psum_tensor(f"sc{i}", [P, NPAIR * P], F32)) for i in range(2)]
        ring = [st.enter_context(nc.psum_tensor(f"ring{i}", [P, 512], F32)) for i in range(RING)]
        out_ps = st.enter_context(nc.psum_tensor("out_ps", [P, 2, NC, P], F32))

        ctx_full = [sem(f"ctx_full{i}") for i in range(2)]
        qs_full = [sem(f"qs_full{i}") for i in range(2)]
        ks_full = [[sem(f"ks_full{o}{i}") for i in range(2)] for o in range(NC)]
        rows_set = sem("rows_set")
        in_ring = {k: sem(f"in_ring_{k}") for k in "TKVBRM"}
        hi_done = {k: sem(f"hi_done_{k}") for k in "TK"}
        out_ring = {k: sem(f"out_ring_{k}") for k in "TKVBRM"}
        maxed = sem("maxed")
        scored, exped, pv_done, acc_done, summed, out_free, outed = (
            sem("scored"), sem("exped"), sem("pv_done"), sem("acc_done"), sem("summed"), sem("out_free"), sem("outed"))

        def p_buf(b, t):
            return (t + b.par) % 3

        def p_before(b, t):
            if t >= 3:
                return t - 3, 0
            return max(s for s in range(KT) if (s + 1 - b.par) % 3 == (t + b.par) % 3), 1

        with nc.Block() as block:
            @block.sync
            def _(sp):
                def loads(b, q):
                    if q.back >= 2:
                        sp.wait_ge(out_ring["T"], (q.n - 1) * COUNT["T"])
                    n = q.n
                    sp.dma_start(ctxT[q.par][:, :, :],
                                 ctx_in[bass.ds(n, 1), :, :].rearrange("a (c p) k -> p (a c) k", p=P)
                                 ).then_inc(ctx_full[q.par], 16)
                    if q.back >= 2:
                        sp.wait_ge(scored, (q.n - 1) * KT)
                    sp.dma_start(QS[q.par][0:96, :, :],
                                 q_rows[:, :, bass.ds(n * P, P)]).then_inc(qs_full[q.par], 16)
                    for o in range(NC):
                        sp.wait_ge(hi_done["K"], q.total(COUNT["K"], NG * (o + 1)))
                        for p in range(4 * o, 4 * o + 4):
                            r = 32 * (p % 4)
                            for blk in (0, 1):
                                sp.dma_start(KS[q.par][32 * blk:32 * blk + 32, p, 0:NKEY],
                                             Kh[r:r + 32, o, 0:NKEY]).then_inc(ks_full[o][q.par], 16)
                        sp.wait_ge(out_ring["K"], q.total(COUNT["K"], NG * (o + 1)))
                        for p in range(4 * o, 4 * o + 4):
                            r = 32 * (p % 4)
                            sp.dma_start(KS[q.par][64:96, p, 0:NKEY],
                                         Kl[r:r + 32, o, 0:NKEY]).then_inc(ks_full[o][q.par], 16)

                loads(None, fixed(0))
                loads(None, fixed(1))
                with sp.Fori(0, (NB - 2) // 2) as k:
                    loads(None, Batch(2 * k + 2, k + 1, 0, 2))
                    loads(None, Batch(2 * k + 3, k + 1, 1, 2))

            @block.gpsimd
            def _(pool):
                def sums(b):
                    for t in range(1, KT):
                        pool.wait_ge(exped, b.total(KT, t + 1))
                        r = rows(t)
                        a = acc[b.par][0:r, :]
                        if t == 1:
                            if b.back >= 2:
                                pool.wait_ge(summed, b.n - 1)
                            pool.tensor_tensor(a, PR[p_buf(b, 0)][:, :], PR[p_buf(b, 1)][:, :],
                                               ALU.add).then_inc(acc_done, 1)
                        else:
                            pool.wait_ge(acc_done, b.total(KT - 1, t - 1))
                            pool.tensor_tensor(a, a, PR[p_buf(b, t)][0:r, :], ALU.add).then_inc(acc_done, 1)

                for i in range(2):
                    pool.memset(KS[i][96:128, :, :], 1.0 / MSC).then_inc(rows_set, 1)
                    pool.memset(QS[i][96:128, :, :], 0.0).then_inc(rows_set, 1)
                sums(fixed(0))
                sums(fixed(1))
                with pool.Fori(0, (NB - 2) // 2) as k:
                    sums(Batch(2 * k + 2, k + 1, 0, 2))
                    sums(Batch(2 * k + 3, k + 1, 1, 2))

            @block.scalar
            def _(act):
                def key_use(q, n):
                    kind, a, j, slot = NUMBERED[n]
                    if kind not in "TKV":
                        return
                    if kind == "T":
                        g, = a
                        w = slice(512 * g, 512 * g + GW[g])
                        if g == 0:
                            act.wait_ge(ctx_full[q.par], 16 * (q.half + 1))
                            if q.back >= 1:
                                act.wait_ge(in_ring["V"], q.n * COUNT["V"])
                        act.copy(cTh[:, :, w], ctxT[q.par][:, :, w]).then_inc(hi_done["T"], 1)
                        return
                    act.wait_ge(in_ring[kind], q.total(COUNT[kind], j + 1))
                    if kind == "K":
                        o, g = a
                        if g == 0 and q.back >= 1:
                            act.wait_ge(ks_full[o][1 - q.par], 16 * 12 * (q.half + q.par))
                        act.activation(Kh[:, o, 512 * g:512 * g + GW[g]], ring[slot][:, 0:GW[g]], ACT.Identity,
                                       bias=bk_c[:, o:o + 1]).then_inc(hi_done["K"], 1)
                    else:
                        u, = a
                        if u == 0 and q.back >= 2:
                            act.wait_ge(pv_done, (q.n - 1) * KT)
                        r = rows(2 * u)
                        nt = 2 if 2 * u + 1 < KT else 1
                        act.copy(V[q.par][0:r, 2 * u:2 * u + nt, :],
                                 ring[slot][0:r, 0:D * nt].rearrange("p (t d) -> p t d", t=nt)).then_inc(out_ring["V"], 1)

                def step(b, q):
                    for t in range(KT):
                        act.wait_ge(scored, b.total(KT, t + 1))
                        s, before = p_before(b, t)
                        if b.back >= before:
                            act.wait_ge(pv_done, (b.n - before) * KT + s + 1)
                            act.wait_ge(acc_done, (b.n - before) * (KT - 1) + max(s, 1))
                        r = rows(t)
                        act.activation(PR[p_buf(b, t)][0:r, :], sc[(t + b.par) % 2][0:r, :], ACT.Exp).then_inc(exped, 1)
                        if q is not None:
                            for n in SLOTS[t]:
                                key_use(q, n)

                for n in range(len(NUMBERED) - 1):
                    key_use(fixed(0), n)
                step(fixed(0), fixed(1))
                with act.Fori(0, (NB - 2) // 2) as k:
                    step(Batch(2 * k + 1, k, 1, 1), Batch(2 * k + 2, k + 1, 0, 2))
                    step(Batch(2 * k + 2, k + 1, 0, 2), Batch(2 * k + 3, k + 1, 1, 2))
                step(fixed(NB - 1), None)

            @block.vector
            def _(dve):
                def key_use(q, n):
                    kind, a, j, slot = NUMBERED[n]
                    if kind == "V":
                        return
                    if kind == "T":
                        g, = a
                        w = slice(512 * g, 512 * g + GW[g])
                        dve.wait_ge(hi_done["T"], q.total(COUNT["T"], j + 1))
                        dve.tensor_tensor(cTl[:, :, w], ctxT[q.par][:, :, w], cTh[:, :, w],
                                          ALU.subtract).then_inc(out_ring["T"], 1)
                    elif kind == "K":
                        o, g = a
                        w = slice(512 * g, 512 * g + GW[g])
                        dve.wait_ge(hi_done["K"], q.total(COUNT["K"], j + 1))
                        dve.scalar_tensor_tensor(Kl[:, o, w], ring[slot][:, 0:GW[g]], bk_c[:, o:o + 1], Kh[:, o, w],
                                                 ALU.add, ALU.subtract).then_inc(out_ring["K"], 1)
                    elif kind == "B":
                        p, g = a
                        dve.wait_ge(in_ring["B"], q.total(COUNT["B"], j + 1))
                        dve.tensor_reduce(mx[:, p, g:g + 1], ring[slot][:, :], AX.X, ALU.max).then_inc(out_ring["B"], 1)
                    elif kind == "R":
                        h, = a
                        dve.wait_ge(in_ring["R"], q.total(COUNT["R"], j + 1))
                        dve.tensor_reduce(mx[:, 4 * h:4 * h + 4, NG - 1],
                                          ring[slot][:, 0:4 * KLAST].rearrange("p (a k) -> p a k", a=4),
                                          AX.X, ALU.max).then_inc(out_ring["R"], 1)
                        if h == 1:
                            dve.wait_ge(out_ring["B"], q.total(COUNT["B"], COUNT["B"]))
                            dve.wait_ge(out_ring["R"], q.total(COUNT["R"], COUNT["R"]))
                            if q.back >= 1:
                                dve.wait_ge(in_ring["M"], q.n)
                            dve.tensor_reduce(nmx[:, :], mx[:, :, :], AX.X, ALU.max, negate=True).then_inc(maxed, 1)
                            dve.wait_ge(maxed, q.total(3, 1))
                            dve.tensor_scalar(mparts[:, :, 0], nmx[:, :], MSC, None, ALU.mult).then_inc(maxed, 1)
                            dve.wait_ge(maxed, q.total(3, 2))
                            dve.scalar_tensor_tensor(mparts[:, :, 1], nmx[:, :], MSC, mparts[:, :, 0],
                                                     ALU.mult, ALU.subtract).then_inc(maxed, 1)
                    else:
                        dve.wait_ge(in_ring["M"], q.total(1, 1))
                        if q.back < 2:
                            dve.wait_ge(rows_set, 4)
                        dve.tensor_copy(QS[q.par][96:98, :, :],
                                        ring[slot][96:98, :].bitcast(F16).rearrange("p (a k) -> p a k", a=NPAIR)
                                        ).then_inc(out_ring["M"], 1)

                def finish(b):
                    dve.wait_ge(summed, b.total(1, 1))
                    if b.back >= 1:
                        dve.wait_ge(outed, b.n * 8)
                    dve.tensor_scalar(s_sel[:], out_ps[:, 1, :, 0:TQ], half[:, 0:1], None, ALU.mult).then_inc(outed, 1)
                    dve.tensor_scalar(o_sel[:], out_ps[:, 0, :, 0:TQ], half[:, 0:1], None, ALU.mult).then_inc(outed, 1)
                    dve.wait_ge(outed, b.total(8, 1))
                    dve.scalar_tensor_tensor(s_all[:], out_ps[:, 1, :, TQ:P], half[:, 1:2], s_sel[:],
                                             ALU.mult, ALU.add).then_inc(outed, 1)
                    dve.wait_ge(outed, b.total(8, 2))
                    dve.scalar_tensor_tensor(o_all[:], out_ps[:, 0, :, TQ:P], half[:, 1:2], o_sel[:],
                                             ALU.mult, ALU.add).then_inc(outed, 1)
                    dve.wait_ge(outed, b.total(8, 3))
                    dve.reciprocal(s_inv[:], s_all[:]).then_inc(outed, 1)
                    dve.wait_ge(outed, b.total(8, 5))
                    dve.tensor_tensor(o_nrm[:], o_all[:], s_inv[:], ALU.mult).then_inc(outed, 1)
                    dve.wait_ge(outed, b.total(8, 6))
                    for c in range(NC):
                        dve.tensor_scalar(combT[:, c, bass.ds(b.n * TQ, TQ)], o_nrm[:, c, :], bv_c[:, c:c + 1],
                                          None, ALU.add).then_inc(outed, 1)

                def step(b, q):
                    if q is not None:
                        for t in range(KT):
                            for n in SLOTS[t]:
                                key_use(q, n)
                        key_use(q, len(NUMBERED) - 1)
                    finish(b)

                for n in range(len(NUMBERED)):
                    key_use(fixed(0), n)
                step(fixed(0), fixed(1))
                with dve.Fori(0, (NB - 2) // 2) as k:
                    step(Batch(2 * k + 1, k, 1, 1), Batch(2 * k + 2, k + 1, 0, 2))
                    step(Batch(2 * k + 2, k + 1, 0, 2), Batch(2 * k + 3, k + 1, 1, 2))
                step(fixed(NB - 1), None)

            @block.tensor
            def _(pe):
                def key_use(q, n):
                    kind, a, j, slot = NUMBERED[n]
                    if kind == "T":
                        return
                    before, m, last_batch = previous_in_slot(n)
                    if q.back >= last_batch:
                        pe.wait_ge(out_ring[before], (q.n - last_batch) * COUNT[before] + m + 1)
                    bank = ring[slot]
                    if kind == "K":
                        o, g = a
                        pe.wait_ge(out_ring["T"], q.total(COUNT["T"], g + 1))
                        w = slice(512 * g, 512 * g + GW[g])
                        ow = slice(P * o, P * o + P)
                        terms = [(wkh, cTh), (wkl, cTh), (wkh, cTl)]
                        for i, (wt, ct) in enumerate(terms):
                            for c in range(NC):
                                last = pe.matmul(bank[:, 0:GW[g]], wt[:, c, ow], ct[:, c, w],
                                                 start=(i == 0 and c == 0), stop=(i == 2 and c == NC - 1))
                    elif kind == "V":
                        u, = a
                        pe.wait_ge(out_ring["T"], q.total(COUNT["T"], COUNT["T"]))
                        for i in range(2):
                            t = 2 * u + i
                            if t >= KT:
                                continue
                            r = rows(t)
                            w = slice(P * t, P * t + r)
                            for c in range(NC):
                                for ct, wt in ((cTh, wvh), (cTh, wvl), (cTl, wvh)):
                                    last = pe.matmul(bank[0:r, D * i:D * i + D], ct[:, c, w], wt[:, c, :],
                                                     start=(c == 0 and ct is cTh and wt is wvh),
                                                     stop=(c == NC - 1 and ct is cTl))
                    elif kind == "B":
                        p, g = a
                        if p % 4 == 0 and g == 0:
                            pe.wait_ge(ks_full[p // 4][q.par], 16 * 12 * (q.half + 1))
                            pe.wait_ge(qs_full[q.par], 16 * (q.half + 1))
                        last = pe.matmul(bank[:, :], QS[q.par][0:96, p, :], KS[q.par][0:96, p, 512 * g:512 * g + 512],
                                         start=True, stop=True)
                    elif kind == "R":
                        h, = a
                        for i in range(4):
                            last = pe.matmul(bank[:, KLAST * i:KLAST * i + KLAST], QS[q.par][0:96, 4 * h + i, :],
                                             KS[q.par][0:96, 4 * h + i, 512 * (NG - 1):NKEY], start=True, stop=True)
                    else:
                        pe.wait_ge(maxed, q.total(3, 3))
                        for p in range(NPAIR):
                            last = pe.transpose(bank[96:98, :].bitcast(F16)[:, P * p:P * p + P], mparts[:, p, :],
                                                ident16[:, :])
                    last.then_inc(in_ring[kind], 1)

                def scores(b, t):
                    if t == 0:
                        pe.wait_ge(out_ring["M"], b.total(1, 1))
                    if t >= 2:
                        pe.wait_ge(exped, b.total(KT, t - 1))
                    elif b.back >= 1:
                        pe.wait_ge(exped, b.total(KT, t - 1))
                    r = rows(t)
                    for p in range(NPAIR):
                        last = pe.matmul(sc[(t + b.par) % 2][0:r, P * p:P * p + P], KS[b.par][:, p, P * t:P * t + r],
                                         QS[b.par][:, p, :], start=True, stop=True)
                    last.then_inc(scored, 1)

                def products(b, t):
                    pe.wait_ge(exped, b.total(KT, t + 1))
                    if t == 0:
                        pe.wait_ge(out_ring["V"], b.total(COUNT["V"], COUNT["V"]))
                        if b.back >= 1:
                            pe.wait_ge(outed, b.n * 8)
                    r = rows(t)
                    for p in range(NPAIR):
                        o, j = p // 4, p % 4
                        last = pe.matmul(out_ps[32 * j:32 * j + 32, 0, o, :], V[b.par][0:r, t, 32 * p:32 * p + 32],
                                         PR[p_buf(b, t)][0:r, P * p:P * p + P], start=(t == 0 and o == 0),
                                         stop=(t == KT - 1), skip_group_check=True, tile_position=(0, 32 * j))
                    last.then_inc(pv_done, 1)

                def totals(b):
                    pe.wait_ge(acc_done, b.total(KT - 1, KT - 1))
                    for p in range(NPAIR):
                        o, j = p // 4, p % 4
                        last = pe.matmul(out_ps[32 * j:32 * j + 32, 1, o, :], ones[:, 0:32],
                                         acc[b.par][:, P * p:P * p + P], start=False, stop=True,
                                         skip_group_check=True, tile_position=(0, 32 * j))
                    last.then_inc(summed, 1)

                def step(b, q):
                    for t in range(KT):
                        scores(b, t)
                        if q is not None:
                            for n in SLOTS[t]:
                                key_use(q, n)
                        if t >= 1:
                            products(b, t - 1)
                    products(b, KT - 1)
                    if q is not None:
                        key_use(q, len(NUMBERED) - 1)
                    totals(b)

                pe.wait_ge(rows_set, 4)
                for n in range(len(NUMBERED)):
                    key_use(fixed(0), n)
                step(fixed(0), fixed(1))
                with pe.Fori(0, (NB - 2) // 2) as k:
                    step(Batch(2 * k + 1, k, 1, 1), Batch(2 * k + 2, k + 1, 0, 2))
                    step(Batch(2 * k + 2, k + 1, 0, 2), Batch(2 * k + 3, k + 1, 1, 2))
                step(fixed(NB - 1), None)


GTOK = 512
NGT = TOK // GTOK
GTT = GTOK // P
GB = GTOK // TQ
HID = 1024
NHC = HID // P
TRING = 8


def tail_order():
    uses = [("O", 0), ("O", 1), ("Z1", 0), ("Z1", 1)]
    uses += [("X", m, o) for m in range(3) for o in range(NC)]
    uses += [("Y", 0), ("Y", 1), ("Z2", 0), ("Z2", 1)]
    uses += [("CR", 0), ("CR", 1)] + [("CK", h) for h in range(NHC)] + [("CV", 0), ("CV", 1)]
    uses += [("Z3", 0), ("Z3", 1)] + [("FC", h) for h in range(NHC)] + [("FP", 0), ("FP", 1)]
    return uses


TUSES = tail_order()
TKINDS = ["O", "Z1", "X", "Y", "Z2", "CR", "CK", "CV", "Z3", "FC", "FP"]
TCOUNT = {k: sum(u[0] == k for u in TUSES) for k in TKINDS}
TPER = (len(TUSES) + TRING - 1) // TRING * TRING


def tail_place(use):
    n = TUSES.index(use)
    j = [u for u in TUSES if u[0] == use[0]].index(use)
    m, group = (n - TRING, 0) if n >= TRING else (n - TRING + TPER, 1)
    while m >= len(TUSES):
        m -= TRING
    b = TUSES[m]
    return j, n % TRING, b[0], [u for u in TUSES if u[0] == b[0]].index(b), group


def tail_block(nc, w, out, ident, xN, combT):
    with ExitStack() as st:
        def sb(name, shape, dt=F32):
            return st.enter_context(nc.sbuf_tensor(name, shape, dt))

        def sem(name):
            return st.enter_context(nc.semaphore(name))

        wo = sb("wo", [P, NC, D])
        wkvr = sb("wkvr", [P, 3, NC, D])
        wcr = sb("wcr", [P, NC, D])
        wck = sb("wck", [P, NC, HID])
        wcv = sb("wcv", [P, NHC, D])
        wfc = sb("wfc", [P, NC, HID])
        wfp = sb("wfp", [P, NHC, D])
        bo_row = sb("bo_row", [P, D])
        cols = sb("cols", [P, 6, NC])
        low_u = sb("low_u", [16, HID])
        low_v = sb("low_v", [16, D])
        fast = sb("fast", [16, 16])
        gate = sb("gate", [16, 1])
        mix = sb("mix", [16, HID])

        ps = [st.enter_context(nc.psum_tensor(f"tps{i}", [P, 512], F32)) for i in range(TRING)]
        weights_in = sem("weights_in")
        weight_block(nc, w, ident, ps, weights_in, wo, wkvr, wcr, wck, wcv, wfc, wfp, bo_row, cols,
                     low_u, low_v, fast, gate, mix, xN)


        x1 = sb("x1", [P, GTT, D])
        y = sb("y", [P, GTT, D])
        z = sb("z", [P, GTT, D])
        y2 = sb("y2", [P, GTT, D])
        xy = sb("xy", [P, GTT, D])
        x2 = sb("x2", [P, GTT, D])
        res = sb("res", [P, GTT, D])
        stats = sb("tstats", [P, GTT, 6])
        mv = sb("tmv", [P, 6, GTT])
        veps = sb("tveps", [P, GTT])
        rstd = sb("trstd", [P, GTT])
        power = sb("tpower", [P, GTT])
        hT = sb("hT", [P, NC, GTOK])
        dT = sb("dT", [P, NC, GTOK])
        xT = sb("xT", [P, NC, GTOK])
        kT = sb("kT", [P, NC, GTOK])
        vT = sb("vT", [P, NC, GTOK])
        cb = kT
        eT = sb("eT", [P, NC, GTOK])
        low = sb("low", [P, NC, GTOK])
        top = sb("top", [P, NC, GTOK])
        dd = sb("dd", [P, 2, NC, GTOK])
        ee = sb("ee", [P, 2, NC, GTOK])
        sT = sb("sT", [P, NC, GTOK])
        lT = sb("lT", [P, NC, GTOK])
        bb = sb("bb", [P, NC, GTOK])
        pT = sb("pT", [P, NC, GTOK])
        aT = sb("aT", [P, NC, GTOK])
        nT = sb("nT", [P, NC, GTOK])
        mT = sb("mT", [P, NC, GTOK])
        rw = lT
        hid = sb("hid", [P, NHC, GTOK])
        rl = [aT[:, i, :] for i in range(2)]

        def by_tokens_view(a):
            return a[:, :, :].rearrange("p c k -> p (c k)").rearrange("p (n d) -> p n d", d=D)

        cr, crs, cri = by_tokens_view(eT), by_tokens_view(mT), by_tokens_view(pT)

        full = {k: sem(f"full_{k}") for k in TKINDS}
        free = {k: sem(f"free_{k}") for k in TKINDS}
        preset, cb_in, x1_in = sem("preset"), sem("cb_in"), sem("x1_in")
        ln_stat, ln_aggr, ln_eps, ln_rstd, ln_out = (
            sem("ln_stat"), sem("ln_aggr"), sem("ln_eps"), sem("ln_rstd"), sem("ln_out"))
        shifted, mixed, wkv, exps, squared, summed, stored = (
            sem("shifted"), sem("mixed"), sem("wkv"), sem("exps"), sem("squared"), sem("xy_in"), sem("stored"))
        gated = sem("gated")
        NLN, NWKV, NEXP, NAG = 4, 26, 4, 6

        def flat(a):
            return a[:, :, :].rearrange("p c k -> p (c k)")

        def steps(a):
            return a[:, :, :].rearrange("p c (b t) -> p (c b) t", t=TQ)

        with nc.Block() as block:
            @block.sync
            def _(sp):
                with sp.Fori(0, NGT) as g:
                    for i in range(2):
                        sp.wait_ge(free["FP"], 2 * g + i + 1)
                        sp.dma_start(out[bass.ds(g * GTT + 2 * i, 2), :, :].rearrange("n p d -> p n d"),
                                     res[:, 2 * i:2 * i + 2, :]).then_inc(stored, 16)
                sp.wait_ge(stored, 16 * 2 * NGT + 16)

            @block.gpsimd
            def _(pool):
                pool.memset(res[:], 0.0).then_inc(stored, 16)
                pool.memset(power[:], -0.5).then_inc(preset, 1)
                pool.memset(low[:], 3.0e38).then_inc(preset, 1)
                pool.memset(bb[:], 0.0).then_inc(preset, 1)
                pool.memset(nT[:], 0.0).then_inc(preset, 1)
                pool.wait_ge(preset, 4)
                pool.memset(steps(low)[:, :, 0:1], 0.0).then_inc(preset, 1)
                with pool.Fori(0, NGT) as g:
                    for k in range(NLN):
                        pool.wait_ge(ln_eps, NLN * g + k + 1)
                        pool.tensor_tensor(rstd[:], veps[:], power[:], ALU.pow).then_inc(ln_rstd, 1)
                        if k == 2:
                            pool.tensor_tensor(xy[:], x1[:], y2[:], ALU.add).then_inc(summed, 1)

            @block.scalar
            def _(act):
                with act.Fori(0, NGT) as g:
                    def take(kind, j):
                        act.wait_ge(full[kind], TCOUNT[kind] * g + j + 1)

                    for c in range(NC):
                        use = ("Z1", c)
                        take("Z1", c)
                        act.activation(hT[:, c, :], ps[tail_place(use)[1]][:, :], ACT.Identity,
                                       bias=cols[:, 1, c:c + 1], scale=cols[:, 0, c:c + 1]).then_inc(free["Z1"], 1)
                    for m, dst in ((0, kT), (1, vT), (2, eT)):
                        for o in range(NC):
                            take("X", NC * m + o)
                            bank = ps[tail_place(("X", m, o))[1]]
                            if m < 2:
                                act.copy(dst[:, o, :], bank[:, :]).then_inc(free["X"], 1)
                            else:
                                act.activation(dst[:, o, :], bank[:, :], ACT.Exp, scale=-1.0).then_inc(free["X"], 1)
                    act.wait_ge(wkv, NWKV * g + 4)
                    act.activation(ee[:], dd[:], ACT.Exp).then_inc(exps, 1)
                    act.wait_ge(wkv, NWKV * g + 7)
                    act.activation(lT[:], sT[:], ACT.Ln).then_inc(exps, 1)
                    act.wait_ge(wkv, NWKV * g + 11)
                    act.activation(ee[:], dd[:], ACT.Exp).then_inc(exps, 1)
                    act.wait_ge(wkv, NWKV * g + 19)
                    act.activation(ee[:], dd[:], ACT.Exp).then_inc(exps, 1)
                    for c in range(NC):
                        take("Z2", c)
                        act.activation(hT[:, c, :], ps[tail_place(("Z2", c))[1]][:, :], ACT.Identity,
                                       bias=cols[:, 3, c:c + 1], scale=cols[:, 2, c:c + 1]).then_inc(free["Z2"], 1)
                    for i in range(2):
                        take("CR", i)
                        act.activation(cr[:, 2 * i:2 * i + 2, :],
                                       ps[tail_place(("CR", i))[1]][:, :].rearrange("p (n d) -> p n d", n=2),
                                       ACT.Exp, scale=-1.0).then_inc(free["CR"], 1)
                    for r, kind in enumerate(("CK", "FC")):
                        if kind == "FC":
                            for c in range(NC):
                                take("Z3", c)
                                act.copy(hT[:, c, :], ps[tail_place(("Z3", c))[1]][:, :]).then_inc(free["Z3"], 1)
                        for h in range(NHC):
                            take(kind, h)
                            n = r * NHC + h
                            if n >= 2:
                                act.wait_ge(squared, 2 * NHC * g + n - 1)
                            act.activation(rl[h % 2], ps[tail_place((kind, h))[1]][:, :],
                                           ACT.Relu).then_inc(free[kind], 1)

            @block.vector
            def _(dve):
                dve.wait_ge(preset, 5)
                with dve.Fori(0, NGT) as g:
                    def norm(k, src, dst):
                        for n in range(GTT):
                            dve.bn_stats(stats[:, n, :], src[:, n, :]).then_inc(ln_stat, 1)
                        dve.wait_ge(ln_stat, (NLN * g + k + 1) * GTT)
                        dve.tensor_tensor(mv[:, 0, :], stats[:, :, 1], stats[:, :, 4], ALU.add).then_inc(ln_aggr, 1)
                        dve.tensor_tensor(mv[:, 1, :], stats[:, :, 1], stats[:, :, 4], ALU.subtract).then_inc(ln_aggr, 1)
                        dve.tensor_tensor(mv[:, 2, :], stats[:, :, 2], stats[:, :, 5], ALU.add).then_inc(ln_aggr, 1)
                        dve.wait_ge(ln_aggr, (NLN * g + k) * NAG + 3)
                        dve.tensor_scalar(mv[:, 3, :], mv[:, 0, :], 0.5, None, ALU.mult).then_inc(ln_aggr, 1)
                        dve.tensor_tensor(mv[:, 4, :], mv[:, 1, :], mv[:, 1, :], ALU.mult).then_inc(ln_aggr, 1)
                        dve.wait_ge(ln_aggr, (NLN * g + k) * NAG + 5)
                        dve.scalar_tensor_tensor(mv[:, 5, :], mv[:, 4, :], D / 4.0, mv[:, 2, :],
                                                 ALU.mult, ALU.add).then_inc(ln_aggr, 1)
                        dve.wait_ge(ln_aggr, (NLN * g + k) * NAG + 6)
                        dve.tensor_scalar(veps[:], mv[:, 5, :], 1.0 / D, EPS, ALU.mult, ALU.add).then_inc(ln_eps, 1)
                        dve.wait_ge(ln_rstd, NLN * g + k + 1)
                        for n in range(GTT):
                            dve.tensor_scalar(dst[:, n, :], src[:, n, :], mv[:, 3, n:n + 1], rstd[:, n:n + 1],
                                              ALU.subtract, ALU.mult).then_inc(ln_out, 1)
                        dve.wait_ge(ln_out, (NLN * g + k + 1) * GTT)

                    def did(j):
                        dve.wait_ge(wkv, NWKV * g + j)

                    def take(kind, j):
                        dve.wait_ge(full[kind], TCOUNT[kind] * g + j + 1)

                    dve.tensor_copy(cb[:], combT[:, :, bass.ds(g * GTOK, GTOK)]).then_inc(cb_in, 1)
                    for i in range(2):
                        take("O", i)
                        dve.tensor_tensor(x1[:, 2 * i:2 * i + 2, :],
                                          ps[tail_place(("O", i))[1]][:, :].rearrange("p (n d) -> p n d", n=2),
                                          xN[:, bass.ds(g * GTT + 2 * i, 2), :], ALU.add).then_inc(free["O"], 1)
                    dve.wait_ge(free["O"], 2 * g + 2)
                    norm(0, x1, y)
                    norm(1, y, z)
                    dve.wait_ge(free["Z1"], 2 * g + 2)
                    dve.tensor_tensor(steps(dT)[:, :, 1:TQ], steps(hT)[:, :, 1:TQ], steps(hT)[:, :, 0:TQ - 1],
                                      ALU.subtract).then_inc(shifted, 1)
                    for c in range(NC):
                        dve.tensor_scalar(steps(dT)[:, GB * c:GB * c + GB, 0:1], steps(hT)[:, GB * c:GB * c + GB, 0:1],
                                          cols[:, 4, c:c + 1], None, ALU.subtract).then_inc(shifted, 1)
                    dve.wait_ge(shifted, 5 * g + 3)
                    for c in range(NC):
                        dve.scalar_tensor_tensor(xT[:, c, :], dT[:, c, :], cols[:, 4, c:c + 1], hT[:, c, :],
                                                 ALU.mult, ALU.add).then_inc(mixed, 1)
                    dve.wait_ge(free["X"], 6 * g + 2)
                    dve.tensor_tensor_scan(flat(top), flat(low), flat(kT), 0.0, ALU.min, ALU.max).then_inc(wkv, 1)
                    did(1)
                    da, db = dd[:, 0, :, :], dd[:, 1, :, :]
                    ea, eb = ee[:, 0, :, :], ee[:, 1, :, :]
                    dve.tensor_tensor(steps(da)[:, :, 1:TQ], steps(top)[:, :, 0:TQ - 1], steps(top)[:, :, 1:TQ],
                                      ALU.subtract).then_inc(wkv, 1)
                    dve.tensor_scalar(steps(da)[:, :, 0:1], steps(top)[:, :, 0:1], -1.0, None, ALU.mult).then_inc(wkv, 1)
                    dve.tensor_tensor(db, kT[:], top[:], ALU.subtract).then_inc(wkv, 1)
                    dve.wait_ge(exps, NEXP * g + 1)
                    dve.tensor_tensor(steps(eb)[:, :, 0:1], steps(eb)[:, :, 0:1], steps(ea)[:, :, 0:1],
                                      ALU.add).then_inc(wkv, 1)
                    did(5)
                    dve.memset(steps(ea)[:, :, 0:1], 0.0).then_inc(wkv, 1)
                    did(6)
                    dve.tensor_tensor_scan(flat(sT), ea.rearrange("p c k -> p (c k)"), eb.rearrange("p c k -> p (c k)"),
                                           0.0, ALU.mult, ALU.add).then_inc(wkv, 1)
                    dve.wait_ge(exps, NEXP * g + 2)
                    dve.tensor_tensor(steps(bb)[:, :, 1:TQ], steps(top)[:, :, 0:TQ - 1], steps(lT)[:, :, 0:TQ - 1],
                                      ALU.add).then_inc(wkv, 1)
                    did(8)
                    dve.tensor_tensor(pT[:], bb[:], kT[:], ALU.max).then_inc(wkv, 1)
                    did(9)
                    dve.tensor_tensor(da, bb[:], pT[:], ALU.subtract).then_inc(wkv, 1)
                    dve.tensor_tensor(db, kT[:], pT[:], ALU.subtract).then_inc(wkv, 1)
                    dve.wait_ge(exps, NEXP * g + 3)
                    dve.tensor_tensor(mT[:], eb, vT[:], ALU.mult).then_inc(wkv, 1)
                    dve.memset(steps(ea)[:, :, 0:1], 0.0).then_inc(wkv, 1)
                    did(13)
                    dve.tensor_tensor_scan(flat(aT), ea.rearrange("p c k -> p (c k)"), flat(mT), 0.0,
                                           ALU.mult, ALU.add).then_inc(wkv, 1)
                    for c in range(NC):
                        dve.scalar_tensor_tensor(pT[:, c, :], kT[:, c, :], cols[:, 5, c:c + 1], bb[:, c, :],
                                                 ALU.add, ALU.max).then_inc(wkv, 1)
                    did(16)
                    dve.tensor_tensor(da, bb[:], pT[:], ALU.subtract).then_inc(wkv, 1)
                    for c in range(NC):
                        dve.scalar_tensor_tensor(db[:, c, :], kT[:, c, :], cols[:, 5, c:c + 1], pT[:, c, :],
                                                 ALU.add, ALU.subtract).then_inc(wkv, 1)
                    dve.wait_ge(exps, NEXP * g + 4)
                    dve.tensor_tensor(steps(nT)[:, :, 1:TQ], steps(ea)[:, :, 1:TQ], steps(aT)[:, :, 0:TQ - 1],
                                      ALU.mult).then_inc(wkv, 1)
                    dve.tensor_tensor(mT[:], eb, vT[:], ALU.mult).then_inc(wkv, 1)
                    dve.tensor_tensor(sT[:], ea, eb, ALU.add).then_inc(wkv, 1)
                    did(21)
                    dve.tensor_tensor(aT[:], nT[:], mT[:], ALU.add).then_inc(wkv, 1)
                    did(22)
                    dve.scalar_tensor_tensor(pT[:], eT[:], 1.0, sT[:], ALU.add, ALU.mult).then_inc(wkv, 1)
                    did(24)
                    dve.reciprocal(sT[:], pT[:]).then_inc(wkv, 1)
                    did(25)
                    dve.tensor_tensor(rw[:], aT[:], sT[:], ALU.mult).then_inc(wkv, 1)
                    for i in range(2):
                        take("Y", i)
                        dve.tensor_tensor(y2[:, 2 * i:2 * i + 2, :],
                                          ps[tail_place(("Y", i))[1]][:, :].rearrange("p (n d) -> p n d", n=2),
                                          y[:, 2 * i:2 * i + 2, :], ALU.add).then_inc(free["Y"], 1)
                    dve.wait_ge(free["Y"], 2 * g + 2)
                    norm(2, y2, z)
                    dve.wait_ge(free["Z2"], 2 * g + 2)
                    dve.tensor_tensor(steps(dT)[:, :, 1:TQ], steps(hT)[:, :, 0:TQ - 1], steps(hT)[:, :, 1:TQ],
                                      ALU.subtract).then_inc(shifted, 1)
                    dve.tensor_tensor(steps(dT)[:, :, 0:1], steps(hT)[:, :, TQ - 1:TQ], steps(hT)[:, :, 0:1],
                                      ALU.subtract).then_inc(shifted, 1)
                    dve.wait_ge(shifted, 5 * g + 5)
                    for c in range(NC):
                        dve.scalar_tensor_tensor(xT[:, c, :], dT[:, c, :], cols[:, 4, c:c + 1], hT[:, c, :],
                                                 ALU.mult, ALU.add).then_inc(mixed, 1)
                    dve.wait_ge(free["CR"], 2 * g + 2)
                    dve.tensor_scalar(crs, cr, 1.0, None, ALU.add).then_inc(gated, 1)
                    dve.wait_ge(gated, 3 * g + 1)
                    dve.reciprocal(cri, crs).then_inc(gated, 1)
                    for h in range(NHC):
                        dve.wait_ge(free["CK"], NHC * g + h + 1)
                        dve.tensor_tensor(hid[:, h, :], rl[h % 2], rl[h % 2], ALU.mult).then_inc(squared, 1)
                    dve.wait_ge(gated, 3 * g + 2)
                    for i in range(2):
                        take("CV", i)
                        dve.tensor_tensor(crs[:, 2 * i:2 * i + 2, :],
                                          ps[tail_place(("CV", i))[1]][:, :].rearrange("p (n d) -> p n d", n=2),
                                          cri[:, 2 * i:2 * i + 2, :], ALU.mult).then_inc(free["CV"], 1)
                    dve.wait_ge(free["CV"], 2 * g + 2)
                    dve.wait_ge(summed, g + 1)
                    dve.tensor_tensor(x2[:], crs, xy[:], ALU.add).then_inc(gated, 1)
                    dve.wait_ge(gated, 3 * g + 3)
                    norm(3, x2, z)
                    for h in range(NHC):
                        dve.wait_ge(free["FC"], NHC * g + h + 1)
                        dve.tensor_tensor(hid[:, h, :], rl[h % 2], rl[h % 2], ALU.mult).then_inc(squared, 1)
                    for i in range(2):
                        take("FP", i)
                        dve.wait_ge(stored, 32 * g + 16)
                        dve.tensor_tensor(res[:, 2 * i:2 * i + 2, :],
                                          ps[tail_place(("FP", i))[1]][:, :].rearrange("p (n d) -> p n d", n=2),
                                          x2[:, 2 * i:2 * i + 2, :], ALU.add).then_inc(free["FP"], 1)

            @block.tensor
            def _(pe):
                with pe.Fori(0, NGT) as g:
                    def bank_of(use):
                        j, slot, kind, m, before = tail_place(use)
                        if not before:
                            pe.wait_ge(free[kind], TCOUNT[kind] * g + m + 1)
                        return ps[slot]

                    def turn(kind, src):
                        for c in range(NC):
                            bank = bank_of((kind, c))
                            for n in range(GTT):
                                last = pe.transpose(bank[:, P * n:P * n + P], src[:, n, P * c:P * c + P], ident[:])
                            last.then_inc(full[kind], 1)

                    def by_tokens(kind, i, src, wt, n_in):
                        bank = bank_of((kind, i))
                        for n in range(2):
                            for c in range(n_in):
                                last = pe.matmul(bank[:, D * n:D * n + D], src[:, c, P * (2 * i + n):P * (2 * i + n) + P],
                                                 wt[:, c, :], start=(c == 0), stop=(c == n_in - 1))
                        last.then_inc(full[kind], 1)

                    pe.wait_ge(cb_in, g + 1)
                    for i in range(2):
                        by_tokens("O", i, cb, wo, NC)
                    pe.wait_ge(ln_out, (NLN * g + 2) * GTT)
                    turn("Z1", z)
                    pe.wait_ge(mixed, 4 * g + 2)
                    for m in range(3):
                        for o in range(NC):
                            bank = bank_of(("X", m, o))
                            for c in range(NC):
                                last = pe.matmul(bank[:, :], wkvr[:, m, c, P * o:P * o + P], xT[:, c, :],
                                                 start=(c == 0), stop=(c == NC - 1))
                            last.then_inc(full["X"], 1)
                    pe.wait_ge(wkv, NWKV * g + 26)
                    for i in range(2):
                        bank = bank_of(("Y", i))
                        for n in range(2):
                            for c in range(NC):
                                last = pe.transpose(bank[:, D * n + P * c:D * n + P * c + P],
                                                    rw[:, c, P * (2 * i + n):P * (2 * i + n) + P], ident[:])
                        last.then_inc(full["Y"], 1)
                    pe.wait_ge(ln_out, (NLN * g + 3) * GTT)
                    turn("Z2", z)
                    pe.wait_ge(mixed, 4 * g + 4)
                    for i in range(2):
                        by_tokens("CR", i, xT, wcr, NC)
                    for h in range(NHC):
                        bank = bank_of(("CK", h))
                        for c in range(NC):
                            last = pe.matmul(bank[:, :], wck[:, c, P * h:P * h + P], xT[:, c, :],
                                             start=(c == 0), stop=(c == NC - 1))
                        last.then_inc(full["CK"], 1)
                    pe.wait_ge(squared, 2 * NHC * g + NHC)
                    for i in range(2):
                        by_tokens("CV", i, hid, wcv, NHC)
                    pe.wait_ge(ln_out, (NLN * g + 4) * GTT)
                    turn("Z3", z)
                    pe.wait_ge(free["Z3"], 2 * g + 2)
                    for h in range(NHC):
                        bank = bank_of(("FC", h))
                        for c in range(NC):
                            last = pe.matmul(bank[:, :], wfc[:, c, P * h:P * h + P], hT[:, c, :],
                                             start=(c == 0), stop=(c == NC - 1))
                        last.then_inc(full["FC"], 1)
                    pe.wait_ge(squared, 2 * NHC * g + 2 * NHC)
                    for i in range(2):
                        by_tokens("FP", i, hid, wfp, NHC)


def weight_block(nc, w, ident, ps, weights_in, wo, wkvr, wcr, wck, wcv, wfc, wfp, bo_row, cols,
                 low_u, low_v, fast, gate, mix, xN):
    MAGIC = 1.5 * 2.0 ** 23
    with ExitStack() as st:
        def sem(name):
            return st.enter_context(nc.semaphore(name))

        def sb(name, shape):
            return st.enter_context(nc.sbuf_tensor(name, shape, F32))

        shapes = [(NHC, D), (NC, HID)]
        nat = [sb(f"nat{m}", [P, r, n]) for m, (r, n) in enumerate(shapes)]
        u1 = [sb(f"u1{m}", [P, r, n]) for m, (r, n) in enumerate(shapes)]
        u2 = [sb(f"u2{m}", [P, r, n]) for m, (r, n) in enumerate(shapes)]
        mean = [sb(f"mean{m}", [P, r]) for m, (r, n) in enumerate(shapes)]
        scale = [sb(f"scale{m}", [P, r]) for m, (r, n) in enumerate(shapes)]
        inv = [sb(f"inv{m}", [P, r]) for m, (r, n) in enumerate(shapes)]
        nat_in, low_in, terned, turned, kept, low_ps, low_kept, biased = (
            sem("nat_in"), sem("low_in"), sem("terned"), sem("w_turned"), sem("w_kept"), sem("low_ps"),
            sem("low_kept"), sem("biased"))
        with nc.Block() as block:
            @block.sync
            def _(sp):
                sp.dma_start(nat[0][:], w["w_fc"].rearrange("(r p) n -> p r n", p=P)).then_inc(nat_in, 16)
                sp.dma_start(nat[1][:], w["w_proj"].rearrange("(r p) n -> p r n", p=P)).then_inc(nat_in, 16)
                for dst, name in ((low_u, "u_T"), (low_v, "v"), (fast, "fast_b"), (gate, "gate"), (bo_row, "b_o")):
                    sp.dma_start(dst[:], w[name]).then_inc(low_in, 16)
                sp.dma_start(wo[:], w["w_o"].rearrange("(c p) n -> p c n", p=P)).then_inc(weights_in, 16)
                for m, name in enumerate(("wk_T", "wv_T", "wr_T")):
                    sp.dma_start(wkvr[:, m, :, :], w[name].rearrange("(c p) n -> p c n", p=P)).then_inc(weights_in, 16)
                sp.dma_start(wcr[:], w["wcr_T"].rearrange("(c p) n -> p c n", p=P)).then_inc(weights_in, 16)
                sp.dma_start(wck[:], w["wck_T"].rearrange("(c p) n -> p c n", p=P)).then_inc(weights_in, 16)
                sp.dma_start(wcv[:], w["wcv_T"].rearrange("(c p) n -> p c n", p=P)).then_inc(weights_in, 16)
                sp.dma_start(cols[:], w["cols"]).then_inc(weights_in, 16)
                sp.wait_ge(weights_in, 16 * 8)

            @block.gpsimd
            def _(pool):
                pool.wait_ge(low_in, 16 * 5)
                for n in range(NTT):
                    pool.tensor_tensor(xN[:, n, :], xN[:, n, :], bo_row[:], ALU.add).then_inc(biased, 1)

            @block.vector
            def _(dve):
                dve.wait_ge(nat_in, 32)
                done = 0
                for m, (r, n) in enumerate(shapes):
                    dve.tensor_reduce(mean[m][:], nat[m][:], AX.X, ALU.add, apply_absolute_value=True).then_inc(terned, 1)
                    dve.wait_ge(terned, done + 1)
                    dve.tensor_scalar(scale[m][:], mean[m][:], 1.0 / n, 1e-5, ALU.mult, ALU.max).then_inc(terned, 1)
                    dve.wait_ge(terned, done + 2)
                    dve.reciprocal(inv[m][:], scale[m][:]).then_inc(terned, 1)
                    dve.wait_ge(terned, done + 3)
                    for i in range(r):
                        dve.tensor_scalar(u1[m][:, i, :], nat[m][:, i, :], inv[m][:, i:i + 1], -1.0,
                                          ALU.mult, ALU.max).then_inc(terned, 1)
                    dve.wait_ge(terned, done + 3 + r)
                    dve.tensor_scalar(u2[m][:], u1[m][:], 1.0, MAGIC, ALU.min, ALU.add).then_inc(terned, 1)
                    dve.wait_ge(terned, done + 4 + r)
                    dve.scalar_tensor_tensor(u1[m][:], u2[m][:], MAGIC, nat[m][:], ALU.subtract,
                                             ALU.subtract).then_inc(terned, 1)
                    dve.wait_ge(terned, done + 5 + r)
                    dve.tensor_tensor(u2[m][:], u1[m][:], nat[m][:], ALU.add).then_inc(terned, 1)
                    dve.wait_ge(terned, done + 6 + r)
                    for i in range(r):
                        dve.tensor_scalar(u1[m][:, i, :], u2[m][:, i, :], scale[m][:, i:i + 1], None,
                                          ALU.mult).then_inc(terned, 1)
                    done += 6 + 2 * r
                dve.wait_ge(low_in, 16 * 5)
                for i in range(2):
                    dve.wait_ge(low_ps, i + 1)
                    dve.tensor_scalar(mix[:, 512 * i:512 * i + 512], ps[i][0:16, :], gate[:, 0:1], None,
                                      ALU.mult).then_inc(low_kept, 1)
                for b in range(4):
                    k, i = b // 2, b % 2
                    dve.wait_ge(kept, b + 1)
                    dve.wait_ge(low_ps, 2 + b + 1)
                    dve.tensor_tensor(wfc[:, k, 512 * i:512 * i + 512], ps[b][:, :],
                                      wfc[:, k, 512 * i:512 * i + 512], ALU.add).then_inc(low_kept, 1)

            @block.scalar
            def _(act):
                for b in range(4):
                    k, i = b // 2, b % 2
                    act.wait_ge(turned, b + 1)
                    act.copy(wfc[:, k, 512 * i:512 * i + 512], ps[4 + b][:, :]).then_inc(kept, 1)
                for b in range(4):
                    act.wait_ge(turned, 4 + b + 1)
                    act.copy(wfp[:, 2 * b:2 * b + 2, :],
                             ps[4 + b][:, :].rearrange("p (h d) -> p h d", h=2)).then_inc(kept, 1)

            @block.tensor
            def _(pe):
                pe.wait_ge(low_in, 16 * 5)
                for i in range(2):
                    pe.matmul(ps[i][0:16, :], fast[:, :], low_u[:, 512 * i:512 * i + 512],
                              start=True, stop=True).then_inc(low_ps, 1)
                pe.wait_ge(low_kept, 2)
                for b in range(4):
                    k, i = b // 2, b % 2
                    pe.matmul(ps[b][:, :], low_v[:, P * k:P * k + P], mix[:, 512 * i:512 * i + 512],
                              start=True, stop=True).then_inc(low_ps, 1)
                pe.wait_ge(terned, 6 + 2 * NHC)
                for b in range(4):
                    k, i = b // 2, b % 2
                    for h in range(4):
                        last = pe.transpose(ps[4 + b][:, P * h:P * h + P], u1[0][:, 4 * i + h, P * k:P * k + P], ident[:])
                    last.then_inc(turned, 1)
                pe.wait_ge(terned, 12 + 2 * NHC + 2 * NC)
                for b in range(4):
                    pe.wait_ge(kept, b + 1)
                    for h in range(2):
                        for o in range(NC):
                            last = pe.transpose(ps[4 + b][:, D * h + P * o:D * h + P * o + P],
                                                u1[1][:, o, P * (2 * b + h):P * (2 * b + h) + P], ident[:])
                    last.then_inc(turned, 1)


def kernel(**inputs):
    import numpy as _np
    import concourse.bacc as _bacc
    from concourse import mybir as _mybir
    from concourse.bass_utils import run_bass_kernel_spmd as _run

    a = {k: _np.asarray(v) for k, v in inputs.items()}

    def turned(name):
        return _np.ascontiguousarray(a[name].T)

    def columns(v):
        return _np.ascontiguousarray(v.reshape(NC, P).T)

    first = (_np.arange(P) % 32 < DK).astype(_np.float32)
    data = {
        "x": a["x"],
        "ctx_T": _np.ascontiguousarray(a["ctx_1024"].transpose(0, 2, 1)),
        "ident": _np.eye(P, dtype=_np.float32),
        "half": _np.stack([first, 1 - first], axis=1),
        "w_q": a["L0_xattn_W_Q"], "w_k": a["L0_xattn_W_K"], "w_v": a["L0_xattn_W_V"], "w_o": a["L0_xattn_W_O"],
        "b_q": columns(a["L0_xattn_b_Q"]), "b_k": columns(a["L0_xattn_b_K"]), "b_v": columns(a["L0_xattn_b_V"]),
        "b_o": _np.ascontiguousarray(_np.broadcast_to(a["L0_xattn_b_O"], (P, D))),
        "wk_T": turned("L0_attn_Wk"), "wv_T": turned("L0_attn_Wv"), "wr_T": turned("L0_attn_Wr"),
        "wcr_T": turned("L0_attn_Wcr"), "wck_T": turned("L0_attn_Wck"), "wcv_T": turned("L0_attn_Wcv"),
        "cols": _np.ascontiguousarray(_np.stack(
            [columns(a["L0_attn_" + n].reshape(D)) for n in
             ("ln1_w", "ln1_b", "ln2_w", "ln2_b", "time_shift", "time_first")], axis=1)),
        "w_fc": a["L0_ffn_w_fc"], "w_proj": a["L0_ffn_w_proj"], "u_T": turned("L0_ffn_u"), "v": a["L0_ffn_v"],
        "fast_b": a["L0_ffn_fast_b"],
        "gate": _np.ascontiguousarray(_np.broadcast_to(a["L0_ffn_gate"].reshape(1, 1), (16, 1))),
    }
    nc = _bacc.Bacc("TRN2", target_bir_lowering=False, num_devices=1)
    t = {n: nc.dram_tensor(f"in_{n}", v.shape, _mybir.dt.from_np(v.dtype), kind="ExternalInput").ap()
         for n, v in data.items()}
    out = nc.dram_tensor("out_dram", (NTT, P, D), F32, kind="ExternalOutput").ap()
    perceiver_kernel(nc, t, out)
    r = _run(nc, [{f"in_{n}": v for n, v in data.items()}], core_ids=[0])
    return r.results[0]["out_dram"].reshape(NB, TQ, D)
```

```python
from contextlib import ExitStack

import concourse.bass as bass
from concourse import mybir

F32 = mybir.dt.float32
F16 = mybir.dt.float16
ALU = mybir.AluOpType
ACT = mybir.ActivationFunctionType
AX = mybir.AxisListType

P = 128
NB, TQ, D = 32, 64, 256
NKEY = 1601
NH, DK = 16, 16
NC = D // P
NPAIR = NH // 2
KT = (NKEY + P - 1) // P
KLAST = NKEY - (KT - 1) * P
KPAD = KT * P
GT = 4
NG = (KT + GT - 1) // GT
GW = [min(512, NKEY - 512 * g) for g in range(NG)]
TOK = NB * TQ
NTT = TOK // P
EPS = 1e-5
MSC = 1.0 / 256.0


def rows(t):
    return P if t < KT - 1 else KLAST


RING = 4
SC = 3


def spread(few, many):
    out = []
    for n, m in enumerate(many):
        if n * len(few) // len(many) != (n - 1) * len(few) // len(many):
            out.append(few[n * len(few) // len(many)])
        out.append(m)
    return out


def key_side_order():
    k = [("K", o, g) for o in range(NC) for g in range(NG)]
    v = [("V", u) for u in range((KT + 1) // 2)]
    maxima = []
    for h in range(2):
        maxima += [("B", p, g) for p in range(4 * h, 4 * h + 4) for g in range(NG - 1)] + [("R", h)]
    early, after = 4, 2
    return v[:early] + spread(v[early:] + k[:-after], maxima) + k[-after:] + [("M",)]


USES = key_side_order()
COUNT = {k: sum(u[0] == k for u in USES) for k in "KVBRM"}
COST = {"K": 1.28, "V": 1.3, "B": 0.45, "R": 0.4, "M": 0.3}


def numbered(uses):
    seen = dict.fromkeys("KVBRM", 0)
    out = []
    for u in uses:
        out.append((u[0], u[1:], seen[u[0]]))
        seen[u[0]] += 1
    return out


NUMBERED = numbered(USES)
K_USES = [n for n, u in enumerate(NUMBERED) if u[0] == "K"]


def ring_slot(q, n):
    return (n + q.par * len(USES)) % RING


def previous_in_slot(n, with_k):
    m = n - RING
    while m >= 0 and NUMBERED[m][0] == "K" and not with_k:
        m -= RING
    last_batch = 1 if m < 0 else 0
    kind, _, j = NUMBERED[m % len(NUMBERED)]
    return kind, j, last_batch


def score_bank_before(j):
    if j >= SC:
        return j - SC, 0
    return max(i for i in range(2 * KT) if i % SC == j), 1


def in_slots():
    body = range(len(NUMBERED) - 1)
    whole = sum(COST[NUMBERED[n][0]] for n in body)
    slots = [[] for _ in range(KT)]
    done = 0.0
    for n in body:
        slots[min(KT - 1, int(done / whole * KT))].append(n)
        done += COST[NUMBERED[n][0]]
    return slots


SLOTS = in_slots()

SPLITS = {0: 0, 1: 1, 2: 2, 3: 3}


class Batch:

    def __init__(self, n, half, par, back):
        self.n, self.half, self.par, self.back = n, half, par, back

    def total(self, per, j):
        return self.n * per + j


def fixed(n):
    return Batch(n, n // 2, n % 2, n)


def run_of(k):
    return (Batch(2 * k + 1, k, 1, 1), Batch(2 * k + 2, k + 1, 0, 2), Batch(2 * k + 3, k + 1, 1, 2),
            Batch(2 * k + 4, k + 2, 0, 2), Batch(2 * k + 5, k + 2, 1, 2), Batch(2 * k + 6, k + 3, 0, 2))


def perceiver_kernel(nc: bass.Bass, t, out):
    q_rows = nc.dram_tensor("q_rows", (96, NPAIR, NB * P), F16, kind="Internal").ap()
    with ExitStack() as st:
        def sb(name, shape, dt=F32):
            return st.enter_context(nc.sbuf_tensor(name, shape, dt))

        ident = sb("ident", [P, P])
        xN = sb("xN", [P, NTT, D])
        combT = sb("combT", [P, NC, TOK])
        with ExitStack() as st2:
            def sb2(name, shape, dt=F32):
                return st2.enter_context(nc.sbuf_tensor(name, shape, dt))

            ident16 = sb2("ident16", [P, P], F16)
            half = sb2("half", [P, 2])
            halfq = sb2("halfq", [P, 2])
            ones = sb2("ones", [P, 32])
            wkh, wkl, wvh, wvl = (sb2(n, [P, NC, D], F16) for n in ("wkh", "wkl", "wvh", "wvl"))
            bq_c, bk_c, bv_c = (sb2(n, [P, NC]) for n in ("bq_c", "bk_c", "bv_c"))
            setup_block(nc, t["x"], t["w_q"], t["b_q"], t["w_k"], t["b_k"], t["w_v"], t["b_v"], t["ident"], t["half"],
                        q_rows, ident, ident16, half, halfq, ones, xN, wkh, wkl, wvh, wvl, bq_c, bk_c, bv_c)
            attention_block(nc, t["ctx_T"], q_rows, ident, ident16, half, ones, wkh, wkl, wvh, wvl,
                            bk_c, bv_c, combT)
        tail_block(nc, t, out, ident, xN, combT)


def setup_block(nc, x, wq, bq, wk, bk, wv, bv, ident_in, half_in, q_rows,
                ident, ident16, half, halfq, ones, xN, wkh, wkl, wvh, wvl, bq_c, bk_c, bv_c):
    NQ = TOK // 512
    with ExitStack() as st:
        def sb(name, shape, dt):
            return st.enter_context(nc.sbuf_tensor(name, shape, dt))

        def sem(name):
            return st.enter_context(nc.semaphore(name))

        wq_s = sb("wq_s", [P, NC, D], F32)
        wk_s = sb("wk_s", [P, NC, D], F32)
        wv_s = sb("wv_s", [P, NC, D], F32)
        stats = sb("stats", [P, NTT, 6], F32)
        mv = sb("mv", [P, NTT, 2], F32)
        power = sb("power", [P, NTT], F32)
        veps = sb("veps", [P, NTT], F32)
        rstd = sb("rstd", [P, NTT], F32)
        xn = sb("xn", [P, NTT, D], F32)
        xnT = sb("xnT", [P, NC, TOK], F32)
        qf = sb("qf", [P, 2, 8, 2, TQ], F32)
        qh = sb("qh", [P, NC, NB, 2 * TQ], F16)
        ql = sb("ql", [P, NC, NB, 2 * TQ], F16)
        ps_t = [st.enter_context(nc.psum_tensor(f"ps_t{i}", [P, 512], F32)) for i in range(4)]
        ps_q = [st.enter_context(nc.psum_tensor(f"ps_q{i}", [P, 512], F32)) for i in range(4)]

        x_in, w_in, c_in = sem("x_in"), sem("w_in"), sem("c_in")
        consts, split = sem("consts"), sem("split")
        stat, aggr, eps_in, rstd_in, normed = sem("stat"), sem("aggr"), sem("eps_in"), sem("rstd_in"), sem("normed")
        turned, copied, q_ps, q_f, q_hi, q_lo, q_out = (
            sem("turned"), sem("copied"), sem("q_ps"), sem("q_f"), sem("q_hi"), sem("q_lo"), sem("q_out"))

        with nc.Block() as block:
            @block.sync
            def _(sp):
                sp.dma_start(xN[:], x.rearrange("b t d -> (b t) d").rearrange("(n p) d -> p n d", p=P)).then_inc(x_in, 16)
                for dst, src in ((ident, ident_in), (half, half_in)):
                    sp.dma_start(dst[:], src).then_inc(c_in, 16)
                for dst, src in ((bq_c, bq), (bk_c, bk), (bv_c, bv)):
                    sp.dma_start(dst[:], src).then_inc(c_in, 16)
                for dst, src in ((wq_s, wq), (wk_s, wk), (wv_s, wv)):
                    sp.dma_start(dst[:], src.rearrange("(c p) n -> p c n", p=P)).then_inc(w_in, 16)
                for p in range(NPAIR):
                    o, r = p // 4, 32 * (p % 4)
                    sp.wait_ge(q_lo, NQ * (o + 1))
                    sp.wait_ge(q_hi, NQ * (o + 1))
                    for blk, src in ((0, qh), (1, ql), (2, qh)):
                        sp.dma_start(q_rows[32 * blk:32 * blk + 32, p, :],
                                     src[r:r + 32, o, :, :].rearrange("p b t -> p (b t)")).then_inc(q_out, 16)
                sp.wait_ge(q_out, 16 * 3 * NPAIR)

            @block.gpsimd
            def _(pool):
                pool.memset(power[:], -0.5).then_inc(consts, 1)
                pool.memset(ones[:], 1.0).then_inc(consts, 1)
                pool.wait_ge(consts, 2)
                pool.wait_ge(eps_in, 1)
                pool.tensor_tensor(rstd[:], veps[:], power[:], ALU.pow).then_inc(rstd_in, 1)

            @block.vector
            def _(dve):
                dve.wait_ge(x_in, 16)
                for n in range(NTT):
                    dve.bn_stats(stats[:, n, :], xN[:, n, :]).then_inc(stat, 1)
                for n in range(NTT):
                    dve.wait_ge(stat, n + 1)
                    dve.bn_aggr(mv[:, n, :], stats[:, n, :]).then_inc(aggr, 1)
                dve.wait_ge(aggr, NTT)
                dve.tensor_scalar(veps[:], mv[:, :, 1], EPS, None, ALU.add).then_inc(eps_in, 1)
                dve.wait_ge(c_in, 16 * 5)
                dve.wait_ge(w_in, 16 * 3)
                dve.tensor_copy(ident16[:], ident[:]).then_inc(split, 1)
                dve.tensor_scalar(halfq[:], half[:], float(DK) ** -0.5, None, ALU.mult).then_inc(split, 1)
                dve.tensor_copy(wkh[:], wk_s[:]).then_inc(split, 1)
                dve.tensor_copy(wvh[:], wv_s[:]).then_inc(split, 1)
                dve.wait_ge(split, 4)
                dve.tensor_tensor(wkl[:], wk_s[:], wkh[:], ALU.subtract).then_inc(split, 1)
                dve.tensor_tensor(wvl[:], wv_s[:], wvh[:], ALU.subtract).then_inc(split, 1)
                dve.wait_ge(rstd_in, 1)
                for n in range(NTT):
                    dve.tensor_scalar(xn[:, n, :], xN[:, n, :], mv[:, n, 0:1], rstd[:, n:n + 1],
                                      ALU.subtract, ALU.mult).then_inc(normed, 1)
                for o in range(NC):
                    for n in range(NQ):
                        k = o * NQ + n
                        dve.wait_ge(q_ps, k + 1)
                        if k >= 2:
                            dve.wait_ge(q_lo, k - 1)
                            dve.wait_ge(q_hi, k - 1)
                        for h in range(2):
                            dve.tensor_scalar(qf[:, k % 2, :, h, :], ps_q[k % 4][:, :].rearrange("p (b t) -> p b t", t=TQ),
                                              bq_c[:, o:o + 1], halfq[:, h:h + 1], ALU.add, ALU.mult).then_inc(q_f, 1)
                        dve.wait_ge(q_hi, k + 1)
                        dve.wait_ge(q_f, 2 * k + 2)
                        dve.tensor_tensor(ql[:, o, 8 * n:8 * n + 8, :], qf[:, k % 2, :, :, :].rearrange("p b h t -> p b (h t)"),
                                          qh[:, o, 8 * n:8 * n + 8, :], ALU.subtract).then_inc(q_lo, 1)

            @block.scalar
            def _(act):
                for c in range(NC):
                    for n in range(NQ):
                        k = c * NQ + n
                        act.wait_ge(turned, k + 1)
                        act.copy(xnT[:, c, 512 * n:512 * n + 512], ps_t[k % 4][:, :]).then_inc(copied, 1)
                for o in range(NC):
                    for n in range(NQ):
                        k = o * NQ + n
                        act.wait_ge(q_f, 2 * k + 2)
                        act.copy(qh[:, o, 8 * n:8 * n + 8, :],
                                 qf[:, k % 2, :, :, :].rearrange("p b h t -> p b (h t)")).then_inc(q_hi, 1)

            @block.tensor
            def _(pe):
                pe.wait_ge(c_in, 16 * 5)
                pe.wait_ge(w_in, 16 * 3)
                for c in range(NC):
                    for n in range(NQ):
                        k = c * NQ + n
                        pe.wait_ge(normed, 4 * n + 4)
                        if k >= 4:
                            pe.wait_ge(copied, k - 3)
                        for j in range(4):
                            last = pe.transpose(ps_t[k % 4][:, P * j:P * j + P], xn[:, 4 * n + j, P * c:P * c + P], ident[:])
                        last.then_inc(turned, 1)
                pe.wait_ge(copied, NC * NQ)
                for o in range(NC):
                    for n in range(NQ):
                        k = o * NQ + n
                        if k >= 4:
                            pe.wait_ge(q_f, 2 * (k - 3))
                        for c in range(NC):
                            last = pe.matmul(ps_q[k % 4][:, :], wq_s[:, c, P * o:P * o + P],
                                             xnT[:, c, 512 * n:512 * n + 512], start=(c == 0), stop=(c == NC - 1))
                        last.then_inc(q_ps, 1)


def attention_block(nc, ctx_in, q_rows, ident, ident16, half, ones, wkh, wkl, wvh, wvl, bk_c, bv_c, combT):
    with ExitStack() as st:
        def sb(name, shape, dt):
            return st.enter_context(nc.sbuf_tensor(name, shape, dt))

        def sem(name):
            return st.enter_context(nc.semaphore(name))

        ctxT = [sb(f"ctxT{i}", [P, NC, NKEY], F32) for i in range(2)]
        cTh = [sb(f"cTh{i}", [P, NC, KPAD], F16) for i in range(2)]
        cTl = [sb(f"cTl{i}", [P, NC, KPAD], F16) for i in range(2)]
        Kh = sb("Kh", [P, NC, KPAD], F16)
        Kl = sb("Kl", [P, NC, KPAD], F16)
        KS = [sb(f"KS{i}", [P, NPAIR, KPAD], F16) for i in range(2)]
        V = [sb(f"V{i}", [P, KT, D], F32) for i in range(2)]
        QS = [sb(f"QS{i}", [P, NPAIR, P], F16) for i in range(2)]
        PR = [sb(f"PR{i}", [P, NPAIR * P], F32) for i in range(3)]
        acc = [sb(f"acc{i}", [P, NPAIR * P], F32) for i in range(2)]
        mx = sb("mx", [P, NPAIR, NG], F32)
        nmx = sb("nmx", [P, NPAIR], F32)
        mparts = sb("mparts", [P, NPAIR, 2], F16)
        s_sel = sb("s_sel", [P, NC, TQ], F32)
        o_sel = sb("o_sel", [P, NC, TQ], F32)
        s_all = sb("s_all", [P, NC, TQ], F32)
        o_all = sb("o_all", [P, NC, TQ], F32)
        s_inv = sb("s_inv", [P, NC, TQ], F32)
        o_nrm = sb("o_nrm", [P, NC, TQ], F32)

        sc = [st.enter_context(nc.psum_tensor(f"sc{i}", [P, 512], F32)) for i in range(SC)]
        ring = [st.enter_context(nc.psum_tensor(f"ring{i}", [P, 512], F32)) for i in range(RING)]
        out_ps = st.enter_context(nc.psum_tensor("out_ps", [P, 2, NC, P], F32))

        ctx_full = [sem(f"ctx_full{i}") for i in range(2)]
        qs_full = [sem(f"qs_full{i}") for i in range(2)]
        ks_full = [[sem(f"ks_full{o}{i}") for i in range(2)] for o in range(NC)]
        rows_set = sem("rows_set")
        in_ring = {k: sem(f"in_ring_{k}") for k in "KVBRM"}
        k_high = sem("k_high")
        ctx_high, ctx_split = sem("ctx_high"), sem("ctx_split")
        out_ring = {k: sem(f"out_ring_{k}") for k in "KVBRM"}
        maxed = sem("maxed")
        scored, exped, pv_done, acc_done, summed, out_free, outed = (
            sem("scored"), sem("exped"), sem("pv_done"), sem("acc_done"), sem("summed"), sem("out_free"), sem("outed"))

        def p_buf(b, t):
            return (t + b.par) % 3

        def p_before(b, t):
            if t >= 3:
                return t - 3, 0
            return max(s for s in range(KT) if (s + 1 - b.par) % 3 == (t + b.par) % 3), 1

        with nc.Block() as block:
            @block.sync
            def _(sp):
                def load_ctx(q):
                    if q.back >= 2:
                        sp.wait_ge(ctx_split, (q.n - 1) * NG)
                    sp.dma_start(ctxT[q.par][:, :, :],
                                 ctx_in[bass.ds(q.n, 1), :, :].rearrange("a (c p) k -> p (a c) k", p=P)
                                 ).then_inc(ctx_full[q.par], 16)

                def load_rows(q):
                    if q.back >= 2:
                        sp.wait_ge(scored, (q.n - 1) * 2 * KT)
                    sp.dma_start(QS[q.par][0:96, :, :],
                                 q_rows[:, :, bass.ds(q.n * P, P)]).then_inc(qs_full[q.par], 16)
                    for o in range(NC):
                        sp.wait_ge(k_high, q.total(COUNT["K"], NG * (o + 1)))
                        for p in range(4 * o, 4 * o + 4):
                            r = 32 * (p % 4)
                            for blk in (0, 1):
                                sp.dma_start(KS[q.par][32 * blk:32 * blk + 32, p, 0:NKEY],
                                             Kh[r:r + 32, o, 0:NKEY]).then_inc(ks_full[o][q.par], 16)
                        sp.wait_ge(out_ring["K"], q.total(COUNT["K"], NG * (o + 1)))
                        for p in range(4 * o, 4 * o + 4):
                            r = 32 * (p % 4)
                            sp.dma_start(KS[q.par][64:96, p, 0:NKEY],
                                         Kl[r:r + 32, o, 0:NKEY]).then_inc(ks_full[o][q.par], 16)

                load_ctx(fixed(0))
                load_ctx(fixed(1))
                load_rows(fixed(0))
                load_ctx(fixed(2))
                load_ctx(fixed(3))
                load_rows(fixed(1))
                load_ctx(fixed(4))
                load_rows(fixed(2))
                with sp.Fori(0, (NB - 6) // 2) as k:
                    b1, b2, b3, b4, b5, b6 = run_of(k)
                    load_ctx(b5)
                    load_rows(b3)
                    load_ctx(b6)
                    load_rows(b4)
                load_ctx(fixed(NB - 1))
                for n in range(NB - 3, NB):
                    load_rows(fixed(n))

            @block.gpsimd
            def _(pool):
                def sums(b):
                    for t in range(1, KT):
                        pool.wait_ge(exped, b.total(2 * KT, 2 * t + 2))
                        r = rows(t)
                        a = acc[b.par][0:r, :]
                        if t == 1:
                            if b.back >= 2:
                                pool.wait_ge(summed, b.n - 1)
                            pool.tensor_tensor(a, PR[p_buf(b, 0)][:, :], PR[p_buf(b, 1)][:, :],
                                               ALU.add).then_inc(acc_done, 1)
                        else:
                            pool.wait_ge(acc_done, b.total(KT - 1, t - 1))
                            pool.tensor_tensor(a, a, PR[p_buf(b, t)][0:r, :], ALU.add).then_inc(acc_done, 1)

                for i in range(2):
                    pool.memset(KS[i][96:128, :, :], 1.0 / MSC).then_inc(rows_set, 1)
                    pool.memset(QS[i][96:128, :, :], 0.0).then_inc(rows_set, 1)
                sums(fixed(0))
                sums(fixed(1))
                with pool.Fori(0, (NB - 2) // 2) as k:
                    sums(Batch(2 * k + 2, k + 1, 0, 2))
                    sums(Batch(2 * k + 3, k + 1, 1, 2))

            @block.scalar
            def _(act):
                def split(q, g):
                    w = slice(512 * g, 512 * g + GW[g])
                    if g == 0:
                        act.wait_ge(ctx_full[q.par], 16 * (q.half + 1))
                        if q.back >= 2:
                            act.wait_ge(in_ring["V"], (q.n - 1) * COUNT["V"])
                    act.copy(cTh[q.par][:, :, w], ctxT[q.par][:, :, w]).then_inc(ctx_high, 1)

                def key_use(q, r, n):
                    kind, a, j = NUMBERED[n]
                    slot_of = q or fixed(-1)
                    if kind not in "KV":
                        return
                    if kind == "K":
                        if r is None:
                            return
                    bank = ring[ring_slot(slot_of, n)]
                    if kind == "K":
                        q = r
                    act.wait_ge(in_ring[kind], q.total(COUNT[kind], j + 1))
                    if kind == "K":
                        o, g = a
                        if g == 0 and q.back >= 1:
                            act.wait_ge(ks_full[o][1 - q.par], 16 * 12 * (q.half + q.par))
                        act.activation(Kh[:, o, 512 * g:512 * g + GW[g]], bank[:, 0:GW[g]], ACT.Identity,
                                       bias=bk_c[:, o:o + 1]).then_inc(k_high, 1)
                    else:
                        u, = a
                        if u == 0 and q.back >= 2:
                            act.wait_ge(pv_done, (q.n - 1) * KT)
                        r = rows(2 * u)
                        nt = 2 if 2 * u + 1 < KT else 1
                        act.copy(V[q.par][0:r, 2 * u:2 * u + nt, :],
                                 bank[0:r, 0:D * nt].rearrange("p (t d) -> p t d", t=nt)).then_inc(out_ring["V"], 1)

                def step(b, q, r):
                    for t in range(KT):
                        s, before = p_before(b, t)
                        if b.back >= before:
                            act.wait_ge(pv_done, (b.n - before) * KT + s + 1)
                            act.wait_ge(acc_done, (b.n - before) * (KT - 1) + max(s, 1))
                        m = rows(t)
                        for j in (2 * t, 2 * t + 1):
                            act.wait_ge(scored, b.total(2 * KT, j + 1))
                            act.activation(PR[p_buf(b, t)][0:m, 512 * (j % 2):512 * (j % 2) + 512], sc[j % SC][0:m, :],
                                           ACT.Exp).then_inc(exped, 1)
                        if q is not None:
                            for n in SLOTS[t]:
                                key_use(q, r, n)
                        if r is not None and t in SPLITS:
                            split(r, SPLITS[t])

                for g in range(NG):
                    split(fixed(0), g)
                for n in K_USES:
                    key_use(None, fixed(0), n)
                for g in range(NG):
                    split(fixed(1), g)
                for n in range(len(NUMBERED) - 1):
                    key_use(fixed(0), fixed(1), n)
                step(fixed(0), fixed(1), fixed(2))
                step(fixed(1), fixed(2), fixed(3))
                with act.Fori(0, (NB - 4) // 2) as k:
                    b1, b2, b3, b4, b5, b6 = run_of(k)
                    step(b2, b3, b4)
                    step(b3, b4, b5)
                step(fixed(NB - 2), fixed(NB - 1), None)
                step(fixed(NB - 1), None, None)

            @block.vector
            def _(dve):
                def split(q, g):
                    w = slice(512 * g, 512 * g + GW[g])
                    dve.wait_ge(ctx_high, q.total(NG, g + 1))
                    dve.tensor_tensor(cTl[q.par][:, :, w], ctxT[q.par][:, :, w], cTh[q.par][:, :, w],
                                      ALU.subtract).then_inc(ctx_split, 1)

                def key_use(q, r, n):
                    kind, a, j = NUMBERED[n]
                    if kind == "V":
                        return
                    bank = ring[ring_slot(q or fixed(-1), n)]
                    if kind == "K":
                        if r is None:
                            return
                        q = r
                        o, g = a
                        w = slice(512 * g, 512 * g + GW[g])
                        dve.wait_ge(k_high, q.total(COUNT["K"], j + 1))
                        dve.scalar_tensor_tensor(Kl[:, o, w], bank[:, 0:GW[g]], bk_c[:, o:o + 1], Kh[:, o, w],
                                                 ALU.add, ALU.subtract).then_inc(out_ring["K"], 1)
                    elif kind == "B":
                        p, g = a
                        dve.wait_ge(in_ring["B"], q.total(COUNT["B"], j + 1))
                        dve.tensor_reduce(mx[:, p, g:g + 1], bank[:, :], AX.X, ALU.max).then_inc(out_ring["B"], 1)
                    elif kind == "R":
                        h, = a
                        dve.wait_ge(in_ring["R"], q.total(COUNT["R"], j + 1))
                        dve.tensor_reduce(mx[:, 4 * h:4 * h + 4, NG - 1],
                                          bank[:, 0:4 * KLAST].rearrange("p (a k) -> p a k", a=4),
                                          AX.X, ALU.max).then_inc(out_ring["R"], 1)
                        if h == 1:
                            dve.wait_ge(out_ring["B"], q.total(COUNT["B"], COUNT["B"]))
                            dve.wait_ge(out_ring["R"], q.total(COUNT["R"], COUNT["R"]))
                            if q.back >= 1:
                                dve.wait_ge(in_ring["M"], q.n)
                            dve.tensor_reduce(nmx[:, :], mx[:, :, :], AX.X, ALU.max, negate=True).then_inc(maxed, 1)
                            dve.wait_ge(maxed, q.total(3, 1))
                            dve.tensor_scalar(mparts[:, :, 0], nmx[:, :], MSC, None, ALU.mult).then_inc(maxed, 1)
                            dve.wait_ge(maxed, q.total(3, 2))
                            dve.scalar_tensor_tensor(mparts[:, :, 1], nmx[:, :], MSC, mparts[:, :, 0],
                                                     ALU.mult, ALU.subtract).then_inc(maxed, 1)
                    else:
                        dve.wait_ge(in_ring["M"], q.total(1, 1))
                        if q.back < 2:
                            dve.wait_ge(rows_set, 4)
                        dve.tensor_copy(QS[q.par][96:98, :, :],
                                        bank[96:98, :].bitcast(F16).rearrange("p (a k) -> p a k", a=NPAIR)
                                        ).then_inc(out_ring["M"], 1)

                def finish(b):
                    dve.wait_ge(summed, b.total(1, 1))
                    if b.back >= 1:
                        dve.wait_ge(outed, b.n * 8)
                    dve.tensor_scalar(s_sel[:], out_ps[:, 1, :, 0:TQ], half[:, 0:1], None, ALU.mult).then_inc(outed, 1)
                    dve.tensor_scalar(o_sel[:], out_ps[:, 0, :, 0:TQ], half[:, 0:1], None, ALU.mult).then_inc(outed, 1)
                    dve.wait_ge(outed, b.total(8, 1))
                    dve.scalar_tensor_tensor(s_all[:], out_ps[:, 1, :, TQ:P], half[:, 1:2], s_sel[:],
                                             ALU.mult, ALU.add).then_inc(outed, 1)
                    dve.wait_ge(outed, b.total(8, 2))
                    dve.scalar_tensor_tensor(o_all[:], out_ps[:, 0, :, TQ:P], half[:, 1:2], o_sel[:],
                                             ALU.mult, ALU.add).then_inc(outed, 1)
                    dve.wait_ge(outed, b.total(8, 3))
                    dve.reciprocal(s_inv[:], s_all[:]).then_inc(outed, 1)
                    dve.wait_ge(outed, b.total(8, 5))
                    dve.tensor_tensor(o_nrm[:], o_all[:], s_inv[:], ALU.mult).then_inc(outed, 1)
                    dve.wait_ge(outed, b.total(8, 6))
                    for c in range(NC):
                        dve.tensor_scalar(combT[:, c, bass.ds(b.n * TQ, TQ)], o_nrm[:, c, :], bv_c[:, c:c + 1],
                                          None, ALU.add).then_inc(outed, 1)

                def step(prev, q, r):
                    for t in range(KT):
                        for n in SLOTS[t]:
                            key_use(q, r, n)
                        if t == 0 and prev is not None:
                            finish(prev)
                        if r is not None and t in SPLITS:
                            split(r, SPLITS[t])
                    key_use(q, r, len(NUMBERED) - 1)

                for g in range(NG):
                    split(fixed(0), g)
                for n in K_USES:
                    key_use(None, fixed(0), n)
                for g in range(NG):
                    split(fixed(1), g)
                for n in range(len(NUMBERED)):
                    key_use(fixed(0), fixed(1), n)
                step(None, fixed(1), fixed(2))
                step(fixed(0), fixed(2), fixed(3))
                with dve.Fori(0, (NB - 4) // 2) as k:
                    b1, b2, b3, b4, b5, b6 = run_of(k)
                    step(b1, b3, b4)
                    step(b2, b4, b5)
                step(fixed(NB - 3), fixed(NB - 1), None)
                finish(fixed(NB - 2))
                finish(fixed(NB - 1))

            @block.tensor
            def _(pe):
                def key_use(q, r, n):
                    kind, a, j = NUMBERED[n]
                    if kind == "K" and r is None:
                        return
                    if q is not None:
                        before, m, last_batch = previous_in_slot(n, r is not None)
                        if q.back >= last_batch:
                            ahead = 1 if before == "K" else 0
                            pe.wait_ge(out_ring[before], (q.n - last_batch + ahead) * COUNT[before] + m + 1)
                    bank = ring[ring_slot(q or fixed(-1), n)]
                    if kind == "K":
                        q = r
                    if kind == "K":
                        o, g = a
                        pe.wait_ge(ctx_split, q.total(NG, g + 1))
                        w = slice(512 * g, 512 * g + GW[g])
                        ow = slice(P * o, P * o + P)
                        ch, cl = cTh[q.par], cTl[q.par]
                        terms = [(wkh, ch), (wkl, ch), (wkh, cl)]
                        for i, (wt, ct) in enumerate(terms):
                            for c in range(NC):
                                last = pe.matmul(bank[:, 0:GW[g]], wt[:, c, ow], ct[:, c, w],
                                                 start=(i == 0 and c == 0), stop=(i == 2 and c == NC - 1))
                    elif kind == "V":
                        u, = a
                        ch, cl = cTh[q.par], cTl[q.par]
                        for i in range(2):
                            t = 2 * u + i
                            if t >= KT:
                                continue
                            r = rows(t)
                            w = slice(P * t, P * t + r)
                            for c in range(NC):
                                for ct, wt in ((ch, wvh), (ch, wvl), (cl, wvh)):
                                    last = pe.matmul(bank[0:r, D * i:D * i + D], ct[:, c, w], wt[:, c, :],
                                                     start=(c == 0 and ct is ch and wt is wvh),
                                                     stop=(c == NC - 1 and ct is cl))
                    elif kind == "B":
                        p, g = a
                        if p % 4 == 0 and g == 0:
                            pe.wait_ge(ks_full[p // 4][q.par], 16 * 12 * (q.half + 1))
                            pe.wait_ge(qs_full[q.par], 16 * (q.half + 1))
                        last = pe.matmul(bank[:, :], QS[q.par][0:96, p, :], KS[q.par][0:96, p, 512 * g:512 * g + 512],
                                         start=True, stop=True)
                    elif kind == "R":
                        h, = a
                        for i in range(4):
                            last = pe.matmul(bank[:, KLAST * i:KLAST * i + KLAST], QS[q.par][0:96, 4 * h + i, :],
                                             KS[q.par][0:96, 4 * h + i, 512 * (NG - 1):NKEY], start=True, stop=True)
                    else:
                        pe.wait_ge(maxed, q.total(3, 3))
                        for p in range(NPAIR):
                            last = pe.transpose(bank[96:98, :].bitcast(F16)[:, P * p:P * p + P], mparts[:, p, :],
                                                ident16[:, :])
                    last.then_inc(in_ring[kind], 1)

                def scores(b, t):
                    if t == 0:
                        pe.wait_ge(out_ring["M"], b.total(1, 1))
                    r = rows(t)
                    for j in (2 * t, 2 * t + 1):
                        before, last_batch = score_bank_before(j)
                        if b.back >= last_batch:
                            pe.wait_ge(exped, (b.n - last_batch) * 2 * KT + before + 1)
                        for i in range(4):
                            p = 4 * (j % 2) + i
                            last = pe.matmul(sc[j % SC][0:r, P * i:P * i + P], KS[b.par][:, p, P * t:P * t + r],
                                             QS[b.par][:, p, :], start=True, stop=True)
                        last.then_inc(scored, 1)

                def products(b, t):
                    if t == 0:
                        pe.wait_ge(out_ring["V"], b.total(COUNT["V"], COUNT["V"]))
                        if b.back >= 1:
                            pe.wait_ge(outed, b.n * 8)
                    r = rows(t)
                    for o in range(NC):
                        pe.wait_ge(exped, b.total(2 * KT, 2 * t + o + 1))
                        for j in range(4):
                            p = 4 * o + j
                            last = pe.matmul(out_ps[32 * j:32 * j + 32, 0, o, :], V[b.par][0:r, t, 32 * p:32 * p + 32],
                                             PR[p_buf(b, t)][0:r, P * p:P * p + P], start=(t == 0 and o == 0),
                                             stop=(t == KT - 1), skip_group_check=True, tile_position=(0, 32 * j))
                    last.then_inc(pv_done, 1)

                def totals(b):
                    pe.wait_ge(acc_done, b.total(KT - 1, KT - 1))
                    for p in range(NPAIR):
                        o, j = p // 4, p % 4
                        last = pe.matmul(out_ps[32 * j:32 * j + 32, 1, o, :], ones[:, 0:32],
                                         acc[b.par][:, P * p:P * p + P], start=False, stop=True,
                                         skip_group_check=True, tile_position=(0, 32 * j))
                    last.then_inc(summed, 1)

                def step(prev, b, q, r):
                    for t in range(KT):
                        scores(b, t)
                        uses = SLOTS[t] if q is not None else []
                        first = (len(uses) + 1) // 2
                        for n in uses[:first]:
                            key_use(q, r, n)
                        if t == 0 and prev is not None:
                            totals(prev)
                        if t >= 1:
                            products(b, t - 1)
                        for n in uses[first:]:
                            key_use(q, r, n)
                    products(b, KT - 1)
                    if q is not None:
                        key_use(q, r, len(NUMBERED) - 1)

                pe.wait_ge(rows_set, 4)
                for i, n in enumerate(K_USES):
                    same = [j for j in range(i) if (K_USES[j] - n) % RING == 0]
                    if same:
                        pe.wait_ge(out_ring["K"], same[-1] + 1)
                    key_use(None, fixed(0), n)
                pe.wait_ge(out_ring["K"], COUNT["K"])
                for n in range(len(NUMBERED)):
                    key_use(fixed(0), fixed(1), n)
                step(None, fixed(0), fixed(1), fixed(2))
                step(fixed(0), fixed(1), fixed(2), fixed(3))
                with pe.Fori(0, (NB - 4) // 2) as k:
                    b1, b2, b3, b4, b5, b6 = run_of(k)
                    step(b1, b2, b3, b4)
                    step(b2, b3, b4, b5)
                step(fixed(NB - 3), fixed(NB - 2), fixed(NB - 1), None)
                step(fixed(NB - 2), fixed(NB - 1), None, None)
                totals(fixed(NB - 1))


GTOK = 256
NS = 2
NGT = TOK // GTOK // NS
GTT = GTOK // P
GB = GTOK // TQ
HID = 1024
NHC = HID // P
NHP = NHC // 2
TRING = 4

TUSES = ([("O", 0), ("Z1", 0), ("X", 0), ("X", 1), ("X", 2), ("Y", 0), ("Z2", 0), ("CR", 0)]
         + [("CK", i) for i in range(NHP)] + [("CV", 0), ("Z3", 0)]
         + [("FC", i) for i in range(NHP)] + [("FP", 0)])
TKINDS = ["O", "Z1", "X", "Y", "Z2", "CR", "CK", "CV", "Z3", "FC", "FP"]
TCOUNT = {k: sum(u[0] == k for u in TUSES) for k in TKINDS}


def tail_bank(kind, j):
    return TUSES.index((kind, j)) % TRING


def tail_before(kind, j):
    n = TUSES.index((kind, j)) - TRING
    return TUSES[n] if n >= 0 else None


def tail_block(nc, w, out, ident, xN, combT):
    with ExitStack() as st:
        def sb(name, shape, dt=F32):
            return st.enter_context(nc.sbuf_tensor(name, shape, dt))

        def both(name, shape):
            return [sb(f"{name}_{s}", shape) for s in range(NS)]

        def sem(name):
            return st.enter_context(nc.semaphore(name))

        def sems(name):
            return [sem(f"{name}_{s}") for s in range(NS)]

        wo = sb("wo", [P, NC, D])
        wkvr = sb("wkvr", [P, 3, NC, D])
        wcr = sb("wcr", [P, NC, D])
        wck = sb("wck", [P, NC, HID])
        wcv = sb("wcv", [P, NHC, D])
        wfc = sb("wfc", [P, NC, HID])
        wfp = sb("wfp", [P, NHC, D])
        bo_row = sb("bo_row", [P, D])
        cols = sb("cols", [P, 6, NC])
        low_u = sb("low_u", [16, HID])
        low_v = sb("low_v", [16, D])
        fast = sb("fast", [16, 16])
        gate = sb("gate", [16, 1])
        mix = sb("mix", [16, HID])

        ps = [st.enter_context(nc.psum_tensor(f"tps{i}", [P, 512], F32)) for i in range(NS * TRING)]
        weights_in = sem("weights_in")
        weight_block(nc, w, ident, ps, weights_in, wo, wkvr, wcr, wck, wcv, wfc, wfp, bo_row, cols,
                     low_u, low_v, fast, gate, mix, xN)

        x1, y, z, y2, xy, x2, res = (both(n, [P, GTT, D]) for n in ("x1", "y", "z", "y2", "xy", "x2", "res"))
        stats = both("tstats", [P, GTT, 6])
        mv = both("tmv", [P, 7, GTT])
        veps = both("tveps", [P, GTT])
        rstd = both("trstd", [P, GTT])
        rn = both("rn", [P, 4, GTT])
        power = sb("tpower", [P, GTT])
        eps_t = sb("eps_t", [P, GTT])
        hT, dT, xT, kT, vT, eT = (both(n, [P, NC, GTOK]) for n in ("hT", "dT", "xT", "kT", "vT", "eT"))
        top, sT, lT, pT, aT, mT = (both(n, [P, NC, GTOK]) for n in ("top", "sT", "lT", "pT", "aT", "mT"))
        cb = kT
        rw = lT
        rl = [[aT[s], sT[s]] for s in range(NS)]
        cr, crs, cri = ([a[s][:, :, :] for s in range(NS)] for a in (eT, mT, pT))
        bb = both("bb", [P, NC, GTOK])
        nT = both("nT", [P, NC, GTOK])
        low = sb("low", [P, NC, GTOK])
        dd = both("dd", [P, 2, NC, GTOK])
        ee = both("ee", [P, 2, NC, GTOK])
        hid = both("hid", [P, NHC, GTOK])

        full = [{k: sem(f"full_{k}_{s}") for k in TKINDS} for s in range(NS)]
        free = [{k: sem(f"free_{k}_{s}") for k in TKINDS} for s in range(NS)]
        preset = sem("preset")
        cb_in, y_out, again = sems("cb_in"), sems("y_out"), sems("again")
        ln_stat, ln_aggr, ln_eps, ln_rstd, ln_out = (
            sems(n) for n in ("ln_stat", "ln_aggr", "ln_eps", "ln_rstd", "ln_out"))
        shifted, mixed, wkv, exps, squared, summed, stored, gated = (
            sems(n) for n in ("shifted", "mixed", "wkv", "exps", "squared", "xy_in", "stored", "gated"))
        NLN, NWKV, NEXP, NAG = 3, 26, 4, 6

        def bank(s, kind, j=0):
            return ps[TRING * s + tail_bank(kind, j)]

        def in_two(a):
            return a[:, :].rearrange("p (n d) -> p n d", n=2)

        def flat(a):
            return a[:, :, :].rearrange("p c k -> p (c k)")

        def steps(a):
            return a[:, :, :].rearrange("p c (b t) -> p (c b) t", t=TQ)

        def both_streams(eng, entry, first, second, pair):
            entry(0, 0)
            first(0, 0)
            entry(1, 0)
            pair(1, 0, 0, 0, True)
            with eng.Fori(1, NGT - 1) as g:
                pair(0, g, 1, g - 1, True)
                pair(1, g, 0, g, True)
            pair(0, NGT - 1, 1, NGT - 2, True)
            pair(1, NGT - 1, 0, NGT - 1, False)
            second(1, NGT - 1)

        with nc.Block() as block:
            @block.sync
            def _(sp):
                def store(s, g):
                    sp.wait_ge(free[s]["FP"], g + 1)
                    sp.dma_start(out[bass.ds((NS * g + s) * GTT, GTT), :, :].rearrange("n p d -> p n d"),
                                 res[s][:]).then_inc(stored[s], 16)

                store(0, 0)
                with sp.Fori(1, NGT) as g:
                    store(1, g - 1)
                    store(0, g)
                store(1, NGT - 1)
                for s in range(NS):
                    sp.wait_ge(stored[s], 16 * NGT + 16)

            @block.gpsimd
            def _(pool):
                def root(s, g, k):
                    pool.wait_ge(ln_eps[s], NLN * g + k + 1)
                    pool.tensor_tensor(rstd[s][:], veps[s][:], power[:], ALU.pow).then_inc(ln_rstd[s], 1)

                def root_again(s, g):
                    r = rn[s]
                    base = 4 * g
                    pool.wait_ge(ln_rstd[s], NLN * g + 1)
                    pool.tensor_tensor(r[:, 0, :], mv[s][:, 6, :], rstd[s][:], ALU.mult).then_inc(again[s], 1)
                    pool.wait_ge(again[s], base + 1)
                    pool.tensor_tensor(r[:, 1, :], r[:, 0, :], rstd[s][:], ALU.mult).then_inc(again[s], 1)
                    pool.wait_ge(again[s], base + 2)
                    pool.tensor_tensor(r[:, 2, :], r[:, 1, :], eps_t[:], ALU.add).then_inc(again[s], 1)
                    pool.wait_ge(again[s], base + 3)
                    pool.tensor_tensor(r[:, 3, :], r[:, 2, :], power[:], ALU.pow).then_inc(again[s], 1)

                def residuals(s, g):
                    pool.wait_ge(free[s]["Y"], g + 1)
                    pool.tensor_tensor(xy[s][:], x1[s][:], y2[s][:], ALU.add).then_inc(summed[s], 1)

                def entry(s, g):
                    root(s, g, 0)
                    root_again(s, g)

                def first(s, g):
                    root(s, g, 1)
                    residuals(s, g)

                def second(s, g):
                    root(s, g, 2)

                def pair(x, gx, y, gy, more):
                    root(y, gy, 2)
                    if more:
                        entry(y, gy + 1)
                    first(x, gx)

                for s in range(NS):
                    pool.memset(res[s][:], 0.0).then_inc(stored[s], 16)
                    pool.memset(bb[s][:], 0.0).then_inc(preset, 1)
                    pool.memset(nT[s][:], 0.0).then_inc(preset, 1)
                pool.memset(power[:], -0.5).then_inc(preset, 1)
                pool.memset(eps_t[:], EPS).then_inc(preset, 1)
                pool.memset(low[:], 3.0e38).then_inc(preset, 1)
                pool.wait_ge(preset, 7)
                pool.memset(steps(low)[:, :, 0:1], 0.0).then_inc(preset, 1)
                both_streams(pool, entry, first, second, pair)

            @block.scalar
            def _(act):
                def take(s, g, kind, j=0):
                    act.wait_ge(full[s][kind], TCOUNT[kind] * g + j + 1)
                    return bank(s, kind, j)

                def affine(s, g, kind, k):
                    b = take(s, g, kind)
                    for c in range(NC):
                        ins = act.activation(hT[s][:, c, :], in_two(b)[:, c, :], ACT.Identity,
                                             bias=cols[:, k + 1, c:c + 1], scale=cols[:, k, c:c + 1])
                        ins.then_inc(free[s][kind], 1)

                def keys(s, g):
                    act.copy(kT[s][:], in_two(take(s, g, "X", 0))).then_inc(free[s]["X"], 1)

                def values(s, g):
                    act.copy(vT[s][:], in_two(take(s, g, "X", 1))).then_inc(free[s]["X"], 1)

                def gates(s, g):
                    act.activation(eT[s][:], in_two(take(s, g, "X", 2)), ACT.Exp, scale=-1.0).then_inc(free[s]["X"], 1)

                def exp_pair(s, g, after):
                    act.wait_ge(wkv[s], NWKV * g + after)
                    act.activation(ee[s][:], dd[s][:], ACT.Exp).then_inc(exps[s], 1)

                def log(s, g):
                    act.wait_ge(wkv[s], NWKV * g + 7)
                    act.activation(lT[s][:], sT[s][:], ACT.Ln).then_inc(exps[s], 1)

                def receptance(s, g):
                    act.activation(cr[s], in_two(take(s, g, "CR")), ACT.Exp, scale=-1.0).then_inc(free[s]["CR"], 1)

                def hidden(s, g, r, i):
                    kind = "FC" if r else "CK"
                    b = take(s, g, kind, i)
                    if r or i >= 2:
                        act.wait_ge(squared[s], 2 * NHP * g + r * NHP + i - 1)
                    act.activation(rl[s][i % 2][:], in_two(b), ACT.Relu).then_inc(free[s][kind], 1)
                    act.wait_ge(free[s][kind], NHP * g + i + 1)
                    act.activation(hid[s][:, 2 * i:2 * i + 2, :], rl[s][i % 2][:], ACT.Square).then_inc(squared[s], 1)

                def plain(s, g):
                    act.copy(hT[s][:], in_two(take(s, g, "Z3"))).then_inc(free[s]["Z3"], 1)

                def entry(s, g):
                    affine(s, g, "Z1", 0)

                def first(s, g):
                    keys(s, g)
                    exp_pair(s, g, 4)
                    log(s, g)
                    values(s, g)
                    exp_pair(s, g, 11)
                    gates(s, g)
                    exp_pair(s, g, 19)
                    affine(s, g, "Z2", 2)

                def second(s, g):
                    hidden(s, g, 0, 0)
                    receptance(s, g)
                    for i in range(1, NHP):
                        hidden(s, g, 0, i)
                    plain(s, g)
                    for i in range(NHP):
                        hidden(s, g, 1, i)

                def pair(x, gx, y, gy, more):
                    hidden(y, gy, 0, 0)
                    receptance(y, gy)
                    for i in range(1, NHP):
                        hidden(y, gy, 0, i)
                    keys(x, gx)
                    exp_pair(x, gx, 4)
                    log(x, gx)
                    values(x, gx)
                    exp_pair(x, gx, 11)
                    gates(x, gx)
                    plain(y, gy)
                    hidden(y, gy, 1, 0)
                    exp_pair(x, gx, 19)
                    for i in range(1, NHP):
                        hidden(y, gy, 1, i)
                    affine(x, gx, "Z2", 2)
                    if more:
                        entry(y, gy + 1)

                both_streams(act, entry, first, second, pair)

            @block.vector
            def _(dve):
                def take(s, g, kind, j=0):
                    dve.wait_ge(full[s][kind], TCOUNT[kind] * g + j + 1)
                    return bank(s, kind, j)

                def deviation(s, g, k, src):
                    m = mv[s]
                    for n in range(GTT):
                        dve.bn_stats(stats[s][:, n, :], src[:, n, :]).then_inc(ln_stat[s], 1)
                    dve.wait_ge(ln_stat[s], (NLN * g + k + 1) * GTT)
                    even, odd = stats[s][:, :, 1:3], stats[s][:, :, 4:6]
                    dve.tensor_tensor(m[:, 0, :], even[:, :, 0], odd[:, :, 0], ALU.add).then_inc(ln_aggr[s], 1)
                    dve.tensor_tensor(m[:, 1, :], even[:, :, 0], odd[:, :, 0], ALU.subtract).then_inc(ln_aggr[s], 1)
                    dve.tensor_tensor(m[:, 2, :], even[:, :, 1], odd[:, :, 1], ALU.add).then_inc(ln_aggr[s], 1)
                    dve.wait_ge(ln_aggr[s], (NLN * g + k) * NAG + 3)
                    dve.tensor_scalar(m[:, 3, :], m[:, 0, :], 0.5, None, ALU.mult).then_inc(ln_aggr[s], 1)
                    dve.tensor_tensor(m[:, 4, :], m[:, 1, :], m[:, 1, :], ALU.mult).then_inc(ln_aggr[s], 1)
                    dve.wait_ge(ln_aggr[s], (NLN * g + k) * NAG + 5)
                    dve.scalar_tensor_tensor(m[:, 5, :], m[:, 4, :], D / 4.0, m[:, 2, :],
                                             ALU.mult, ALU.add).then_inc(ln_aggr[s], 1)
                    dve.wait_ge(ln_aggr[s], (NLN * g + k) * NAG + 6)
                    if k == 0:
                        dve.tensor_scalar(m[:, 6, :], m[:, 5, :], 1.0 / D, None, ALU.mult).then_inc(y_out[s], 1)
                    dve.tensor_scalar(veps[s][:], m[:, 5, :], 1.0 / D, EPS, ALU.mult, ALU.add).then_inc(ln_eps[s], 1)

                def scaled(s, g, k, src, dst, done):
                    dve.wait_ge(ln_rstd[s], NLN * g + k + 1)
                    for n in range(GTT):
                        dve.tensor_scalar(dst[:, n, :], src[:, n, :], mv[s][:, 3, n:n + 1], rstd[s][:, n:n + 1],
                                          ALU.subtract, ALU.mult).then_inc(done, 1)

                def fetch(s, g):
                    dve.tensor_copy(cb[s][:], combT[:, :, bass.ds((NS * g + s) * GTOK, GTOK)]).then_inc(cb_in[s], 1)

                def enter(s, g):
                    dve.tensor_tensor(x1[s][:], in_two(take(s, g, "O")), xN[:, bass.ds((NS * g + s) * GTT, GTT), :],
                                      ALU.add).then_inc(free[s]["O"], 1)
                    dve.wait_ge(free[s]["O"], g + 1)
                    deviation(s, g, 0, x1[s])

                def enter_end(s, g, after):
                    scaled(s, g, 0, x1[s], y[s], y_out[s])
                    dve.wait_ge(y_out[s], 3 * g + 3)
                    if after:
                        dve.wait_ge(full[s]["Z3"], g)
                    dve.wait_ge(again[s], 4 * g + 4)
                    for n in range(GTT):
                        dve.tensor_scalar(z[s][:, n, :], y[s][:, n, :], rn[s][:, 3, n:n + 1], None,
                                          ALU.mult).then_inc(ln_out[s], 1)

                def mixing(s):
                    for c in range(NC):
                        dve.scalar_tensor_tensor(xT[s][:, c, :], dT[s][:, c, :], cols[:, 4, c:c + 1], hT[s][:, c, :],
                                                 ALU.mult, ALU.add).then_inc(mixed[s], 1)

                def time_mix(s, g):
                    d, h = steps(dT[s]), steps(hT[s])
                    dve.wait_ge(free[s]["Z1"], NC * g + NC)
                    dve.tensor_tensor(d[:, :, 1:TQ], h[:, :, 1:TQ], h[:, :, 0:TQ - 1], ALU.subtract).then_inc(shifted[s], 1)
                    for c in range(NC):
                        dve.tensor_scalar(d[:, GB * c:GB * c + GB, 0:1], h[:, GB * c:GB * c + GB, 0:1],
                                          cols[:, 4, c:c + 1], None, ALU.subtract).then_inc(shifted[s], 1)
                    dve.wait_ge(shifted[s], 5 * g + 3)
                    mixing(s)

                def channel_mix(s, g):
                    d, h = steps(dT[s]), steps(hT[s])
                    dve.wait_ge(free[s]["Z2"], NC * g + NC)
                    dve.tensor_tensor(d[:, :, 1:TQ], h[:, :, 0:TQ - 1], h[:, :, 1:TQ], ALU.subtract).then_inc(shifted[s], 1)
                    dve.tensor_tensor(d[:, :, 0:1], h[:, :, TQ - 1:TQ], h[:, :, 0:1], ALU.subtract).then_inc(shifted[s], 1)
                    dve.wait_ge(shifted[s], 5 * g + 5)
                    mixing(s)

                def did(s, g, j):
                    dve.wait_ge(wkv[s], NWKV * g + j)

                def running_max(s, g):
                    da, db, t = steps(dd[s][:, 0, :, :]), dd[s][:, 1, :, :], steps(top[s])
                    dve.wait_ge(free[s]["X"], 3 * g + 1)
                    dve.tensor_tensor_scan(flat(top[s]), flat(low), flat(kT[s]), 0.0, ALU.min, ALU.max).then_inc(wkv[s], 1)
                    did(s, g, 1)
                    dve.tensor_tensor(da[:, :, 1:TQ], t[:, :, 0:TQ - 1], t[:, :, 1:TQ], ALU.subtract).then_inc(wkv[s], 1)
                    dve.tensor_scalar(da[:, :, 0:1], t[:, :, 0:1], -1.0, None, ALU.mult).then_inc(wkv[s], 1)
                    dve.tensor_tensor(db, kT[s][:], top[s][:], ALU.subtract).then_inc(wkv[s], 1)

                def sum_scan(s, g):
                    ea, eb = ee[s][:, 0, :, :], ee[s][:, 1, :, :]
                    dve.wait_ge(exps[s], NEXP * g + 1)
                    dve.tensor_tensor(steps(eb)[:, :, 0:1], steps(eb)[:, :, 0:1], steps(ea)[:, :, 0:1],
                                      ALU.add).then_inc(wkv[s], 1)
                    did(s, g, 5)
                    dve.memset(steps(ea)[:, :, 0:1], 0.0).then_inc(wkv[s], 1)
                    did(s, g, 6)
                    dve.tensor_tensor_scan(flat(sT[s]), flat(ea), flat(eb), 0.0, ALU.mult, ALU.add).then_inc(wkv[s], 1)

                def log_before(s, g):
                    da, db = dd[s][:, 0, :, :], dd[s][:, 1, :, :]
                    dve.wait_ge(exps[s], NEXP * g + 2)
                    dve.tensor_tensor(steps(bb[s])[:, :, 1:TQ], steps(top[s])[:, :, 0:TQ - 1],
                                      steps(lT[s])[:, :, 0:TQ - 1], ALU.add).then_inc(wkv[s], 1)
                    did(s, g, 8)
                    dve.tensor_tensor(pT[s][:], bb[s][:], kT[s][:], ALU.max).then_inc(wkv[s], 1)
                    did(s, g, 9)
                    dve.tensor_tensor(da, bb[s][:], pT[s][:], ALU.subtract).then_inc(wkv[s], 1)
                    dve.tensor_tensor(db, kT[s][:], pT[s][:], ALU.subtract).then_inc(wkv[s], 1)

                def value_scan(s, g):
                    da, db = dd[s][:, 0, :, :], dd[s][:, 1, :, :]
                    ea, eb = ee[s][:, 0, :, :], ee[s][:, 1, :, :]
                    dve.wait_ge(exps[s], NEXP * g + 3)
                    dve.wait_ge(free[s]["X"], 3 * g + 2)
                    dve.tensor_tensor(mT[s][:], eb, vT[s][:], ALU.mult).then_inc(wkv[s], 1)
                    dve.memset(steps(ea)[:, :, 0:1], 0.0).then_inc(wkv[s], 1)
                    did(s, g, 13)
                    dve.tensor_tensor_scan(flat(aT[s]), flat(ea), flat(mT[s]), 0.0, ALU.mult, ALU.add).then_inc(wkv[s], 1)
                    for c in range(NC):
                        dve.scalar_tensor_tensor(pT[s][:, c, :], kT[s][:, c, :], cols[:, 5, c:c + 1], bb[s][:, c, :],
                                                 ALU.add, ALU.max).then_inc(wkv[s], 1)
                    did(s, g, 16)
                    dve.tensor_tensor(da, bb[s][:], pT[s][:], ALU.subtract).then_inc(wkv[s], 1)
                    for c in range(NC):
                        dve.scalar_tensor_tensor(db[:, c, :], kT[s][:, c, :], cols[:, 5, c:c + 1], pT[s][:, c, :],
                                                 ALU.add, ALU.subtract).then_inc(wkv[s], 1)

                def quotient(s, g):
                    ea, eb = ee[s][:, 0, :, :], ee[s][:, 1, :, :]
                    dve.wait_ge(exps[s], NEXP * g + 4)
                    dve.tensor_tensor(steps(nT[s])[:, :, 1:TQ], steps(ea)[:, :, 1:TQ], steps(aT[s])[:, :, 0:TQ - 1],
                                      ALU.mult).then_inc(wkv[s], 1)
                    dve.tensor_tensor(mT[s][:], eb, vT[s][:], ALU.mult).then_inc(wkv[s], 1)
                    dve.tensor_tensor(sT[s][:], ea, eb, ALU.add).then_inc(wkv[s], 1)
                    did(s, g, 21)
                    dve.tensor_tensor(aT[s][:], nT[s][:], mT[s][:], ALU.add).then_inc(wkv[s], 1)
                    did(s, g, 22)
                    dve.wait_ge(free[s]["X"], 3 * g + 3)
                    dve.scalar_tensor_tensor(pT[s][:], eT[s][:], 1.0, sT[s][:], ALU.add, ALU.mult).then_inc(wkv[s], 1)
                    did(s, g, 24)
                    dve.reciprocal(sT[s][:], pT[s][:]).then_inc(wkv[s], 1)
                    did(s, g, 25)
                    dve.tensor_tensor(rw[s][:], aT[s][:], sT[s][:], ALU.mult).then_inc(wkv[s], 1)

                def middle(s, g):
                    dve.tensor_tensor(y2[s][:], in_two(take(s, g, "Y")), y[s][:], ALU.add).then_inc(free[s]["Y"], 1)
                    dve.wait_ge(free[s]["Y"], g + 1)
                    deviation(s, g, 1, y2[s])

                def middle_end(s, g):
                    scaled(s, g, 1, y2[s], z[s], ln_out[s])

                def receptance(s, g):
                    dve.wait_ge(free[s]["CR"], g + 1)
                    dve.tensor_scalar(crs[s], cr[s], 1.0, None, ALU.add).then_inc(gated[s], 1)
                    dve.wait_ge(gated[s], 3 * g + 1)
                    dve.reciprocal(cri[s], crs[s]).then_inc(gated[s], 1)

                def channel_out(s, g):
                    dve.wait_ge(gated[s], 3 * g + 2)
                    dve.tensor_tensor(cr[s], in_two(take(s, g, "CV")), cri[s], ALU.mult).then_inc(free[s]["CV"], 1)
                    dve.wait_ge(free[s]["CV"], g + 1)
                    dve.wait_ge(summed[s], g + 1)
                    dve.tensor_tensor(x2[s][:], cr[s], xy[s][:], ALU.add).then_inc(gated[s], 1)
                    dve.wait_ge(gated[s], 3 * g + 3)
                    deviation(s, g, 2, x2[s])

                def channel_end(s, g):
                    scaled(s, g, 2, x2[s], z[s], ln_out[s])

                def leave(s, g):
                    b = take(s, g, "FP")
                    dve.wait_ge(stored[s], 16 * g + 16)
                    dve.tensor_tensor(res[s][:], in_two(b), x2[s][:], ALU.add).then_inc(free[s]["FP"], 1)

                def entry(s, g):
                    fetch(s, g)
                    enter(s, g)
                    enter_end(s, g, False)
                    time_mix(s, g)

                def first(s, g):
                    running_max(s, g)
                    sum_scan(s, g)
                    log_before(s, g)
                    value_scan(s, g)
                    quotient(s, g)
                    middle(s, g)
                    middle_end(s, g)
                    channel_mix(s, g)

                def second(s, g):
                    receptance(s, g)
                    channel_out(s, g)
                    channel_end(s, g)
                    leave(s, g)

                def pair(x, gx, y, gy, more):
                    receptance(y, gy)
                    running_max(x, gx)
                    sum_scan(x, gx)
                    log_before(x, gx)
                    channel_out(y, gy)
                    channel_end(y, gy)
                    if more:
                        fetch(y, gy + 1)
                    value_scan(x, gx)
                    quotient(x, gx)
                    if more:
                        enter(y, gy + 1)
                    middle(x, gx)
                    if more:
                        enter_end(y, gy + 1, True)
                    middle_end(x, gx)
                    channel_mix(x, gx)
                    if more:
                        time_mix(y, gy + 1)
                    leave(y, gy)

                dve.wait_ge(preset, 8)
                both_streams(dve, entry, first, second, pair)

            @block.tensor
            def _(pe):
                def give(s, g, kind, j=0):
                    before = tail_before(kind, j)
                    if before:
                        k, m = before
                        reads = NC if k in ("Z1", "Z2") else 1
                        pe.wait_ge(free[s][k], TCOUNT[k] * reads * g + (m + 1) * reads)
                    return bank(s, kind, j)

                def turn(s, g, kind, norms):
                    pe.wait_ge(ln_out[s], norms * GTT)
                    b = give(s, g, kind)
                    for c in range(NC):
                        for n in range(GTT):
                            last = pe.transpose(b[:, GTOK * c + P * n:GTOK * c + P * n + P],
                                                z[s][:, n, P * c:P * c + P], ident[:])
                    last.then_inc(full[s][kind], 1)

                def by_tokens(s, g, kind, src, wt, n_in, between=None):
                    b = give(s, g, kind)
                    for n in range(GTT):
                        for c in range(n_in):
                            last = pe.matmul(b[:, D * n:D * n + D], src[:, c, P * n:P * n + P], wt[:, c, :],
                                             start=(c == 0), stop=(c == n_in - 1))
                        if n == 0 and between is not None:
                            between()
                    last.then_inc(full[s][kind], 1)

                def by_channels(s, g, kind, j, wt, o, src):
                    b = give(s, g, kind, j)
                    for i in range(2):
                        for c in range(NC):
                            last = pe.matmul(b[:, GTOK * i:GTOK * i + GTOK], wt[:, c, P * (o + i):P * (o + i) + P],
                                             src[:, c, :], start=(c == 0), stop=(c == NC - 1))
                    last.then_inc(full[s][kind], 1)

                def turn_in(s, g, after=False):
                    if after:
                        pe.wait_ge(free[s]["FC"], NHP * g)
                    turn(s, g, "Z1", NLN * g + 1)

                def project(s, g, after=False):
                    pe.wait_ge(cb_in[s], g + 1)
                    if after:
                        pe.wait_ge(free[s]["FC"], NHP * g - 1)
                    by_tokens(s, g, "O", cb[s], wo, NC)

                def keys(s, g, after=False):
                    if after:
                        pe.wait_ge(free[s]["FP"], g)
                    pe.wait_ge(mixed[s], 4 * g + 2)
                    by_channels(s, g, "X", 0, wkvr[:, 0, :, :], 0, xT[s])

                def values(s, g):
                    for m in (1, 2):
                        by_channels(s, g, "X", m, wkvr[:, m, :, :], 0, xT[s])

                def turn_back(s, g):
                    pe.wait_ge(wkv[s], NWKV * g + 26)
                    b = give(s, g, "Y")
                    for n in range(GTT):
                        for c in range(NC):
                            last = pe.transpose(b[:, D * n + P * c:D * n + P * c + P], rw[s][:, c, P * n:P * n + P], ident[:])
                    last.then_inc(full[s]["Y"], 1)

                def channel_keys(s, g):
                    pe.wait_ge(mixed[s], 4 * g + 4)
                    by_tokens(s, g, "CR", xT[s], wcr, NC)
                    for i in range(NHP):
                        by_channels(s, g, "CK", i, wck, 2 * i, xT[s])

                def channel_values(s, g):
                    pe.wait_ge(squared[s], 2 * NHP * g + NHP)
                    by_tokens(s, g, "CV", hid[s], wcv, NHC)

                def feed_in(s, g):
                    pe.wait_ge(free[s]["Z3"], g + 1)
                    for i in range(NHP):
                        by_channels(s, g, "FC", i, wfc, 2 * i, hT[s])

                def feed_out(s, g, between=None):
                    pe.wait_ge(squared[s], 2 * NHP * g + 2 * NHP)
                    by_tokens(s, g, "FP", hid[s], wfp, NHC, between)

                def entry(s, g, after=False):
                    project(s, g, after)
                    turn_in(s, g, after)

                def first(s, g):
                    keys(s, g)
                    values(s, g)
                    turn_back(s, g)
                    turn(s, g, "Z2", NLN * g + 2)

                def second(s, g):
                    channel_keys(s, g)
                    channel_values(s, g)
                    turn(s, g, "Z3", NLN * g + 3)
                    feed_in(s, g)
                    feed_out(s, g)

                def pair(x, gx, y, gy, more):
                    channel_keys(y, gy)
                    keys(x, gx, not (isinstance(gx, int) and gx == 0))
                    channel_values(y, gy)
                    values(x, gx)
                    turn(y, gy, "Z3", NLN * gy + 3)
                    feed_in(y, gy)
                    if more:
                        project(y, gy + 1, True)
                    turn_back(x, gx)

                    def turns():
                        turn(x, gx, "Z2", NLN * gx + 2)
                        if more:
                            turn_in(y, gy + 1, True)
                    feed_out(y, gy, turns)

                both_streams(pe, entry, first, second, pair)


def weight_block(nc, w, ident, ps, weights_in, wo, wkvr, wcr, wck, wcv, wfc, wfp, bo_row, cols,
                 low_u, low_v, fast, gate, mix, xN):
    MAGIC = 1.5 * 2.0 ** 23
    with ExitStack() as st:
        def sem(name):
            return st.enter_context(nc.semaphore(name))

        def sb(name, shape):
            return st.enter_context(nc.sbuf_tensor(name, shape, F32))

        shapes = [(NHC, D), (NC, HID)]
        nat = [sb(f"nat{m}", [P, r, n]) for m, (r, n) in enumerate(shapes)]
        u1 = [sb(f"u1{m}", [P, r, n]) for m, (r, n) in enumerate(shapes)]
        u2 = [sb(f"u2{m}", [P, r, n]) for m, (r, n) in enumerate(shapes)]
        mean = [sb(f"mean{m}", [P, r]) for m, (r, n) in enumerate(shapes)]
        scale = [sb(f"scale{m}", [P, r]) for m, (r, n) in enumerate(shapes)]
        inv = [sb(f"inv{m}", [P, r]) for m, (r, n) in enumerate(shapes)]
        nat_in, low_in, terned, turned, kept, low_ps, low_kept, biased = (
            sem("nat_in"), sem("low_in"), sem("terned"), sem("w_turned"), sem("w_kept"), sem("low_ps"),
            sem("low_kept"), sem("biased"))
        with nc.Block() as block:
            @block.sync
            def _(sp):
                sp.dma_start(nat[0][:], w["w_fc"].rearrange("(r p) n -> p r n", p=P)).then_inc(nat_in, 16)
                sp.dma_start(nat[1][:], w["w_proj"].rearrange("(r p) n -> p r n", p=P)).then_inc(nat_in, 16)
                for dst, name in ((low_u, "u_T"), (low_v, "v"), (fast, "fast_b"), (gate, "gate"), (bo_row, "b_o")):
                    sp.dma_start(dst[:], w[name]).then_inc(low_in, 16)
                sp.dma_start(wo[:], w["w_o"].rearrange("(c p) n -> p c n", p=P)).then_inc(weights_in, 16)
                for m, name in enumerate(("wk_T", "wv_T", "wr_T")):
                    sp.dma_start(wkvr[:, m, :, :], w[name].rearrange("(c p) n -> p c n", p=P)).then_inc(weights_in, 16)
                sp.dma_start(wcr[:], w["wcr_T"].rearrange("(c p) n -> p c n", p=P)).then_inc(weights_in, 16)
                sp.dma_start(wck[:], w["wck_T"].rearrange("(c p) n -> p c n", p=P)).then_inc(weights_in, 16)
                sp.dma_start(wcv[:], w["wcv_T"].rearrange("(c p) n -> p c n", p=P)).then_inc(weights_in, 16)
                sp.dma_start(cols[:], w["cols"]).then_inc(weights_in, 16)
                sp.wait_ge(weights_in, 16 * 8)

            @block.gpsimd
            def _(pool):
                pool.wait_ge(low_in, 16 * 5)
                for n in range(NTT):
                    pool.tensor_tensor(xN[:, n, :], xN[:, n, :], bo_row[:], ALU.add).then_inc(biased, 1)

            @block.vector
            def _(dve):
                dve.wait_ge(nat_in, 32)
                done = 0
                for m, (r, n) in enumerate(shapes):
                    dve.tensor_reduce(mean[m][:], nat[m][:], AX.X, ALU.add, apply_absolute_value=True).then_inc(terned, 1)
                    dve.wait_ge(terned, done + 1)
                    dve.tensor_scalar(scale[m][:], mean[m][:], 1.0 / n, 1e-5, ALU.mult, ALU.max).then_inc(terned, 1)
                    dve.wait_ge(terned, done + 2)
                    dve.reciprocal(inv[m][:], scale[m][:]).then_inc(terned, 1)
                    dve.wait_ge(terned, done + 3)
                    for i in range(r):
                        dve.tensor_scalar(u1[m][:, i, :], nat[m][:, i, :], inv[m][:, i:i + 1], -1.0,
                                          ALU.mult, ALU.max).then_inc(terned, 1)
                    dve.wait_ge(terned, done + 3 + r)
                    dve.tensor_scalar(u2[m][:], u1[m][:], 1.0, MAGIC, ALU.min, ALU.add).then_inc(terned, 1)
                    dve.wait_ge(terned, done + 4 + r)
                    dve.scalar_tensor_tensor(u1[m][:], u2[m][:], MAGIC, nat[m][:], ALU.subtract,
                                             ALU.subtract).then_inc(terned, 1)
                    dve.wait_ge(terned, done + 5 + r)
                    dve.tensor_tensor(u2[m][:], u1[m][:], nat[m][:], ALU.add).then_inc(terned, 1)
                    dve.wait_ge(terned, done + 6 + r)
                    for i in range(r):
                        dve.tensor_scalar(u1[m][:, i, :], u2[m][:, i, :], scale[m][:, i:i + 1], None,
                                          ALU.mult).then_inc(terned, 1)
                    done += 6 + 2 * r
                dve.wait_ge(low_in, 16 * 5)
                for i in range(2):
                    dve.wait_ge(low_ps, i + 1)
                    dve.tensor_scalar(mix[:, 512 * i:512 * i + 512], ps[i][0:16, :], gate[:, 0:1], None,
                                      ALU.mult).then_inc(low_kept, 1)
                for b in range(4):
                    k, i = b // 2, b % 2
                    dve.wait_ge(kept, b + 1)
                    dve.wait_ge(low_ps, 2 + b + 1)
                    dve.tensor_tensor(wfc[:, k, 512 * i:512 * i + 512], ps[b][:, :],
                                      wfc[:, k, 512 * i:512 * i + 512], ALU.add).then_inc(low_kept, 1)

            @block.scalar
            def _(act):
                for b in range(4):
                    k, i = b // 2, b % 2
                    act.wait_ge(turned, b + 1)
                    act.copy(wfc[:, k, 512 * i:512 * i + 512], ps[4 + b][:, :]).then_inc(kept, 1)
                for b in range(4):
                    act.wait_ge(turned, 4 + b + 1)
                    act.copy(wfp[:, 2 * b:2 * b + 2, :],
                             ps[4 + b][:, :].rearrange("p (h d) -> p h d", h=2)).then_inc(kept, 1)

            @block.tensor
            def _(pe):
                pe.wait_ge(low_in, 16 * 5)
                for i in range(2):
                    pe.matmul(ps[i][0:16, :], fast[:, :], low_u[:, 512 * i:512 * i + 512],
                              start=True, stop=True).then_inc(low_ps, 1)
                pe.wait_ge(low_kept, 2)
                for b in range(4):
                    k, i = b // 2, b % 2
                    pe.matmul(ps[b][:, :], low_v[:, P * k:P * k + P], mix[:, 512 * i:512 * i + 512],
                              start=True, stop=True).then_inc(low_ps, 1)
                pe.wait_ge(terned, 6 + 2 * NHC)
                for b in range(4):
                    k, i = b // 2, b % 2
                    for h in range(4):
                        last = pe.transpose(ps[4 + b][:, P * h:P * h + P], u1[0][:, 4 * i + h, P * k:P * k + P], ident[:])
                    last.then_inc(turned, 1)
                pe.wait_ge(terned, 12 + 2 * NHC + 2 * NC)
                for b in range(4):
                    pe.wait_ge(kept, b + 1)
                    for h in range(2):
                        for o in range(NC):
                            last = pe.transpose(ps[4 + b][:, D * h + P * o:D * h + P * o + P],
                                                u1[1][:, o, P * (2 * b + h):P * (2 * b + h) + P], ident[:])
                    last.then_inc(turned, 1)


def kernel(**inputs):
    import numpy as _np
    import concourse.bacc as _bacc
    from concourse import mybir as _mybir
    from concourse.bass_utils import run_bass_kernel_spmd as _run

    a = {k: _np.asarray(v) for k, v in inputs.items()}

    def turned(name):
        return _np.ascontiguousarray(a[name].T)

    def columns(v):
        return _np.ascontiguousarray(v.reshape(NC, P).T)

    first = (_np.arange(P) % 32 < DK).astype(_np.float32)
    data = {
        "x": a["x"],
        "ctx_T": _np.ascontiguousarray(a["ctx_1024"].transpose(0, 2, 1)),
        "ident": _np.eye(P, dtype=_np.float32),
        "half": _np.stack([first, 1 - first], axis=1),
        "w_q": a["L0_xattn_W_Q"], "w_k": a["L0_xattn_W_K"], "w_v": a["L0_xattn_W_V"], "w_o": a["L0_xattn_W_O"],
        "b_q": columns(a["L0_xattn_b_Q"]), "b_k": columns(a["L0_xattn_b_K"]), "b_v": columns(a["L0_xattn_b_V"]),
        "b_o": _np.ascontiguousarray(_np.broadcast_to(a["L0_xattn_b_O"], (P, D))),
        "wk_T": turned("L0_attn_Wk"), "wv_T": turned("L0_attn_Wv"), "wr_T": turned("L0_attn_Wr"),
        "wcr_T": turned("L0_attn_Wcr"), "wck_T": turned("L0_attn_Wck"), "wcv_T": turned("L0_attn_Wcv"),
        "cols": _np.ascontiguousarray(_np.stack(
            [columns(a["L0_attn_" + n].reshape(D)) for n in
             ("ln1_w", "ln1_b", "ln2_w", "ln2_b", "time_shift", "time_first")], axis=1)),
        "w_fc": a["L0_ffn_w_fc"], "w_proj": a["L0_ffn_w_proj"], "u_T": turned("L0_ffn_u"), "v": a["L0_ffn_v"],
        "fast_b": a["L0_ffn_fast_b"],
        "gate": _np.ascontiguousarray(_np.broadcast_to(a["L0_ffn_gate"].reshape(1, 1), (16, 1))),
    }
    nc = _bacc.Bacc("TRN2", target_bir_lowering=False, num_devices=1)
    t = {n: nc.dram_tensor(f"in_{n}", v.shape, _mybir.dt.from_np(v.dtype), kind="ExternalInput").ap()
         for n, v in data.items()}
    out = nc.dram_tensor("out_dram", (NTT, P, D), F32, kind="ExternalOutput").ap()
    perceiver_kernel(nc, t, out)
    r = _run(nc, [{f"in_{n}": v for n, v in data.items()}], core_ids=[0])
    return r.results[0]["out_dram"].reshape(NB, TQ, D)
```

```python
from contextlib import ExitStack

import numpy as np

import concourse.bass as bass
from concourse import mybir

F32 = mybir.dt.float32
F16 = mybir.dt.float16
ALU = mybir.AluOpType
ACT = mybir.ActivationFunctionType
AX = mybir.AxisListType

P = 128
NB, TQ, D = 32, 64, 256
NKEY = 1601
NH, DK = 16, 16
NC = D // P
NPAIR = NH // 2
KT = (NKEY + P - 1) // P
KLAST = NKEY - (KT - 1) * P
KPAD = KT * P
GT = 4
NG = (KT + GT - 1) // GT
HID = 1024
NHC = HID // P
MAGIC = 1.5 * 2.0 ** 23
GW = [min(512, NKEY - 512 * g) for g in range(NG)]
TOK = NB * TQ
NTT = TOK // P
EPS = 1e-5
TWO_OF_256 = float(np.full(2, 256.0, np.float16).view(np.float32)[0])
MSC = 1.0 / 256.0


def rows(t):
    return P if t < KT - 1 else KLAST


RING = 4
SC = 3


def spread(few, many):
    out = []
    for n, m in enumerate(many):
        if n * len(few) // len(many) != (n - 1) * len(few) // len(many):
            out.append(few[n * len(few) // len(many)])
        out.append(m)
    return out


def key_side_order():
    k = [("K", o, g) for o in range(NC) for g in range(NG)]
    v = [("V", u) for u in range((KT + 1) // 2)]
    maxima = []
    for h in range(2):
        maxima += [("B", p, g) for p in range(4 * h, 4 * h + 4) for g in range(NG - 1)] + [("R", h)]
    early, after = 4, 3
    return v[:early] + spread(v[early:] + k[:-after], maxima) + k[-after:] + [("M",)]


USES = key_side_order()
COUNT = {k: sum(u[0] == k for u in USES) for k in "KVBRM"}
COST = {"K": 1.28, "V": 1.3, "B": 0.45, "R": 0.4, "M": 0.3}


def numbered(uses):
    seen = dict.fromkeys("KVBRM", 0)
    out = []
    for u in uses:
        out.append((u[0], u[1:], seen[u[0]]))
        seen[u[0]] += 1
    return out


NUMBERED = numbered(USES)
K_USES = [n for n, u in enumerate(NUMBERED) if u[0] == "K"]


def ring_slot(q, n):
    if q is None:
        return K_USES.index(n) % RING
    return (n + q.par * len(USES)) % RING


def previous_in_slot(n, with_k):
    m = n - RING
    while m >= 0 and NUMBERED[m][0] == "K" and not with_k:
        m -= RING
    last_batch = 1 if m < 0 else 0
    kind, _, j = NUMBERED[m % len(NUMBERED)]
    return kind, j, last_batch


def score_bank_before(j):
    if j >= SC:
        return j - SC, 0
    return max(i for i in range(2 * KT) if i % SC == j), 1


def in_slots():
    body = range(len(NUMBERED) - 1)
    whole = sum(COST[NUMBERED[n][0]] for n in body)
    slots = [[] for _ in range(KT)]
    done = 0.0
    for n in body:
        slots[min(KT - 1, int(done / whole * KT))].append(n)
        done += COST[NUMBERED[n][0]]
    return slots


SLOTS = in_slots()

SPLITS = {0: 0, 1: 1, 2: 2, 3: 3}


class Batch:

    def __init__(self, n, half, par, back):
        self.n, self.half, self.par, self.back = n, half, par, back

    def total(self, per, j):
        return self.n * per + j


def fixed(n):
    return Batch(n, n // 2, n % 2, n)


def run_of(k):
    return (Batch(2 * k + 1, k, 1, 1), Batch(2 * k + 2, k + 1, 0, 2), Batch(2 * k + 3, k + 1, 1, 2),
            Batch(2 * k + 4, k + 2, 0, 2), Batch(2 * k + 5, k + 2, 1, 2), Batch(2 * k + 6, k + 3, 0, 2))


def perceiver_kernel(nc: bass.Bass, t, out):
    q_rows = nc.dram_tensor("q_rows", (96, NPAIR, NB * P), F16, kind="Internal").ap()
    with ExitStack() as st:
        def sb(name, shape, dt=F32):
            return st.enter_context(nc.sbuf_tensor(name, shape, dt))

        ident = sb("ident", [P, P])
        xN = sb("xN", [P, NTT, D])
        combT = sb("combT", [P, NC, TOK])
        wo = sb("wo", [P, NC, D])
        cols = sb("cols", [P, 6, NC])
        ctx_w = sb("ctx_w", [P, 2 * NC * NKEY])
        ctxT = [ctx_w[:, i * NC * NKEY:(i + 1) * NC * NKEY].rearrange("p (c k) -> p c k", c=NC) for i in range(2)]
        wfc = ctx_w[:, 0:NC * HID].rearrange("p (c n) -> p c n", c=NC)
        wfp = ctx_w[:, NC * HID:2 * NC * HID].rearrange("p (h d) -> p h d", h=NHC)
        with ExitStack() as st2:
            def sb2(name, shape, dt=F32):
                return st2.enter_context(nc.sbuf_tensor(name, shape, dt))

            ident16 = sb2("ident16", [P, P], F16)
            half = sb2("half", [P, 2])
            halfq = sb2("halfq", [P, 2])
            ones = sb2("ones", [P, 32])
            wkh, wkl, wvh, wvl = (sb2(n, [P, NC, D], F16) for n in ("wkh", "wkl", "wvh", "wvl"))
            bq_c, bk_c, bv_c = (sb2(n, [P, NC]) for n in ("bq_c", "bk_c", "bv_c"))
            bo_row = sb2("bo_row", [P, D])
            cTh = [sb2(f"cTh{i}", [P, NC, KPAD], F16) for i in range(2)]
            cTl = [sb2(f"cTl{i}", [P, NC, KPAD], F16) for i in range(2)]
            ctx_full = [st2.enter_context(nc.semaphore(f"ctx_full{i}")) for i in range(2)]
            ctx_high, ctx_split, q_out = (st2.enter_context(nc.semaphore(n)) for n in ("ctx_high", "ctx_split", "q_out"))
            ctx = (t["ctx_T"], ctxT, cTh, cTl, ctx_full, ctx_high, ctx_split)
            setup_block(nc, t["x"], t["w_q"], t["b_q"], t["w_k"], t["b_k"], t["w_v"], t["b_v"], t["ident"], t["half"],
                        q_rows, ident, ident16, half, halfq, ones, xN, wkh, wkl, wvh, wvl, bq_c, bk_c, bv_c,
                        t["b_o"], bo_row, ctx, q_out)
            attention_block(nc, ctx, q_rows, q_out, ident, ident16, half, ones, wkh, wkl, wvh, wvl,
                            bk_c, bv_c, bo_row, xN, combT, t, ctx_w, wfc, wfp, wo, cols)
        tail_block(nc, t, out, ident, xN, combT, wfc, wfp, wo, cols)


def setup_block(nc, x, wq, bq, wk, bk, wv, bv, ident_in, half_in, q_rows,
                ident, ident16, half, halfq, ones, xN, wkh, wkl, wvh, wvl, bq_c, bk_c, bv_c,
                bo_in, bo_row, ctx, q_out):
    ctx_in, ctxT, cTh, cTl, ctx_full, ctx_high, ctx_split = ctx
    XC = 4
    XT = NTT // XC
    NQ = TOK // 512
    with ExitStack() as st:
        def sb(name, shape, dt):
            return st.enter_context(nc.sbuf_tensor(name, shape, dt))

        def sem(name):
            return st.enter_context(nc.semaphore(name))

        wq_s = sb("wq_s", [P, NC, D], F32)
        wk_s = sb("wk_s", [P, NC, D], F32)
        wv_s = sb("wv_s", [P, NC, D], F32)
        stats = sb("stats", [P, NTT, 6], F32)
        mv = sb("mv", [P, NTT, 2], F32)
        power = sb("power", [P, NTT], F32)
        veps = sb("veps", [P, NTT], F32)
        rstd = sb("rstd", [P, NTT], F32)
        xn = sb("xn", [P, NTT, D], F32)
        xnT = sb("xnT", [P, NC, TOK], F32)
        qf = sb("qf", [P, 2, 8, 2, TQ], F32)
        qh = sb("qh", [P, NC, NB, 2 * TQ], F16)
        ql = sb("ql", [P, NC, NB, 2 * TQ], F16)
        ps_t = [st.enter_context(nc.psum_tensor(f"ps_t{i}", [P, 512], F32)) for i in range(4)]
        ps_q = [st.enter_context(nc.psum_tensor(f"ps_q{i}", [P, 512], F32)) for i in range(4)]

        w_in, c_in = sem("w_in"), sem("c_in")
        x_in = [sem(f"x_in{i}") for i in range(XC)]
        bqs = sb("bqs", [P, NC], F32)
        bq_in = sem("bq_in")
        consts, split = sem("consts"), sem("split")
        stat, aggr, eps_in, rstd_in, normed = sem("stat"), sem("aggr"), sem("eps_in"), sem("rstd_in"), sem("normed")
        turned, copied, q_ps, q_f0, q_f1, q_hi, q_lo = (
            sem("turned"), sem("copied"), sem("q_ps"), sem("q_f0"), sem("q_f1"), sem("q_hi"), sem("q_lo"))

        with nc.Block() as block:
            @block.sync
            def _(sp):
                for i in range(XC):
                    n = slice(XT * i, XT * i + XT)
                    sp.dma_start(xN[:, n, :], x.rearrange("b t d -> (b t) d").rearrange("(n p) d -> p n d", p=P)[:, n, :]
                                 ).then_inc(x_in[i], 16)
                for dst, src in ((ident, ident_in), (half, half_in)):
                    sp.dma_start(dst[:], src).then_inc(c_in, 16)
                for dst, src in ((bq_c, bq), (bk_c, bk), (bv_c, bv)):
                    sp.dma_start(dst[:], src).then_inc(c_in, 16)
                for dst, src in ((wq_s, wq), (wk_s, wk), (wv_s, wv)):
                    sp.dma_start(dst[:], src.rearrange("(c p) n -> p c n", p=P)).then_inc(w_in, 16)
                for i in range(2):
                    sp.dma_start(ctxT[i][:, :, :], ctx_in[i:i + 1, :, :].rearrange("a (c p) k -> p (a c) k", p=P)
                                 ).then_inc(ctx_full[i], 16)
                sp.dma_start(bo_row[:], bo_in).then_inc(c_in, 16)
                for p in range(NPAIR):
                    o, r = p // 4, 32 * (p % 4)
                    sp.wait_ge(q_lo, NQ * (o + 1))
                    sp.wait_ge(q_hi, NQ * (o + 1))
                    for blk, src in ((0, qh), (1, ql), (2, qh)):
                        sp.dma_start(q_rows[32 * blk:32 * blk + 32, p, :],
                                     src[r:r + 32, o, :, :].rearrange("p b t -> p (b t)")).then_inc(q_out, 16)
                sp.wait_ge(c_in, 16 * 6)
                sp.wait_ge(q_out, 16 * 3 * NPAIR)

            @block.gpsimd
            def _(pool):
                pool.memset(power[:], -0.5).then_inc(consts, 1)
                pool.memset(ones[:], 1.0).then_inc(consts, 1)
                pool.wait_ge(consts, 2)
                pool.wait_ge(eps_in, 1)
                pool.tensor_tensor(rstd[:], veps[:], power[:], ALU.pow).then_inc(rstd_in, 1)

            @block.vector
            def _(dve):
                for n in range(NTT):
                    if n % XT == 0:
                        dve.wait_ge(x_in[n // XT], 16)
                    dve.bn_stats(stats[:, n, :], xN[:, n, :]).then_inc(stat, 1)
                for n in range(NTT):
                    dve.wait_ge(stat, n + 1)
                    dve.bn_aggr(mv[:, n, :], stats[:, n, :]).then_inc(aggr, 1)
                dve.wait_ge(aggr, NTT)
                dve.tensor_scalar(veps[:], mv[:, :, 1], EPS, None, ALU.add).then_inc(eps_in, 1)
                dve.wait_ge(c_in, 16 * 5)
                dve.wait_ge(w_in, 16 * 3)
                dve.tensor_copy(ident16[:], ident[:]).then_inc(split, 1)
                dve.tensor_scalar(halfq[:], half[:], float(DK) ** -0.5, None, ALU.mult).then_inc(split, 1)
                dve.tensor_copy(wkh[:], wk_s[:]).then_inc(split, 1)
                dve.tensor_copy(wvh[:], wv_s[:]).then_inc(split, 1)
                dve.wait_ge(split, 4)
                dve.tensor_tensor(wkl[:], wk_s[:], wkh[:], ALU.subtract).then_inc(split, 1)
                dve.tensor_tensor(wvl[:], wv_s[:], wvh[:], ALU.subtract).then_inc(split, 1)
                dve.wait_ge(rstd_in, 1)
                for n in range(NTT):
                    dve.tensor_scalar(xn[:, n, :], xN[:, n, :], mv[:, n, 0:1], rstd[:, n:n + 1],
                                      ALU.subtract, ALU.mult).then_inc(normed, 1)
                dve.tensor_scalar(bqs[:], bq_c[:], halfq[:, 1:2], None, ALU.mult).then_inc(bq_in, 1)

                def low(k):
                    o, n = k // NQ, k % NQ
                    dve.wait_ge(q_hi, k + 1)
                    dve.tensor_tensor(ql[:, o, 8 * n:8 * n + 8, :], qf[:, k % 2, :, :, :].rearrange("p b h t -> p b (h t)"),
                                      qh[:, o, 8 * n:8 * n + 8, :], ALU.subtract).then_inc(q_lo, 1)

                def split_ctx(q, g):
                    w = slice(512 * g, 512 * g + GW[g])
                    dve.wait_ge(ctx_high, q * NG + g + 1)
                    dve.tensor_tensor(cTl[q][:, :, w], ctxT[q][:, :, w], cTh[q][:, :, w],
                                      ALU.subtract).then_inc(ctx_split, 1)

                for o in range(NC):
                    for n in range(NQ):
                        k = o * NQ + n
                        dve.wait_ge(q_ps, k + 1)
                        if k >= 2:
                            dve.wait_ge(q_lo, k - 1)
                            dve.wait_ge(q_hi, k - 1)
                        dve.tensor_scalar(qf[:, k % 2, :, 0, :], ps_q[k % 4][:, :].rearrange("p (b t) -> p b t", t=TQ),
                                          bq_c[:, o:o + 1], halfq[:, 0:1], ALU.add, ALU.mult).then_inc(q_f0, 1)
                        if k >= 1:
                            low(k - 1)
                low(NC * NQ - 1)
                for q in range(2):
                    for g in range(NG):
                        split_ctx(q, g)

            @block.scalar
            def _(act):
                for c in range(NC):
                    for n in range(NQ):
                        k = c * NQ + n
                        act.wait_ge(turned, k + 1)
                        act.copy(xnT[:, c, 512 * n:512 * n + 512], ps_t[k % 4][:, :]).then_inc(copied, 1)
                for o in range(NC):
                    for n in range(NQ):
                        k = o * NQ + n
                        act.wait_ge(q_f0, k + 1)
                        if k == 0:
                            act.wait_ge(bq_in, 1)
                        if k >= 2:
                            act.wait_ge(q_lo, k - 1)
                            act.wait_ge(q_hi, k - 1)
                        act.activation(qf[:, k % 2, :, 1, :], ps_q[k % 4][:, :].rearrange("p (b t) -> p b t", t=TQ),
                                       ACT.Identity, bias=bqs[:, o:o + 1], scale=halfq[:, 1:2]).then_inc(q_f1, 1)
                        act.wait_ge(q_f1, k + 1)
                        act.copy(qh[:, o, 8 * n:8 * n + 8, :],
                                 qf[:, k % 2, :, :, :].rearrange("p b h t -> p b (h t)")).then_inc(q_hi, 1)
                for q in range(2):
                    act.wait_ge(ctx_full[q], 16)
                    for g in range(NG):
                        w = slice(512 * g, 512 * g + GW[g])
                        act.copy(cTh[q][:, :, w], ctxT[q][:, :, w]).then_inc(ctx_high, 1)

            @block.tensor
            def _(pe):
                pe.wait_ge(c_in, 16 * 5)
                pe.wait_ge(w_in, 16 * 3)
                for c in range(NC):
                    for n in range(NQ):
                        k = c * NQ + n
                        pe.wait_ge(normed, 4 * n + 4)
                        if k >= 4:
                            pe.wait_ge(copied, k - 3)
                        for j in range(4):
                            last = pe.transpose(ps_t[k % 4][:, P * j:P * j + P], xn[:, 4 * n + j, P * c:P * c + P], ident[:])
                        last.then_inc(turned, 1)
                pe.wait_ge(copied, NC * NQ)
                for o in range(NC):
                    for n in range(NQ):
                        k = o * NQ + n
                        if k >= 4:
                            pe.wait_ge(q_f0, k - 3)
                            pe.wait_ge(q_f1, k - 3)
                        for c in range(NC):
                            last = pe.matmul(ps_q[k % 4][:, :], wq_s[:, c, P * o:P * o + P],
                                             xnT[:, c, 512 * n:512 * n + 512], start=(c == 0), stop=(c == NC - 1))
                        last.then_inc(q_ps, 1)


def attention_block(nc, ctx, q_rows, q_out, ident, ident16, half, ones, wkh, wkl, wvh, wvl, bk_c, bv_c,
                    bo_row, xN, combT, w, ctx_w, wfc, wfp, wo, cols):
    ctx_in, ctxT, cTh, cTl, ctx_full, ctx_high, ctx_split = ctx
    with ExitStack() as st:
        def sb(name, shape, dt):
            return st.enter_context(nc.sbuf_tensor(name, shape, dt))

        def sem(name):
            return st.enter_context(nc.semaphore(name))

        Kh = sb("Kh", [P, NC, KPAD], F16)
        Kl = sb("Kl", [P, NC, KPAD], F16)
        KS = [sb(f"KS{i}", [P, NPAIR, KPAD], F16) for i in range(2)]
        V = [sb(f"V{i}", [P, KT, D], F32) for i in range(2)]
        QS = [sb(f"QS{i}", [P, NPAIR, P], F16) for i in range(2)]
        PR = [sb(f"PR{i}", [P, NPAIR * P], F32) for i in range(3)]
        acc = [sb(f"acc{i}", [P, NPAIR * P], F32) for i in range(2)]
        mx = sb("mx", [P, NPAIR, NG], F32)
        nmx = sb("nmx", [P, NPAIR], F32)
        mparts = sb("mparts", [P, NPAIR, 2], F16)
        s_sel = sb("s_sel", [P, NC, TQ], F32)
        o_sel = sb("o_sel", [P, NC, TQ], F32)

        sc = [st.enter_context(nc.psum_tensor(f"sc{i}", [P, 512], F32)) for i in range(SC)]
        ring = [st.enter_context(nc.psum_tensor(f"ring{i}", [P, 512], F32)) for i in range(RING)]
        out_ps = st.enter_context(nc.psum_tensor("out_ps", [P, 2, NC, P], F32))

        qs_full = [sem(f"qs_full{i}") for i in range(2)]
        ks_full = [[sem(f"ks_full{o}{i}") for i in range(2)] for o in range(NC)]
        rows_set, k_rows_set = sem("rows_set"), [sem(f"k_rows_set{i}") for i in range(2)]
        in_ring = {k: sem(f"in_ring_{k}") for k in "KVBRM"}
        k_high = sem("k_high")
        biased = sem("biased")
        nat_in = [sem(f"nat_in{i}") for i in range(2)]
        first_in = sem("first_in")
        low_in, terned, turned, kept, low_ps, low_kept = (
            sem(n) for n in ("low_in", "terned", "w_turned", "w_kept", "low_ps", "low_kept"))

        shapes = [(NHC, D), (NC, HID)]
        words = KS[0][:, :, :].rearrange("p a k -> p (a k)")[:, 0:2 * 2 * NHC * D].bitcast(F32)
        nat = [ctx_w[:, 2 * NC * HID:2 * NC * HID + NHC * D].rearrange("p (r n) -> p r n", n=D),
               words[:, 0:NHC * D].rearrange("p (r n) -> p r n", n=HID)]
        tern = [words[:, NHC * D:2 * NHC * D].rearrange("p (r n) -> p r n", n=n) for r, n in shapes]
        mean, scale, inv = ([V[0][:, 11, 16 * j + NHC * m:16 * j + NHC * m + r] for m, (r, n) in enumerate(shapes)]
                            for j in range(3))
        low_u = V[0][0:16, 0:4, :].rearrange("p a d -> p (a d)")
        low_v = V[0][0:16, 4, :]
        mix = V[0][0:16, 5:9, :].rearrange("p a d -> p (a d)")
        fast = V[0][0:16, 9, 0:16]
        gate = V[0][0:16, 10, 0:1]
        out_ring = {k: sem(f"out_ring_{k}") for k in "KVBRM"}
        maxed = sem("maxed")
        scored, exped, pv_done, acc_done, summed, outed = (
            sem("scored"), sem("exped"), sem("pv_done"), sem("acc_done"), sem("summed"), sem("outed"))

        def p_buf(b, t):
            return (t + b.par) % 3

        def p_before(b, t):
            if t >= 3:
                return t - 3, 0
            return max(s for s in range(KT) if (s + 1 - b.par) % 3 == (t + b.par) % 3), 1

        with nc.Block() as block:
            @block.sync
            def _(sp):
                def load_ctx(q):
                    if q.back >= 2:
                        sp.wait_ge(ctx_split, (q.n - 1) * NG)
                    sp.dma_start(ctxT[q.par][:, :, :],
                                 ctx_in[bass.ds(q.n, 1), :, :].rearrange("a (c p) k -> p (a c) k", p=P)
                                 ).then_inc(ctx_full[q.par], 16)

                def load_rows(q):
                    if q.back >= 2:
                        sp.wait_ge(scored, (q.n - 1) * 2 * KT)
                    sp.dma_start(QS[q.par][0:96, :, :],
                                 q_rows[:, :, bass.ds(q.n * P, P)]).then_inc(qs_full[q.par], 16)
                    for o in range(NC):
                        sp.wait_ge(k_high, q.total(COUNT["K"], NG * (o + 1)))
                        for p in range(4 * o, 4 * o + 4):
                            r = 32 * (p % 4)
                            for blk in (0, 1):
                                sp.dma_start(KS[q.par][32 * blk:32 * blk + 32, p, 0:NKEY],
                                             Kh[r:r + 32, o, 0:NKEY]).then_inc(ks_full[o][q.par], 16)
                        sp.wait_ge(out_ring["K"], q.total(COUNT["K"], NG * (o + 1)))
                        for p in range(4 * o, 4 * o + 4):
                            r = 32 * (p % 4)
                            sp.dma_start(KS[q.par][64:96, p, 0:NKEY],
                                         Kl[r:r + 32, o, 0:NKEY]).then_inc(ks_full[o][q.par], 16)

                load_rows(fixed(0))
                load_ctx(fixed(2))
                load_ctx(fixed(3))
                load_rows(fixed(1))
                load_ctx(fixed(4))
                load_rows(fixed(2))
                with sp.Fori(0, (NB - 6) // 2) as k:
                    b1, b2, b3, b4, b5, b6 = run_of(k)
                    load_ctx(b5)
                    load_rows(b3)
                    load_ctx(b6)
                    load_rows(b4)
                load_ctx(fixed(NB - 1))
                for n in range(NB - 3, NB):
                    load_rows(fixed(n))
                sp.wait_ge(ctx_split, NB * NG)
                sp.dma_start(nat[0], w["w_fc"].rearrange("(r p) n -> p r n", p=P)).then_inc(nat_in[0], 16)
                sp.wait_ge(scored, (NB - 1) * 2 * KT)
                sp.dma_start(nat[1], w["w_proj"].rearrange("(r p) n -> p r n", p=P)).then_inc(nat_in[1], 16)
                sp.wait_ge(pv_done, (NB - 1) * KT)
                for dst, name in ((low_u, "u_T"), (low_v, "v"), (fast, "fast_b"), (gate, "gate")):
                    sp.dma_start(dst, w[name]).then_inc(low_in, 16)
                sp.dma_start(wo[:], w["w_o"].rearrange("(c p) n -> p c n", p=P)).then_inc(first_in, 16)
                sp.dma_start(cols[:], w["cols"]).then_inc(first_in, 16)
                sp.wait_ge(first_in, 32)

            @block.gpsimd
            def _(pool):
                def sums(b):
                    for t in range(1, KT):
                        pool.wait_ge(exped, b.total(2 * KT, 2 * t + 2))
                        r = rows(t)
                        a = acc[b.par][0:r, :]
                        if t == 1:
                            if b.back >= 2:
                                pool.wait_ge(summed, b.n - 1)
                            pool.tensor_tensor(a, PR[p_buf(b, 0)][:, :], PR[p_buf(b, 1)][:, :],
                                               ALU.add).then_inc(acc_done, 1)
                        else:
                            pool.wait_ge(acc_done, b.total(KT - 1, t - 1))
                            pool.tensor_tensor(a, a, PR[p_buf(b, t)][0:r, :], ALU.add).then_inc(acc_done, 1)

                for i in range(2):
                    pool.memset(QS[i][96:128, :, :], 0.0).then_inc(rows_set, 1)
                pool.wait_ge(rows_set, 2)
                pool.memset(KS[1][96:128, :, :].bitcast(F32), TWO_OF_256).then_inc(k_rows_set[1], 1)
                pool.wait_ge(k_rows_set[1], 1)
                for n in range(NTT):
                    pool.tensor_tensor(xN[:, n, :], xN[:, n, :], bo_row[:], ALU.add).then_inc(biased, 1)
                sums(fixed(0))
                sums(fixed(1))
                with pool.Fori(0, (NB - 2) // 2) as k:
                    sums(Batch(2 * k + 2, k + 1, 0, 2))
                    sums(Batch(2 * k + 3, k + 1, 1, 2))

            @block.scalar
            def _(act):
                def split(q, g):
                    w = slice(512 * g, 512 * g + GW[g])
                    if g == 0:
                        act.wait_ge(ctx_full[q.par], 16 * (q.half + 1))
                        if q.back >= 2:
                            act.wait_ge(in_ring["V"], (q.n - 1) * COUNT["V"])
                    act.copy(cTh[q.par][:, :, w], ctxT[q.par][:, :, w]).then_inc(ctx_high, 1)

                def key_use(q, r, n):
                    kind, a, j = NUMBERED[n]
                    if kind not in "KV":
                        return
                    if kind == "K":
                        if r is None:
                            return
                    bank = ring[ring_slot(q, n)]
                    if kind == "K":
                        q = r
                    act.wait_ge(in_ring[kind], q.total(COUNT[kind], j + 1))
                    if kind == "K":
                        o, g = a
                        if g == 0 and q.back >= 1:
                            act.wait_ge(ks_full[o][1 - q.par], 16 * 12 * (q.half + q.par))
                        act.activation(Kh[:, o, 512 * g:512 * g + GW[g]], bank[:, 0:GW[g]], ACT.Identity,
                                       bias=bk_c[:, o:o + 1]).then_inc(k_high, 1)
                    else:
                        u, = a
                        if u == 0 and q.back >= 2:
                            act.wait_ge(pv_done, (q.n - 1) * KT)
                        r = rows(2 * u)
                        nt = 2 if 2 * u + 1 < KT else 1
                        act.copy(V[q.par][0:r, 2 * u:2 * u + nt, :],
                                 bank[0:r, 0:D * nt].rearrange("p (t d) -> p t d", t=nt)).then_inc(out_ring["V"], 1)

                def step(b, q, r):
                    for t in range(KT):
                        s, before = p_before(b, t)
                        if b.back >= before:
                            act.wait_ge(pv_done, (b.n - before) * KT + s + 1)
                            act.wait_ge(acc_done, (b.n - before) * (KT - 1) + max(s, 1))
                        m = rows(t)
                        for j in (2 * t, 2 * t + 1):
                            act.wait_ge(scored, b.total(2 * KT, j + 1))
                            act.activation(PR[p_buf(b, t)][0:m, 512 * (j % 2):512 * (j % 2) + 512], sc[j % SC][0:m, :],
                                           ACT.Exp).then_inc(exped, 1)
                        if q is not None:
                            for n in SLOTS[t]:
                                key_use(q, r, n)
                        if r is not None and t in SPLITS:
                            split(r, SPLITS[t])

                for n in K_USES:
                    key_use(None, fixed(0), n)
                for n in range(len(NUMBERED) - 1):
                    key_use(fixed(0), fixed(1), n)
                step(fixed(0), fixed(1), fixed(2))
                step(fixed(1), fixed(2), fixed(3))
                with act.Fori(0, (NB - 4) // 2) as k:
                    b1, b2, b3, b4, b5, b6 = run_of(k)
                    step(b2, b3, b4)
                    step(b3, b4, b5)
                step(fixed(NB - 2), fixed(NB - 1), None)
                step(fixed(NB - 1), None, None)
                act.wait_ge(ctx_split, NB * NG)
                for b in range(4):
                    k, i = b // 2, b % 2
                    act.wait_ge(turned, b + 1)
                    act.copy(wfc[:, k, 512 * i:512 * i + 512], ring[b][:, :]).then_inc(kept, 1)
                for b in range(4):
                    act.wait_ge(turned, 4 + b + 1)
                    act.copy(wfp[:, 2 * b:2 * b + 2, :],
                             ring[b][:, :].rearrange("p (h d) -> p h d", h=2)).then_inc(kept, 1)

            @block.vector
            def _(dve):
                def split(q, g):
                    w = slice(512 * g, 512 * g + GW[g])
                    dve.wait_ge(ctx_high, q.total(NG, g + 1))
                    dve.tensor_tensor(cTl[q.par][:, :, w], ctxT[q.par][:, :, w], cTh[q.par][:, :, w],
                                      ALU.subtract).then_inc(ctx_split, 1)

                def key_use(q, r, n):
                    kind, a, j = NUMBERED[n]
                    if kind == "V":
                        return
                    bank = ring[ring_slot(q, n)]
                    if kind == "K":
                        if r is None:
                            return
                        q = r
                        o, g = a
                        w = slice(512 * g, 512 * g + GW[g])
                        dve.wait_ge(k_high, q.total(COUNT["K"], j + 1))
                        dve.scalar_tensor_tensor(Kl[:, o, w], bank[:, 0:GW[g]], bk_c[:, o:o + 1], Kh[:, o, w],
                                                 ALU.add, ALU.subtract).then_inc(out_ring["K"], 1)
                    elif kind == "B":
                        p, g = a
                        dve.wait_ge(in_ring["B"], q.total(COUNT["B"], j + 1))
                        dve.tensor_reduce(mx[:, p, g:g + 1], bank[:, :], AX.X, ALU.max).then_inc(out_ring["B"], 1)
                    elif kind == "R":
                        h, = a
                        dve.wait_ge(in_ring["R"], q.total(COUNT["R"], j + 1))
                        dve.tensor_reduce(mx[:, 4 * h:4 * h + 4, NG - 1],
                                          bank[:, 0:4 * KLAST].rearrange("p (a k) -> p a k", a=4),
                                          AX.X, ALU.max).then_inc(out_ring["R"], 1)
                        if h == 1:
                            dve.wait_ge(out_ring["B"], q.total(COUNT["B"], COUNT["B"]))
                            dve.wait_ge(out_ring["R"], q.total(COUNT["R"], COUNT["R"]))
                            if q.back >= 1:
                                dve.wait_ge(in_ring["M"], q.n)
                            dve.tensor_reduce(nmx[:, :], mx[:, :, :], AX.X, ALU.max, negate=True).then_inc(maxed, 1)
                            dve.wait_ge(maxed, q.total(3, 1))
                            dve.tensor_scalar(mparts[:, :, 0], nmx[:, :], MSC, None, ALU.mult).then_inc(maxed, 1)
                            dve.wait_ge(maxed, q.total(3, 2))
                            dve.scalar_tensor_tensor(mparts[:, :, 1], nmx[:, :], MSC, mparts[:, :, 0],
                                                     ALU.mult, ALU.subtract).then_inc(maxed, 1)
                    else:
                        dve.wait_ge(in_ring["M"], q.total(1, 1))
                        if q.back < 2:
                            dve.wait_ge(rows_set, 2)
                        dve.tensor_copy(QS[q.par][96:98, :, :],
                                        bank[96:98, :].bitcast(F16).rearrange("p (a k) -> p a k", a=NPAIR)
                                        ).then_inc(out_ring["M"], 1)

                def finish(b):
                    dve.wait_ge(summed, b.total(1, 1))
                    if b.back >= 1:
                        dve.wait_ge(outed, b.n * 8)
                    dve.tensor_scalar(s_sel[:], out_ps[:, 1, :, 0:TQ], half[:, 0:1], None, ALU.mult).then_inc(outed, 1)
                    dve.tensor_scalar(o_sel[:], out_ps[:, 0, :, 0:TQ], half[:, 0:1], None, ALU.mult).then_inc(outed, 1)
                    dve.wait_ge(outed, b.total(8, 1))
                    dve.scalar_tensor_tensor(s_sel[:], out_ps[:, 1, :, TQ:P], half[:, 1:2], s_sel[:],
                                             ALU.mult, ALU.add).then_inc(outed, 1)
                    dve.wait_ge(outed, b.total(8, 2))
                    dve.scalar_tensor_tensor(o_sel[:], out_ps[:, 0, :, TQ:P], half[:, 1:2], o_sel[:],
                                             ALU.mult, ALU.add).then_inc(outed, 1)
                    dve.wait_ge(outed, b.total(8, 3))
                    dve.reciprocal(s_sel[:], s_sel[:]).then_inc(outed, 1)
                    dve.wait_ge(outed, b.total(8, 5))
                    dve.tensor_tensor(o_sel[:], o_sel[:], s_sel[:], ALU.mult).then_inc(outed, 1)
                    dve.wait_ge(outed, b.total(8, 6))
                    for c in range(NC):
                        dve.tensor_scalar(combT[:, c, bass.ds(b.n * TQ, TQ)], o_sel[:, c, :], bv_c[:, c:c + 1],
                                          None, ALU.add).then_inc(outed, 1)

                def ternary():
                    dve.wait_ge(pv_done, (NB - 1) * KT)
                    done = 0
                    for m, (r, n) in enumerate(shapes):
                        dve.wait_ge(nat_in[m], 16)
                        dve.tensor_reduce(mean[m], nat[m], AX.X, ALU.add, apply_absolute_value=True).then_inc(terned, 1)
                        dve.wait_ge(terned, done + 1)
                        dve.tensor_scalar(scale[m], mean[m], 1.0 / n, 1e-5, ALU.mult, ALU.max).then_inc(terned, 1)
                        dve.wait_ge(terned, done + 2)
                        dve.reciprocal(inv[m], scale[m]).then_inc(terned, 1)
                        dve.wait_ge(terned, done + 3)
                        if m == 0:
                            dve.wait_ge(scored, (NB - 1) * 2 * KT)
                        for i in range(r):
                            dve.tensor_scalar(tern[m][:, i, :], nat[m][:, i, :], inv[m][:, i:i + 1], -1.0,
                                              ALU.mult, ALU.max).then_inc(terned, 1)
                        dve.wait_ge(terned, done + 3 + r)
                        dve.tensor_scalar(tern[m], tern[m], 1.0, MAGIC, ALU.min, ALU.add).then_inc(terned, 1)
                        dve.wait_ge(terned, done + 4 + r)
                        dve.scalar_tensor_tensor(tern[m], tern[m], MAGIC, nat[m], ALU.subtract,
                                                 ALU.subtract).then_inc(terned, 1)
                        dve.wait_ge(terned, done + 5 + r)
                        dve.tensor_tensor(tern[m], tern[m], nat[m], ALU.add).then_inc(terned, 1)
                        dve.wait_ge(terned, done + 6 + r)
                        for i in range(r):
                            dve.tensor_scalar(nat[m][:, i, :], tern[m][:, i, :], scale[m][:, i:i + 1], None,
                                              ALU.mult).then_inc(terned, 1)
                        done += 6 + 2 * r
                        dve.wait_ge(terned, done)
                        if m == 0:
                            low_rank()

                def low_rank():
                    dve.wait_ge(low_in, 16 * 4)
                    for i in range(2):
                        dve.wait_ge(low_ps, i + 1)
                        dve.tensor_scalar(mix[:, 512 * i:512 * i + 512], ring[i][0:16, :], gate, None,
                                          ALU.mult).then_inc(low_kept, 1)

                def step(prev, q, r):
                    for t in range(KT):
                        for n in SLOTS[t]:
                            key_use(q, r, n)
                        if t == 0 and prev is not None:
                            finish(prev)
                        if r is not None and t in SPLITS:
                            split(r, SPLITS[t])
                    key_use(q, r, len(NUMBERED) - 1)

                for n in K_USES:
                    key_use(None, fixed(0), n)
                dve.memset(KS[0][96:128, :, :].bitcast(F32), TWO_OF_256).then_inc(k_rows_set[0], 1)
                for n in range(len(NUMBERED)):
                    key_use(fixed(0), fixed(1), n)
                step(None, fixed(1), fixed(2))
                step(fixed(0), fixed(2), fixed(3))
                with dve.Fori(0, (NB - 4) // 2) as k:
                    b1, b2, b3, b4, b5, b6 = run_of(k)
                    step(b1, b3, b4)
                    step(b2, b4, b5)
                step(fixed(NB - 3), fixed(NB - 1), None)
                finish(fixed(NB - 2))
                ternary()
                finish(fixed(NB - 1))

            @block.tensor
            def _(pe):
                def key_use(q, r, n):
                    kind, a, j = NUMBERED[n]
                    if kind == "K" and r is None:
                        return
                    if q is not None:
                        before, m, last_batch = previous_in_slot(n, r is not None)
                        if q.back >= last_batch:
                            ahead = 1 if before == "K" else 0
                            pe.wait_ge(out_ring[before], (q.n - last_batch + ahead) * COUNT[before] + m + 1)
                    bank = ring[ring_slot(q, n)]
                    if kind == "K":
                        q = r
                    if kind == "K":
                        o, g = a
                        pe.wait_ge(ctx_split, q.total(NG, g + 1))
                        w = slice(512 * g, 512 * g + GW[g])
                        ow = slice(P * o, P * o + P)
                        ch, cl = cTh[q.par], cTl[q.par]
                        terms = [(wkh, ch), (wkl, ch), (wkh, cl)]
                        for i, (wt, ct) in enumerate(terms):
                            for c in range(NC):
                                last = pe.matmul(bank[:, 0:GW[g]], wt[:, c, ow], ct[:, c, w],
                                                 start=(i == 0 and c == 0), stop=(i == 2 and c == NC - 1))
                    elif kind == "V":
                        u, = a
                        ch, cl = cTh[q.par], cTl[q.par]
                        for i in range(2):
                            t = 2 * u + i
                            if t >= KT:
                                continue
                            r = rows(t)
                            w = slice(P * t, P * t + r)
                            for c in range(NC):
                                for ct, wt in ((ch, wvh), (ch, wvl), (cl, wvh)):
                                    last = pe.matmul(bank[0:r, D * i:D * i + D], ct[:, c, w], wt[:, c, :],
                                                     start=(c == 0 and ct is ch and wt is wvh),
                                                     stop=(c == NC - 1 and ct is cl))
                    elif kind == "B":
                        p, g = a
                        if p % 4 == 0 and g == 0:
                            pe.wait_ge(ks_full[p // 4][q.par], 16 * 12 * (q.half + 1))
                            pe.wait_ge(qs_full[q.par], 16 * (q.half + 1))
                        last = pe.matmul(bank[:, :], QS[q.par][0:96, p, :], KS[q.par][0:96, p, 512 * g:512 * g + 512],
                                         start=True, stop=True)
                    elif kind == "R":
                        h, = a
                        for i in range(4):
                            last = pe.matmul(bank[:, KLAST * i:KLAST * i + KLAST], QS[q.par][0:96, 4 * h + i, :],
                                             KS[q.par][0:96, 4 * h + i, 512 * (NG - 1):NKEY], start=True, stop=True)
                    else:
                        pe.wait_ge(maxed, q.total(3, 3))
                        for p in range(NPAIR):
                            last = pe.transpose(bank[96:98, :].bitcast(F16)[:, P * p:P * p + P], mparts[:, p, :],
                                                ident16[:, :])
                    last.then_inc(in_ring[kind], 1)

                def scores(b, t):
                    if t == 0:
                        pe.wait_ge(out_ring["M"], b.total(1, 1))
                    r = rows(t)
                    for j in (2 * t, 2 * t + 1):
                        before, last_batch = score_bank_before(j)
                        if b.back >= last_batch:
                            pe.wait_ge(exped, (b.n - last_batch) * 2 * KT + before + 1)
                        for i in range(4):
                            p = 4 * (j % 2) + i
                            last = pe.matmul(sc[j % SC][0:r, P * i:P * i + P], KS[b.par][:, p, P * t:P * t + r],
                                             QS[b.par][:, p, :], start=True, stop=True)
                        last.then_inc(scored, 1)

                def products(b, t):
                    if t == 0:
                        pe.wait_ge(out_ring["V"], b.total(COUNT["V"], COUNT["V"]))
                        if b.back >= 1:
                            pe.wait_ge(outed, b.n * 8)
                    r = rows(t)
                    for o in range(NC):
                        pe.wait_ge(exped, b.total(2 * KT, 2 * t + o + 1))
                        for j in range(4):
                            p = 4 * o + j
                            last = pe.matmul(out_ps[32 * j:32 * j + 32, 0, o, :], V[b.par][0:r, t, 32 * p:32 * p + 32],
                                             PR[p_buf(b, t)][0:r, P * p:P * p + P], start=(t == 0 and o == 0),
                                             stop=(t == KT - 1), skip_group_check=True, tile_position=(0, 32 * j))
                    last.then_inc(pv_done, 1)

                def totals(b):
                    pe.wait_ge(acc_done, b.total(KT - 1, KT - 1))
                    for p in range(NPAIR):
                        o, j = p // 4, p % 4
                        last = pe.matmul(out_ps[32 * j:32 * j + 32, 1, o, :], ones[:, 0:32],
                                         acc[b.par][:, P * p:P * p + P], start=False, stop=True,
                                         skip_group_check=True, tile_position=(0, 32 * j))
                    last.then_inc(summed, 1)

                def low_rank():
                    pe.wait_ge(low_in, 16 * 4)
                    for i in range(2):
                        pe.matmul(ring[i][0:16, :], fast, low_u[:, 512 * i:512 * i + 512],
                                  start=True, stop=True).then_inc(low_ps, 1)

                def turn_w_fc(b):
                    k, i = b // 2, b % 2
                    pe.wait_ge(low_kept, 2)
                    pe.wait_ge(terned, 6 + 2 * NHC)
                    pe.matmul(ring[b][:, :], low_v[:, P * k:P * k + P], mix[:, 512 * i:512 * i + 512],
                              start=True, stop=False, skip_group_check=True)
                    for h in range(4):
                        last = pe.matmul(ring[b][:, P * h:P * h + P], nat[0][:, 4 * i + h, P * k:P * k + P], ident[:],
                                         start=False, stop=(h == 3), skip_group_check=True)
                    last.then_inc(turned, 1)

                def step(prev, b, q, r):
                    for t in range(KT):
                        if q is None and t == KT // 2:
                            low_rank()
                        if q is None and t >= KT - 4:
                            turn_w_fc(t - (KT - 4))
                        scores(b, t)
                        uses = SLOTS[t] if q is not None else []
                        first = (len(uses) + 1) // 2
                        for n in uses[:first]:
                            key_use(q, r, n)
                        if t == 0 and prev is not None:
                            totals(prev)
                        if t >= 1:
                            products(b, t - 1)
                        for n in uses[first:]:
                            key_use(q, r, n)
                    if q is not None:
                        key_use(q, r, len(NUMBERED) - 1)
                    products(b, KT - 1)

                for i, n in enumerate(K_USES):
                    if i >= RING:
                        pe.wait_ge(out_ring["K"], i - RING + 1)
                    key_use(None, fixed(0), n)
                pe.wait_ge(out_ring["K"], COUNT["K"])
                for n in range(len(NUMBERED)):
                    key_use(fixed(0), fixed(1), n)
                for i in range(2):
                    pe.wait_ge(k_rows_set[i], 1)
                step(None, fixed(0), fixed(1), fixed(2))
                step(fixed(0), fixed(1), fixed(2), fixed(3))
                with pe.Fori(0, (NB - 4) // 2) as k:
                    b1, b2, b3, b4, b5, b6 = run_of(k)
                    step(b1, b2, b3, b4)
                    step(b2, b3, b4, b5)
                step(fixed(NB - 3), fixed(NB - 2), fixed(NB - 1), None)
                step(fixed(NB - 2), fixed(NB - 1), None, None)
                totals(fixed(NB - 1))
                pe.wait_ge(terned, 12 + 2 * NHC + 2 * NC)
                for b in range(4):
                    pe.wait_ge(kept, b + 1)
                    for h in range(2):
                        for o in range(NC):
                            last = pe.transpose(ring[b][:, D * h + P * o:D * h + P * o + P],
                                                nat[1][:, o, P * (2 * b + h):P * (2 * b + h) + P], ident[:])
                    last.then_inc(turned, 1)


GTOK = 256
NS = 2
NGT = TOK // GTOK // NS
GTT = GTOK // P
GB = GTOK // TQ
NHP = NHC // 2
TRING = 4

TUSES = ([("O", 0), ("Z1", 0), ("X", 0), ("X", 1), ("X", 2), ("Y", 0), ("Z2", 0), ("CR", 0)]
         + [("CK", i) for i in range(NHP)] + [("CV", 0), ("Z3", 0)]
         + [("FC", i) for i in range(NHP)] + [("FP", 0)])
TKINDS = ["O", "Z1", "X", "Y", "Z2", "CR", "CK", "CV", "Z3", "FC", "FP"]
TCOUNT = {k: sum(u[0] == k for u in TUSES) for k in TKINDS}


def tail_bank(kind, j):
    return TUSES.index((kind, j)) % TRING


def tail_before(kind, j):
    n = TUSES.index((kind, j)) - TRING
    return TUSES[n] if n >= 0 else None


def tail_block(nc, w, out, ident, xN, combT, wfc, wfp, wo, cols):
    with ExitStack() as st:
        def sb(name, shape, dt=F32):
            return st.enter_context(nc.sbuf_tensor(name, shape, dt))

        def both(name, shape):
            return [sb(f"{name}_{s}", shape) for s in range(NS)]

        def sem(name):
            return st.enter_context(nc.semaphore(name))

        def sems(name):
            return [sem(f"{name}_{s}") for s in range(NS)]

        wkvr = sb("wkvr", [P, 3, NC, D])
        wcr = sb("wcr", [P, NC, D])
        wck = sb("wck", [P, NC, HID])
        wcv = sb("wcv", [P, NHC, D])
        ps = [st.enter_context(nc.psum_tensor(f"tps{i}", [P, 512], F32)) for i in range(NS * TRING)]
        w_in = {n: sem(f"w_in_{n}") for n in ("kvr", "cr", "ck", "cv")}

        x1, y, z, y2, xy, x2, res = (both(n, [P, GTT, D]) for n in ("x1", "y", "z", "y2", "xy", "x2", "res"))
        stats = both("tstats", [P, GTT, 6])
        mv = both("tmv", [P, 7, GTT])
        veps = both("tveps", [P, GTT])
        rstd = both("trstd", [P, GTT])
        rn = both("rn", [P, 4, GTT])
        power = sb("tpower", [P, GTT])
        eps_t = sb("eps_t", [P, GTT])
        hT, dT, xT, kT, vT, eT = (both(n, [P, NC, GTOK]) for n in ("hT", "dT", "xT", "kT", "vT", "eT"))
        top, sT, lT, pT, aT, mT = (both(n, [P, NC, GTOK]) for n in ("top", "sT", "lT", "pT", "aT", "mT"))
        cb = kT
        rw = lT
        rl = [[aT[s], sT[s]] for s in range(NS)]
        cr, crs, cri = ([a[s][:, :, :] for s in range(NS)] for a in (eT, mT, pT))
        bb = both("bb", [P, NC, GTOK])
        nT = both("nT", [P, NC, GTOK])
        low = sb("low", [P, NC, GTOK])
        dd = both("dd", [P, 2, NC, GTOK])
        ee = both("ee", [P, 2, NC, GTOK])
        hid = both("hid", [P, NHC, GTOK])

        full = [{k: sem(f"full_{k}_{s}") for k in TKINDS} for s in range(NS)]
        free = [{k: sem(f"free_{k}_{s}") for k in TKINDS} for s in range(NS)]
        preset = sem("preset")
        cb_in, y_out, again = sems("cb_in"), sems("y_out"), sems("again")
        ln_stat, ln_aggr, ln_eps, ln_rstd, ln_out = (
            sems(n) for n in ("ln_stat", "ln_aggr", "ln_eps", "ln_rstd", "ln_out"))
        shifted, mixed, wkv, exps, squared, summed, stored, gated = (
            sems(n) for n in ("shifted", "mixed", "wkv", "exps", "squared", "xy_in", "stored", "gated"))
        NLN, NWKV, NEXP, NAG = 3, 26, 4, 6

        def bank(s, kind, j=0):
            return ps[TRING * s + tail_bank(kind, j)]

        def in_two(a):
            return a[:, :].rearrange("p (n d) -> p n d", n=2)

        def flat(a):
            return a[:, :, :].rearrange("p c k -> p (c k)")

        def steps(a):
            return a[:, :, :].rearrange("p c (b t) -> p (c b) t", t=TQ)

        def both_streams(eng, entry, first, second, pair, ready=lambda *names: None):
            entry(0, 0)
            ready("kvr")
            first(0, 0)
            entry(1, 0)
            ready("cr", "ck", "cv")
            pair(1, 0, 0, 0, True)
            with eng.Fori(1, NGT - 1) as g:
                pair(0, g, 1, g - 1, True)
                pair(1, g, 0, g, True)
            pair(0, NGT - 1, 1, NGT - 2, True)
            pair(1, NGT - 1, 0, NGT - 1, False)
            second(1, NGT - 1)

        with nc.Block() as block:
            @block.sync
            def _(sp):
                for m, name in enumerate(("wk_T", "wv_T", "wr_T")):
                    sp.dma_start(wkvr[:, m, :, :], w[name].rearrange("(c p) n -> p c n", p=P)).then_inc(w_in["kvr"], 16)
                for dst, name in ((wcr, "cr"), (wck, "ck"), (wcv, "cv")):
                    sp.dma_start(dst[:], w[f"w{name}_T"].rearrange("(c p) n -> p c n", p=P)).then_inc(w_in[name], 16)

                def store(s, g):
                    sp.wait_ge(free[s]["FP"], g + 1)
                    sp.dma_start(out[bass.ds((NS * g + s) * GTT, GTT), :, :].rearrange("n p d -> p n d"),
                                 res[s][:]).then_inc(stored[s], 16)

                store(0, 0)
                with sp.Fori(1, NGT) as g:
                    store(1, g - 1)
                    store(0, g)
                store(1, NGT - 1)
                for s in range(NS):
                    sp.wait_ge(stored[s], 16 * NGT + 16)

            @block.gpsimd
            def _(pool):
                def root(s, g, k):
                    pool.wait_ge(ln_eps[s], NLN * g + k + 1)
                    pool.tensor_tensor(rstd[s][:], veps[s][:], power[:], ALU.pow).then_inc(ln_rstd[s], 1)

                def root_again(s, g):
                    r = rn[s]
                    base = 4 * g
                    pool.wait_ge(ln_rstd[s], NLN * g + 1)
                    pool.tensor_tensor(r[:, 0, :], mv[s][:, 6, :], rstd[s][:], ALU.mult).then_inc(again[s], 1)
                    pool.wait_ge(again[s], base + 1)
                    pool.tensor_tensor(r[:, 1, :], r[:, 0, :], rstd[s][:], ALU.mult).then_inc(again[s], 1)
                    pool.wait_ge(again[s], base + 2)
                    pool.tensor_tensor(r[:, 2, :], r[:, 1, :], eps_t[:], ALU.add).then_inc(again[s], 1)
                    pool.wait_ge(again[s], base + 3)
                    pool.tensor_tensor(r[:, 3, :], r[:, 2, :], power[:], ALU.pow).then_inc(again[s], 1)

                def residuals(s, g):
                    pool.wait_ge(free[s]["Y"], g + 1)
                    pool.tensor_tensor(xy[s][:], x1[s][:], y2[s][:], ALU.add).then_inc(summed[s], 1)

                def entry(s, g):
                    root(s, g, 0)
                    root_again(s, g)

                def first(s, g):
                    root(s, g, 1)
                    residuals(s, g)

                def second(s, g):
                    root(s, g, 2)

                def pair(x, gx, y, gy, more):
                    root(y, gy, 2)
                    root(x, gx, 1)
                    if more:
                        entry(y, gy + 1)
                    residuals(x, gx)

                pool.memset(power[:], -0.5).then_inc(preset, 1)
                pool.memset(eps_t[:], EPS).then_inc(preset, 1)
                for s in range(NS):
                    pool.memset(res[s][:], 0.0).then_inc(stored[s], 16)
                    pool.memset(bb[s][:], 0.0).then_inc(preset, 1)
                    pool.memset(nT[s][:], 0.0).then_inc(preset, 1)
                pool.memset(low[:], 3.0e38).then_inc(preset, 1)
                pool.wait_ge(preset, 7)
                pool.memset(steps(low)[:, :, 0:1], 0.0).then_inc(preset, 1)
                both_streams(pool, entry, first, second, pair)

            @block.scalar
            def _(act):
                def take(s, g, kind, j=0):
                    act.wait_ge(full[s][kind], TCOUNT[kind] * g + j + 1)
                    return bank(s, kind, j)

                def affine(s, g, kind, k):
                    b = take(s, g, kind)
                    for c in range(NC):
                        ins = act.activation(hT[s][:, c, :], in_two(b)[:, c, :], ACT.Identity,
                                             bias=cols[:, k + 1, c:c + 1], scale=cols[:, k, c:c + 1])
                        ins.then_inc(free[s][kind], 1)

                def keys(s, g):
                    act.copy(kT[s][:], in_two(take(s, g, "X", 0))).then_inc(free[s]["X"], 1)

                def values(s, g):
                    act.copy(vT[s][:], in_two(take(s, g, "X", 1))).then_inc(free[s]["X"], 1)

                def gates(s, g):
                    act.activation(eT[s][:], in_two(take(s, g, "X", 2)), ACT.Exp, scale=-1.0).then_inc(free[s]["X"], 1)

                def exp_pair(s, g, after):
                    act.wait_ge(wkv[s], NWKV * g + after)
                    act.activation(ee[s][:], dd[s][:], ACT.Exp).then_inc(exps[s], 1)

                def log(s, g):
                    act.wait_ge(wkv[s], NWKV * g + 7)
                    act.activation(lT[s][:], sT[s][:], ACT.Ln).then_inc(exps[s], 1)

                def receptance(s, g):
                    act.activation(cr[s], in_two(take(s, g, "CR")), ACT.Exp, scale=-1.0).then_inc(free[s]["CR"], 1)

                def hidden(s, g, r, i):
                    kind = "FC" if r else "CK"
                    b = take(s, g, kind, i)
                    if r or i >= 2:
                        act.wait_ge(squared[s], 2 * NHP * g + r * NHP + i - 1)
                    act.activation(rl[s][i % 2][:], in_two(b), ACT.Relu).then_inc(free[s][kind], 1)
                    act.wait_ge(free[s][kind], NHP * g + i + 1)
                    act.activation(hid[s][:, 2 * i:2 * i + 2, :], rl[s][i % 2][:], ACT.Square).then_inc(squared[s], 1)

                def plain(s, g):
                    act.copy(hT[s][:], in_two(take(s, g, "Z3"))).then_inc(free[s]["Z3"], 1)

                def entry(s, g):
                    pass

                def first(s, g):
                    affine(s, g, "Z1", 0)
                    keys(s, g)
                    exp_pair(s, g, 4)
                    log(s, g)
                    values(s, g)
                    exp_pair(s, g, 11)
                    gates(s, g)
                    exp_pair(s, g, 19)
                    affine(s, g, "Z2", 2)

                def second(s, g):
                    hidden(s, g, 0, 0)
                    receptance(s, g)
                    for i in range(1, NHP):
                        hidden(s, g, 0, i)
                    plain(s, g)
                    for i in range(NHP):
                        hidden(s, g, 1, i)

                def pair(x, gx, y, gy, more):
                    hidden(y, gy, 0, 0)
                    receptance(y, gy)
                    affine(x, gx, "Z1", 0)
                    for i in range(1, NHP):
                        hidden(y, gy, 0, i)
                    keys(x, gx)
                    exp_pair(x, gx, 4)
                    log(x, gx)
                    exp_pair(x, gx, 11)
                    values(x, gx)
                    gates(x, gx)
                    plain(y, gy)
                    exp_pair(x, gx, 19)
                    for i in range(NHP):
                        hidden(y, gy, 1, i)
                    affine(x, gx, "Z2", 2)

                both_streams(act, entry, first, second, pair)

            @block.vector
            def _(dve):
                def take(s, g, kind, j=0):
                    dve.wait_ge(full[s][kind], TCOUNT[kind] * g + j + 1)
                    return bank(s, kind, j)

                def deviation(s, g, k, src):
                    m = mv[s]
                    for n in range(GTT):
                        dve.bn_stats(stats[s][:, n, :], src[:, n, :]).then_inc(ln_stat[s], 1)
                    dve.wait_ge(ln_stat[s], (NLN * g + k + 1) * GTT)
                    even, odd = stats[s][:, :, 1:3], stats[s][:, :, 4:6]
                    dve.tensor_tensor(m[:, 0, :], even[:, :, 0], odd[:, :, 0], ALU.add).then_inc(ln_aggr[s], 1)
                    dve.tensor_tensor(m[:, 1, :], even[:, :, 0], odd[:, :, 0], ALU.subtract).then_inc(ln_aggr[s], 1)
                    dve.tensor_tensor(m[:, 2, :], even[:, :, 1], odd[:, :, 1], ALU.add).then_inc(ln_aggr[s], 1)
                    dve.wait_ge(ln_aggr[s], (NLN * g + k) * NAG + 3)
                    dve.tensor_scalar(m[:, 3, :], m[:, 0, :], 0.5, None, ALU.mult).then_inc(ln_aggr[s], 1)
                    dve.tensor_tensor(m[:, 4, :], m[:, 1, :], m[:, 1, :], ALU.mult).then_inc(ln_aggr[s], 1)
                    dve.wait_ge(ln_aggr[s], (NLN * g + k) * NAG + 5)
                    dve.scalar_tensor_tensor(m[:, 5, :], m[:, 4, :], D / 4.0, m[:, 2, :],
                                             ALU.mult, ALU.add).then_inc(ln_aggr[s], 1)
                    dve.wait_ge(ln_aggr[s], (NLN * g + k) * NAG + 6)
                    if k == 0:
                        dve.tensor_scalar(m[:, 6, :], m[:, 5, :], 1.0 / D, None, ALU.mult).then_inc(y_out[s], 1)
                    dve.tensor_scalar(veps[s][:], m[:, 5, :], 1.0 / D, EPS, ALU.mult, ALU.add).then_inc(ln_eps[s], 1)

                def scaled(s, g, k, src, dst, done):
                    dve.wait_ge(ln_rstd[s], NLN * g + k + 1)
                    for n in range(GTT):
                        dve.tensor_scalar(dst[:, n, :], src[:, n, :], mv[s][:, 3, n:n + 1], rstd[s][:, n:n + 1],
                                          ALU.subtract, ALU.mult).then_inc(done, 1)

                def fetch(s, g):
                    dve.tensor_copy(cb[s][:], combT[:, :, bass.ds((NS * g + s) * GTOK, GTOK)]).then_inc(cb_in[s], 1)

                def enter(s, g):
                    dve.tensor_tensor(x1[s][:], in_two(take(s, g, "O")), xN[:, bass.ds((NS * g + s) * GTT, GTT), :],
                                      ALU.add).then_inc(free[s]["O"], 1)
                    dve.wait_ge(free[s]["O"], g + 1)
                    deviation(s, g, 0, x1[s])

                def enter_end(s, g, after):
                    scaled(s, g, 0, x1[s], y[s], y_out[s])
                    dve.wait_ge(y_out[s], 3 * g + 3)
                    if after:
                        dve.wait_ge(full[s]["Z3"], g)
                    dve.wait_ge(again[s], 4 * g + 4)
                    for n in range(GTT):
                        dve.tensor_scalar(z[s][:, n, :], y[s][:, n, :], rn[s][:, 3, n:n + 1], None,
                                          ALU.mult).then_inc(ln_out[s], 1)

                def mixing(s):
                    for c in range(NC):
                        dve.scalar_tensor_tensor(xT[s][:, c, :], dT[s][:, c, :], cols[:, 4, c:c + 1], hT[s][:, c, :],
                                                 ALU.mult, ALU.add).then_inc(mixed[s], 1)

                def time_mix(s, g):
                    d, h = steps(dT[s]), steps(hT[s])
                    dve.wait_ge(free[s]["Z1"], NC * g + NC)
                    dve.tensor_tensor(d[:, :, 1:TQ], h[:, :, 1:TQ], h[:, :, 0:TQ - 1], ALU.subtract).then_inc(shifted[s], 1)
                    for c in range(NC):
                        dve.tensor_scalar(d[:, GB * c:GB * c + GB, 0:1], h[:, GB * c:GB * c + GB, 0:1],
                                          cols[:, 4, c:c + 1], None, ALU.subtract).then_inc(shifted[s], 1)
                    dve.wait_ge(shifted[s], 5 * g + 3)
                    mixing(s)

                def channel_mix(s, g):
                    d, h = steps(dT[s]), steps(hT[s])
                    dve.wait_ge(free[s]["Z2"], NC * g + NC)
                    dve.tensor_tensor(d[:, :, 1:TQ], h[:, :, 0:TQ - 1], h[:, :, 1:TQ], ALU.subtract).then_inc(shifted[s], 1)
                    dve.tensor_tensor(d[:, :, 0:1], h[:, :, TQ - 1:TQ], h[:, :, 0:1], ALU.subtract).then_inc(shifted[s], 1)
                    dve.wait_ge(shifted[s], 5 * g + 5)
                    mixing(s)

                def did(s, g, j):
                    dve.wait_ge(wkv[s], NWKV * g + j)

                def running_max(s, g):
                    da, db, t = steps(dd[s][:, 0, :, :]), dd[s][:, 1, :, :], steps(top[s])
                    dve.wait_ge(free[s]["X"], 3 * g + 1)
                    dve.tensor_tensor_scan(flat(top[s]), flat(low), flat(kT[s]), 0.0, ALU.min, ALU.max).then_inc(wkv[s], 1)
                    did(s, g, 1)
                    dve.tensor_tensor(da[:, :, 1:TQ], t[:, :, 0:TQ - 1], t[:, :, 1:TQ], ALU.subtract).then_inc(wkv[s], 1)
                    dve.tensor_scalar(da[:, :, 0:1], t[:, :, 0:1], -1.0, None, ALU.mult).then_inc(wkv[s], 1)
                    dve.tensor_tensor(db, kT[s][:], top[s][:], ALU.subtract).then_inc(wkv[s], 1)

                def sum_scan(s, g):
                    ea, eb = ee[s][:, 0, :, :], ee[s][:, 1, :, :]
                    dve.wait_ge(exps[s], NEXP * g + 1)
                    dve.tensor_tensor(steps(eb)[:, :, 0:1], steps(eb)[:, :, 0:1], steps(ea)[:, :, 0:1],
                                      ALU.add).then_inc(wkv[s], 1)
                    did(s, g, 5)
                    dve.memset(steps(ea)[:, :, 0:1], 0.0).then_inc(wkv[s], 1)
                    did(s, g, 6)
                    dve.tensor_tensor_scan(flat(sT[s]), flat(ea), flat(eb), 0.0, ALU.mult, ALU.add).then_inc(wkv[s], 1)

                def log_before(s, g):
                    da, db = dd[s][:, 0, :, :], dd[s][:, 1, :, :]
                    dve.wait_ge(exps[s], NEXP * g + 2)
                    dve.tensor_tensor(steps(bb[s])[:, :, 1:TQ], steps(top[s])[:, :, 0:TQ - 1],
                                      steps(lT[s])[:, :, 0:TQ - 1], ALU.add).then_inc(wkv[s], 1)
                    did(s, g, 8)
                    dve.tensor_tensor(pT[s][:], bb[s][:], kT[s][:], ALU.max).then_inc(wkv[s], 1)
                    did(s, g, 9)
                    dve.tensor_tensor(da, bb[s][:], pT[s][:], ALU.subtract).then_inc(wkv[s], 1)
                    dve.tensor_tensor(db, kT[s][:], pT[s][:], ALU.subtract).then_inc(wkv[s], 1)

                def value_scan(s, g):
                    ea, eb = ee[s][:, 0, :, :], ee[s][:, 1, :, :]
                    dve.wait_ge(exps[s], NEXP * g + 3)
                    dve.wait_ge(free[s]["X"], 3 * g + 2)
                    dve.tensor_tensor(mT[s][:], eb, vT[s][:], ALU.mult).then_inc(wkv[s], 1)
                    dve.memset(steps(ea)[:, :, 0:1], 0.0).then_inc(wkv[s], 1)
                    did(s, g, 13)
                    dve.tensor_tensor_scan(flat(aT[s]), flat(ea), flat(mT[s]), 0.0, ALU.mult, ALU.add).then_inc(wkv[s], 1)

                def value_differences(s, g):
                    da, db = dd[s][:, 0, :, :], dd[s][:, 1, :, :]
                    for c in range(NC):
                        dve.scalar_tensor_tensor(pT[s][:, c, :], kT[s][:, c, :], cols[:, 5, c:c + 1], bb[s][:, c, :],
                                                 ALU.add, ALU.max).then_inc(wkv[s], 1)
                    did(s, g, 16)
                    dve.tensor_tensor(da, bb[s][:], pT[s][:], ALU.subtract).then_inc(wkv[s], 1)
                    for c in range(NC):
                        dve.scalar_tensor_tensor(db[:, c, :], kT[s][:, c, :], cols[:, 5, c:c + 1], pT[s][:, c, :],
                                                 ALU.add, ALU.subtract).then_inc(wkv[s], 1)

                def quotient(s, g):
                    ea, eb = ee[s][:, 0, :, :], ee[s][:, 1, :, :]
                    dve.wait_ge(exps[s], NEXP * g + 4)
                    dve.tensor_tensor(steps(nT[s])[:, :, 1:TQ], steps(ea)[:, :, 1:TQ], steps(aT[s])[:, :, 0:TQ - 1],
                                      ALU.mult).then_inc(wkv[s], 1)
                    dve.tensor_tensor(mT[s][:], eb, vT[s][:], ALU.mult).then_inc(wkv[s], 1)
                    dve.tensor_tensor(sT[s][:], ea, eb, ALU.add).then_inc(wkv[s], 1)
                    did(s, g, 21)
                    dve.tensor_tensor(aT[s][:], nT[s][:], mT[s][:], ALU.add).then_inc(wkv[s], 1)
                    did(s, g, 22)
                    dve.wait_ge(free[s]["X"], 3 * g + 3)
                    dve.scalar_tensor_tensor(pT[s][:], eT[s][:], 1.0, sT[s][:], ALU.add, ALU.mult).then_inc(wkv[s], 1)
                    did(s, g, 24)
                    dve.reciprocal(sT[s][:], pT[s][:]).then_inc(wkv[s], 1)
                    did(s, g, 25)
                    dve.tensor_tensor(rw[s][:], aT[s][:], sT[s][:], ALU.mult).then_inc(wkv[s], 1)

                def middle(s, g):
                    dve.tensor_tensor(y2[s][:], in_two(take(s, g, "Y")), y[s][:], ALU.add).then_inc(free[s]["Y"], 1)
                    dve.wait_ge(free[s]["Y"], g + 1)
                    deviation(s, g, 1, y2[s])

                def middle_end(s, g):
                    scaled(s, g, 1, y2[s], z[s], ln_out[s])

                def receptance(s, g):
                    dve.wait_ge(free[s]["CR"], g + 1)
                    dve.tensor_scalar(crs[s], cr[s], 1.0, None, ALU.add).then_inc(gated[s], 1)
                    dve.wait_ge(gated[s], 3 * g + 1)
                    dve.reciprocal(cri[s], crs[s]).then_inc(gated[s], 1)

                def channel_out(s, g):
                    dve.wait_ge(gated[s], 3 * g + 2)
                    dve.tensor_tensor(cr[s], in_two(take(s, g, "CV")), cri[s], ALU.mult).then_inc(free[s]["CV"], 1)
                    dve.wait_ge(free[s]["CV"], g + 1)
                    dve.wait_ge(summed[s], g + 1)
                    dve.tensor_tensor(x2[s][:], cr[s], xy[s][:], ALU.add).then_inc(gated[s], 1)
                    dve.wait_ge(gated[s], 3 * g + 3)
                    deviation(s, g, 2, x2[s])

                def channel_end(s, g):
                    scaled(s, g, 2, x2[s], z[s], ln_out[s])

                def leave(s, g):
                    b = take(s, g, "FP")
                    dve.wait_ge(stored[s], 16 * g + 16)
                    dve.tensor_tensor(res[s][:], in_two(b), x2[s][:], ALU.add).then_inc(free[s]["FP"], 1)

                def entry(s, g):
                    fetch(s, g)
                    enter(s, g)
                    enter_end(s, g, False)

                def first(s, g):
                    time_mix(s, g)
                    running_max(s, g)
                    sum_scan(s, g)
                    log_before(s, g)
                    value_scan(s, g)
                    value_differences(s, g)
                    quotient(s, g)
                    middle(s, g)
                    middle_end(s, g)
                    channel_mix(s, g)

                def second(s, g):
                    receptance(s, g)
                    channel_out(s, g)
                    channel_end(s, g)
                    leave(s, g)

                def pair(x, gx, y, gy, more):
                    time_mix(x, gx)
                    receptance(y, gy)
                    running_max(x, gx)
                    sum_scan(x, gx)
                    log_before(x, gx)
                    channel_out(y, gy)
                    channel_end(y, gy)
                    value_scan(x, gx)
                    value_differences(x, gx)
                    if more:
                        fetch(y, gy + 1)
                    quotient(x, gx)
                    middle(x, gx)
                    middle_end(x, gx)
                    if more:
                        enter(y, gy + 1)
                    channel_mix(x, gx)
                    if more:
                        enter_end(y, gy + 1, True)
                    leave(y, gy)

                def ready(*names):
                    if "kvr" in names:
                        dve.wait_ge(preset, 8)

                both_streams(dve, entry, first, second, pair, ready)

            @block.tensor
            def _(pe):
                def give(s, g, kind, j=0):
                    before = tail_before(kind, j)
                    if before:
                        k, m = before
                        reads = NC if k in ("Z1", "Z2") else 1
                        pe.wait_ge(free[s][k], TCOUNT[k] * reads * g + (m + 1) * reads)
                    return bank(s, kind, j)

                def turn(s, g, kind, norms):
                    pe.wait_ge(ln_out[s], norms * GTT)
                    b = give(s, g, kind)
                    for c in range(NC):
                        for n in range(GTT):
                            last = pe.transpose(b[:, GTOK * c + P * n:GTOK * c + P * n + P],
                                                z[s][:, n, P * c:P * c + P], ident[:])
                    last.then_inc(full[s][kind], 1)

                def by_tokens(s, g, kind, src, wt, n_in, between=None):
                    b = give(s, g, kind)
                    for n in range(GTT):
                        for c in range(n_in):
                            last = pe.matmul(b[:, D * n:D * n + D], src[:, c, P * n:P * n + P], wt[:, c, :],
                                             start=(c == 0), stop=(c == n_in - 1))
                        if n == 0 and between is not None:
                            between()
                    last.then_inc(full[s][kind], 1)

                def by_channels(s, g, kind, j, wt, o, src):
                    b = give(s, g, kind, j)
                    for i in range(2):
                        for c in range(NC):
                            last = pe.matmul(b[:, GTOK * i:GTOK * i + GTOK], wt[:, c, P * (o + i):P * (o + i) + P],
                                             src[:, c, :], start=(c == 0), stop=(c == NC - 1))
                    last.then_inc(full[s][kind], 1)

                def turn_in(s, g, after=False):
                    if after:
                        pe.wait_ge(free[s]["FC"], NHP * g)
                    turn(s, g, "Z1", NLN * g + 1)

                def project(s, g, after=False):
                    pe.wait_ge(cb_in[s], g + 1)
                    if after:
                        pe.wait_ge(free[s]["FC"], NHP * g - 1)
                    by_tokens(s, g, "O", cb[s], wo, NC)

                def keys(s, g, after=False):
                    if after:
                        pe.wait_ge(free[s]["FP"], g)
                    pe.wait_ge(mixed[s], 4 * g + 2)
                    by_channels(s, g, "X", 0, wkvr[:, 0, :, :], 0, xT[s])

                def values(s, g):
                    for m in (1, 2):
                        by_channels(s, g, "X", m, wkvr[:, m, :, :], 0, xT[s])

                def turn_back(s, g):
                    pe.wait_ge(wkv[s], NWKV * g + 26)
                    b = give(s, g, "Y")
                    for n in range(GTT):
                        for c in range(NC):
                            last = pe.transpose(b[:, D * n + P * c:D * n + P * c + P], rw[s][:, c, P * n:P * n + P], ident[:])
                    last.then_inc(full[s]["Y"], 1)

                def channel_keys(s, g, between=None):
                    pe.wait_ge(mixed[s], 4 * g + 4)
                    by_tokens(s, g, "CR", xT[s], wcr, NC)
                    for i in range(NHP):
                        if i == 1 and between is not None:
                            between()
                        by_channels(s, g, "CK", i, wck, 2 * i, xT[s])

                def channel_values(s, g):
                    pe.wait_ge(squared[s], 2 * NHP * g + NHP)
                    by_tokens(s, g, "CV", hid[s], wcv, NHC)

                def feed_in(s, g):
                    pe.wait_ge(free[s]["Z3"], g + 1)
                    for i in range(NHP):
                        by_channels(s, g, "FC", i, wfc, 2 * i, hT[s])

                def feed_out(s, g, between=None):
                    pe.wait_ge(squared[s], 2 * NHP * g + 2 * NHP)
                    by_tokens(s, g, "FP", hid[s], wfp, NHC, between)

                def entry(s, g, after=False):
                    project(s, g, after)

                def first(s, g):
                    turn_in(s, g)
                    keys(s, g)
                    values(s, g)
                    turn_back(s, g)
                    turn(s, g, "Z2", NLN * g + 2)

                def second(s, g):
                    channel_keys(s, g)
                    channel_values(s, g)
                    turn(s, g, "Z3", NLN * g + 3)
                    feed_in(s, g)
                    feed_out(s, g)

                def pair(x, gx, y, gy, more):
                    after = not (isinstance(gx, int) and gx == 0)
                    channel_keys(y, gy, lambda: turn_in(x, gx, after))
                    keys(x, gx, after)
                    channel_values(y, gy)
                    values(x, gx)
                    turn(y, gy, "Z3", NLN * gy + 3)
                    feed_in(y, gy)
                    if more:
                        project(y, gy + 1, True)
                    turn_back(x, gx)
                    feed_out(y, gy, lambda: turn(x, gx, "Z2", NLN * gx + 2))

                def ready(*names):
                    for n in names:
                        pe.wait_ge(w_in[n], 16 * (3 if n == "kvr" else 1))

                both_streams(pe, entry, first, second, pair, ready)


def kernel(**inputs):
    import numpy as _np
    import concourse.bacc as _bacc
    from concourse import mybir as _mybir
    from concourse.bass_utils import run_bass_kernel_spmd as _run

    a = {k: _np.asarray(v) for k, v in inputs.items()}

    def turned(name):
        return _np.ascontiguousarray(a[name].T)

    def columns(v):
        return _np.ascontiguousarray(v.reshape(NC, P).T)

    first = (_np.arange(P) % 32 < DK).astype(_np.float32)
    data = {
        "x": a["x"],
        "ctx_T": _np.ascontiguousarray(a["ctx_1024"].transpose(0, 2, 1)),
        "ident": _np.eye(P, dtype=_np.float32),
        "half": _np.stack([first, 1 - first], axis=1),
        "w_q": a["L0_xattn_W_Q"], "w_k": a["L0_xattn_W_K"], "w_v": a["L0_xattn_W_V"], "w_o": a["L0_xattn_W_O"],
        "b_q": columns(a["L0_xattn_b_Q"]), "b_k": columns(a["L0_xattn_b_K"]), "b_v": columns(a["L0_xattn_b_V"]),
        "b_o": _np.ascontiguousarray(_np.broadcast_to(a["L0_xattn_b_O"], (P, D))),
        "wk_T": turned("L0_attn_Wk"), "wv_T": turned("L0_attn_Wv"), "wr_T": turned("L0_attn_Wr"),
        "wcr_T": turned("L0_attn_Wcr"), "wck_T": turned("L0_attn_Wck"), "wcv_T": turned("L0_attn_Wcv"),
        "cols": _np.ascontiguousarray(_np.stack(
            [columns(a["L0_attn_" + n].reshape(D)) for n in
             ("ln1_w", "ln1_b", "ln2_w", "ln2_b", "time_shift", "time_first")], axis=1)),
        "w_fc": a["L0_ffn_w_fc"], "w_proj": a["L0_ffn_w_proj"], "u_T": turned("L0_ffn_u"), "v": a["L0_ffn_v"],
        "fast_b": a["L0_ffn_fast_b"],
        "gate": _np.ascontiguousarray(_np.broadcast_to(a["L0_ffn_gate"].reshape(1, 1), (16, 1))),
    }
    nc = _bacc.Bacc("TRN2", target_bir_lowering=False, num_devices=1)
    t = {n: nc.dram_tensor(f"in_{n}", v.shape, _mybir.dt.from_np(v.dtype), kind="ExternalInput").ap()
         for n, v in data.items()}
    out = nc.dram_tensor("out_dram", (NTT, P, D), F32, kind="ExternalOutput").ap()
    perceiver_kernel(nc, t, out)
    r = _run(nc, [{f"in_{n}": v for n, v in data.items()}], core_ids=[0])
    return r.results[0]["out_dram"].reshape(NB, TQ, D)
```
